# Optimizing a Trainium2 kernel written in Bass

```python
import numpy as np
import jax
import jax.numpy as jnp

def _softmax(x, axis=-1):
    return jax.nn.softmax(x, axis=axis)

def _gelu(x):
    return jax.nn.gelu(x, approximate=True)

def _silu(x):
    return jax.nn.silu(x)

def _sigmoid(x):
    return jax.nn.sigmoid(x)

def _layernorm(x, axis=-1, eps=1e-05):
    m = jnp.mean(x, axis=axis, keepdims=True)
    v = jnp.var(x, axis=axis, keepdims=True)
    return (x - m) / jnp.sqrt(v + eps)

def _scatter_add(tgt, idx, src, axis=0):
    return tgt.at[idx].add(src)

def _segment_sum(src, seg, n):
    return jax.ops.segment_sum(src, seg, n)
kernel_name = 'mk_gnn_preln_d2_gnn_r64_0cc454'

def setup_inputs(seed: int=0):
    np.random.seed(seed)
    _w = jnp.asarray

    def _rec_inputs():
        import jax
        import jax.numpy as jnp
        _gk = jax.random.key(seed)
        x = -0.0005121 + 1.001 * jax.random.normal(jax.random.fold_in(_gk, 1), (100000, 64), jnp.float32)
        src = jax.random.randint(jax.random.fold_in(_gk, 2), (25000,), 0, 100000, jnp.int32)
        dst = jnp.minimum((100000 * jax.random.uniform(jax.random.fold_in(_gk, 3), (25000,)) ** 2.0).astype(jnp.int32), 99999)
        _o = jnp.argsort(dst, stable=True)
        src = src[_o]
        dst = dst[_o]
        edge_attr_128 = jax.random.uniform(jax.random.fold_in(_gk, 12), (25000, 128), jnp.float32, 0.0, 1)
        edge_attr_64 = -8.16379e-05 + 0.999858 * jax.random.normal(jax.random.fold_in(_gk, 13), (25000, 64), jnp.float32)
        return (x, src, dst, edge_attr_128, edge_attr_64)
    x, src, dst, edge_attr_128, edge_attr_64 = _rec_inputs()

    def _L0_gnn_setup():
        import jax, jax.numpy as jnp
        import numpy as np
        N_NODES = 50000
        N_EDGES = 12500
        D_FEAT = 64
        NEG_SLOPE = 0.01
        key = jax.random.key(seed)
        ks = jax.random.split(key, 8)
        in_feat = jax.random.normal(ks[0], (N_NODES, D_FEAT), dtype=jnp.float32)
        src = jax.random.randint(ks[1], (N_EDGES,), 0, N_NODES, dtype=jnp.int64)
        dst = jax.random.randint(ks[2], (N_EDGES,), 0, N_NODES, dtype=jnp.int64)
        scale = 1.0 / np.sqrt(D_FEAT)
        W1 = jax.random.normal(ks[3], (D_FEAT, D_FEAT), dtype=jnp.float32) * scale
        b1 = jnp.zeros((D_FEAT,), dtype=jnp.float32)
        W2 = jax.random.normal(ks[4], (D_FEAT, D_FEAT), dtype=jnp.float32) * scale
        b2 = jnp.zeros((D_FEAT,), dtype=jnp.float32)
        return {'in_feat': in_feat, 'W1': W1, 'b1': b1, 'W2': W2, 'b2': b2, 'src': src, 'dst': dst}
    _L0_gnn_all = _L0_gnn_setup()
    _L0_gnn_in = {k: v for k, v in _L0_gnn_all.items() if k in ('W1', 'b1', 'W2', 'b2')}
    del _L0_gnn_all

    def _L1_gnn_setup():
        import jax, jax.numpy as jnp
        import numpy as np
        N_NODES = 50000
        N_EDGES = 25000
        IN_FEATS = 64
        RADIAL_FEATS = 128
        OUT_FEATS = 64

        def ssp(x):
            return jax.nn.softplus(x) - jnp.log(2.0).astype(x.dtype)
        key = jax.random.key(seed)
        ks = jax.random.split(key, 10)
        inp = {'node_h': jax.random.normal(ks[0], (N_NODES, IN_FEATS), dtype=jnp.float32), 'edge_h': jax.random.normal(ks[1], (N_EDGES, IN_FEATS), dtype=jnp.float32), 'bf': jax.random.uniform(ks[2], (N_EDGES, RADIAL_FEATS), dtype=jnp.float32), 'W1': jax.random.normal(ks[3], (RADIAL_FEATS, IN_FEATS), dtype=jnp.float32) / np.sqrt(RADIAL_FEATS), 'b1': jnp.zeros((IN_FEATS,), jnp.float32), 'W2': jax.random.normal(ks[4], (IN_FEATS, IN_FEATS), dtype=jnp.float32) / np.sqrt(IN_FEATS), 'b2': jnp.zeros((IN_FEATS,), jnp.float32), 'W3': jax.random.normal(ks[5], (IN_FEATS, OUT_FEATS), dtype=jnp.float32) / np.sqrt(IN_FEATS), 'b3': jnp.zeros((OUT_FEATS,), jnp.float32), 'W4': jax.random.normal(ks[6], (OUT_FEATS, IN_FEATS), dtype=jnp.float32) / np.sqrt(OUT_FEATS), 'b4': jnp.zeros((IN_FEATS,), jnp.float32), 'src': jax.random.randint(ks[7], (N_EDGES,), 0, N_NODES, dtype=jnp.int64 if jax.config.jax_enable_x64 else jnp.int32), 'dst': jax.random.randint(ks[8], (N_EDGES,), 0, N_NODES, dtype=jnp.int64 if jax.config.jax_enable_x64 else jnp.int32)}
        return inp
    _L1_gnn_all = _L1_gnn_setup()
    _L1_gnn_in = {k: v for k, v in _L1_gnn_all.items() if k in ('W1', 'b1', 'W2', 'b2', 'W3', 'b3', 'W4', 'b4')}
    del _L1_gnn_all
    return {'x': x, 'src': src, 'dst': dst, 'edge_attr_128': edge_attr_128, 'edge_attr_64': edge_attr_64, 'L0_gnn_W1': _L0_gnn_in['W1'], 'L0_gnn_b1': _L0_gnn_in['b1'], 'L0_gnn_W2': _L0_gnn_in['W2'], 'L0_gnn_b2': _L0_gnn_in['b2'], 'L1_gnn_W1': _L1_gnn_in['W1'], 'L1_gnn_b1': _L1_gnn_in['b1'], 'L1_gnn_W2': _L1_gnn_in['W2'], 'L1_gnn_b2': _L1_gnn_in['b2'], 'L1_gnn_W3': _L1_gnn_in['W3'], 'L1_gnn_b3': _L1_gnn_in['b3'], 'L1_gnn_W4': _L1_gnn_in['W4'], 'L1_gnn_b4': _L1_gnn_in['b4']}

def reference(x, src, dst, edge_attr_128, edge_attr_64, L0_gnn_W1, L0_gnn_b1, L0_gnn_W2, L0_gnn_b2, L1_gnn_W1, L1_gnn_b1, L1_gnn_W2, L1_gnn_b2, L1_gnn_W3, L1_gnn_b3, L1_gnn_W4, L1_gnn_b4):
    import jax
    import jax.numpy as jnp

    def _L0_gnn_ref(in_feat, W1, b1, W2, b2, src, dst):
        import jax, jax.numpy as jnp
        import numpy as np
        N_NODES = 50000
        N_EDGES = 12500
        D_FEAT = 64
        NEG_SLOPE = 0.01
        N = in_feat.shape[0]
        mask = (src != dst).astype(in_feat.dtype)
        out_deg = jax.ops.segment_sum(mask, src, num_segments=N) + 1.0
        in_deg = jax.ops.segment_sum(mask, dst, num_segments=N) + 1.0
        inv_out = jax.lax.rsqrt(out_deg)[:, None]
        inv_in = jax.lax.rsqrt(in_deg)[:, None]

        def layer(h, W, b):
            hs = h * inv_out
            msg = hs[src] * mask[:, None]
            agg = jax.ops.segment_sum(msg, dst, num_segments=N) + hs
            agg = agg * inv_in
            return jax.nn.leaky_relu(agg @ W + b, negative_slope=NEG_SLOPE)
        h = layer(in_feat, W1, b1)
        h = layer(h, W2, b2)
        return h

    def _L1_gnn_ref(node_h, edge_h, bf, W1, b1, W2, b2, W3, b3, W4, b4, src, dst):
        import jax, jax.numpy as jnp
        import numpy as np
        N_NODES = 50000
        N_EDGES = 25000
        IN_FEATS = 64
        RADIAL_FEATS = 128
        OUT_FEATS = 64

        def ssp(x):
            return jax.nn.softplus(x) - jnp.log(2.0).astype(x.dtype)
        n_nodes = node_h.shape[0]
        w = ssp(bf @ W1 + b1)
        w = ssp(w @ W2 + b2)
        eh = w * edge_h
        m = node_h[src] * eh
        s = jax.ops.segment_sum(m, dst, num_segments=n_nodes)
        cnt = jax.ops.segment_sum(jnp.ones((m.shape[0],), m.dtype), dst, num_segments=n_nodes)
        h = s / jnp.maximum(cnt, 1.0)[:, None]
        out = ssp(h @ W3 + b3)
        return ssp(out @ W4 + b4)
    h = jnp.maximum(_layernorm(x, axis=-1), 0.0)
    x = x + _L0_gnn_ref(h, L0_gnn_W1, L0_gnn_b1, L0_gnn_W2, L0_gnn_b2, src, dst)
    h = jnp.maximum(_layernorm(x, axis=-1), 0.0)
    x = x + _L1_gnn_ref(h, edge_attr_64, edge_attr_128, L1_gnn_W1, L1_gnn_b1, L1_gnn_W2, L1_gnn_b2, L1_gnn_W3, L1_gnn_b3, L1_gnn_W4, L1_gnn_b4, src, dst)
    return x

_drawn_inputs = setup_inputs


def setup_inputs(seed=0):
    import zlib

    import numpy as np

    out = dict(_drawn_inputs(seed))
    spreads = {'L0_gnn_b1': (0.0, 0.1),
     'L0_gnn_b2': (0.0, 0.1),
     'L1_gnn_b1': (0.0, 0.8),
     'L1_gnn_b2': (0.0, 0.8),
     'L1_gnn_b3': (0.0, 0.287),
     'L1_gnn_b4': (0.0, 0.1)}
    factors = {'edge_attr_128': 8.0,
     'edge_attr_64': 4.531,
     'L1_gnn_W1': 4.657,
     'L1_gnn_W2': 5.46,
     'L1_gnn_W3': 4.515}
    for name, (base, spread) in spreads.items():
        noise = np.random.default_rng([zlib.crc32(name.encode()), seed]).standard_normal(out[name].shape)
        drawn = base * np.exp(spread * noise) if base else spread * noise
        out[name] = jnp.asarray(drawn.astype(out[name].dtype))
    for name, factor in factors.items():
        out[name] = (out[name] * factor).astype(out[name].dtype)
    return out
```

```python
import concourse.bass as bass
from concourse import mybir
from contextlib import ExitStack

ALU = mybir.AluOpType
ACT = mybir.ActivationFunctionType
AX_X = mybir.AxisListType.X
F32 = mybir.dt.float32
F16 = mybir.dt.float16
I32 = mybir.dt.int32
U32 = mybir.dt.uint32

P = 128
J = 8
BLOCK = P * J
GROUP = 4
SKIP = 131071
AROW = 66
RING = 2
EPS = 1e-5
SLOPE = 0.01


def done(g):
    return g + 1 + RING


def freed(g):
    return g + 1


def each_group(eng, count, body):
    with eng.Fori(0, count // 2) as i:
        body(2 * i, 0, i)
        body(2 * i + 1, 1, i)
    body(count - 1, 0, count // 2)


def each_group_lead(eng, count, first, then):
    first(0, 0, 0)
    with eng.Fori(0, count // 2) as i:
        first(2 * i + 1, 1, i)
        then(2 * i, 0, i)
        first(2 * i + 2, 0, i + 1)
        then(2 * i + 1, 1, i)
    then(count - 1, 0, count // 2)


def each_group_ahead(eng, count, fetch, body):
    fetch(0, 0)
    fetch(1, 1)
    with eng.Fori(0, count // 2 - 1) as i:
        for u in range(2):
            fetch(2 * i + u + 2, u)
            body(2 * i + u, u, i)
    fetch(count - 1, 0)
    for g in range(count - 3, count):
        body(g, g % 2, g // 2)


def gnn_kernel(nc, x, src, dst, radial, edge_h, gW1, gb1, gW2, gb2,
               sW1, sb1, sW2, sb2, sW3, sb3, sW4, sb4, out):
    N, D = x.shape
    E = src.shape[0]
    R = radial.shape[1]
    T = -(-E // P)
    SLOTS = T * P
    EL = E - (T - 1) * P
    NG = T // GROUP
    NBLK = -(-N // BLOCK)
    PL = (N - (NBLK - 1) * BLOCK) // J
    NC = NBLK * J
    HC = NC // 2
    assert T == NG * GROUP and NBLK == 2 * NG and NG % 2 == 1 and D == 64 and R == P
    assert (N - (NBLK - 1) * BLOCK) % J == 0 and HC <= 512 and N < SKIP
    PAIRS = NG // 2
    GC = GROUP * P
    TL = T - P

    dst_rows = nc.dram_tensor("dst_rows", [1, SLOTS + P], F32, kind="Internal").ap()
    table_a = nc.dram_tensor("table_a", [N, AROW], F32, kind="Internal").ap()
    x_dst = nc.dram_tensor("x_dst", [SLOTS, D], F32, kind="Internal").ap()
    carried = nc.dram_tensor("carried", [NG, GROUP, GC], F32, kind="Internal").ap()
    carried_rows = nc.dram_tensor("carried_rows", [NG, GROUP, P], F32, kind="Internal").ap()
    table_h = nc.dram_tensor("table_h", [SLOTS + NBLK * BLOCK, D], F32, kind="Internal").ap()
    table_x = nc.dram_tensor("table_x", [SLOTS + NBLK * BLOCK, D], F32, kind="Internal").ap()

    local_h, local_x = table_h[SLOTS:, :], table_x[SLOTS:, :]

    def both(t, g):
        return t[bass.ds(g * 2 * BLOCK, 2 * BLOCK), :].rearrange("(k p j) d -> p k (j d)", p=P, j=J)

    def tiles(t, g):
        return t[bass.ds(g * GC, GC), :].rearrange("(t p) d -> p t d", p=P)

    def blocks(t, b, rows=P):
        return t[bass.ds(b * BLOCK, rows * J), :].rearrange("(p j) d -> p (j d)", j=J)

    with ExitStack() as ctx:
        def sb(name, shape, dt=F32):
            return ctx.enter_context(nc.sbuf_tensor(name, shape, dt))

        def sem(name):
            return ctx.enter_context(nc.semaphore(name))

        ident = sb("ident", [P, P])
        ones = sb("ones", [P, P])
        center2 = sb("center2", [P, P])
        gW1_2 = sb("gW1_2", [P, P])
        gW2_2 = sb("gW2_2", [P, P])
        sW4_2 = sb("sW4_2", [P, P])
        gW1_a = sb("gW1_a", [D + 1, D + 1])
        sW3_a = sb("sW3_a", [D + 1, D + 1])
        gW2_s = sb("gW2_s", [D, D])
        sW1_s = sb("sW1_s", [P, D])
        sW2_s = sb("sW2_s", [D, D])
        b1_rows = sb("b1_rows", [1, J * D])
        b2_rows = sb("b2_rows", [1, J * D])
        sb2_rows = sb("sb2_rows", [1, GROUP * D])
        sb4_rows = sb("sb4_rows", [1, GROUP * D])
        b1_all = sb("b1_all", [P, D])
        b2_all = sb("b2_all", [P, D])
        sb3_all = sb("sb3_all", [P, D])
        sb1_row = sb("sb1_row", [1, D])
        ones_row = sb("ones_row", [1, GROUP * P])
        sb3_col = sb("sb3_col", [D, 1])
        rest_row = sb("rest_row", [P, D])
        eps_col = sb("eps_col", [P, 1])
        iota_lo = sb("iota_lo", [P, P], F16)
        zeros = sb("zeros", [P, HC], F16)
        half_col = sb("half_col", [P, 1])
        code_u = sb("code_u", [P, T], U32)
        io_slot = sb("io_slot", [P, T])
        ii_slot = sb("ii_slot", [P, T])
        dst_f = sb("dst_f", [P, T])
        src_u = sb("src_u", [P, T], U32)
        dst_u = sb("dst_u", [P, T], U32)
        out_u = sb("out_u", [P, T], U32)
        keep = sb("keep", [P, T])
        goes_on = sb("goes_on", [P, T])
        dst_kept = sb("dst_kept", [P, T])
        out_scale = sb("out_scale", [P, NC])
        code = sb("code", [P, NC])

        s_const = sem("s_const")
        s_w = sem("s_w")


        signals = []
        with ExitStack() as ph:
            def sb(name, shape, dt=F32):
                return ph.enter_context(nc.sbuf_tensor(f"p1_{name}", shape, dt))

            def sem(name):
                signals.append(nc.alloc_semaphore(name))
                return signals[-1]

            s_padded, s_raw, s_rowf, s_rows, s_next = (
                sem("s_padded"), sem("s_raw"), sem("s_rowf"), sem("s_rows"), sem("s_next"))
            s_turned, s_slots, s_last, s_idx, s_chain, s_chain2 = (
                sem("s_turned"), sem("s_slots"), sem("s_last"), sem("s_idx"), sem("s_chain"), sem("s_chain2"))
            s_hot, s_hist, s_hist_end = sem("s_hot"), sem("s_hist"), sem("s_hist_end")
            s_pp, s_pre, s_root, s_extra = sem("s_pp"), sem("s_pre"), sem("s_root"), sem("s_extra")
            s_staged = sem("s_staged")
            s_prev, s_carr, s_carz, s_carw, s_carc = (
                sem("s_prev"), sem("s_carr"), sem("s_carz"), sem("s_carw"), sem("s_carc"))
            s_rest_a, s_rest_v, s_rest_p = sem("s_rest_a"), sem("s_rest_v"), sem("s_rest_p")
            s_xg = [sem(f"s_xg{u}") for u in range(RING)]
            s_xs = [sem(f"s_xs{u}") for u in range(RING)]
            s_x = [sem(f"s_x{u}") for u in range(RING)]
            s_a = [sem(f"s_a{u}") for u in range(RING)]
            s_xt, s_xtc, s_cen, s_sq = sem("s_xt"), sem("s_xtc"), sem("s_cen"), sem("s_sq")
            s_var, s_sd, s_rs, s_rsio, s_hs = sem("s_var"), sem("s_sd"), sem("s_rs"), sem("s_rsio"), sem("s_hs")

            iota_hi = sb("iota_hi", [P, NC], F16)
            before = sb("before", [P, P])
            last_row = sb("last_row", [P, P])
            src_f = sb("src_f", [P, T])
            next_f = sb("next_f", [P, T])
            src_lo = sb("src_lo", [P, T])
            src_hi = sb("src_hi", [P, T])
            dst_lo = sb("dst_lo", [P, T])
            dst_hi = sb("dst_hi", [P, T])
            dst_last = sb("dst_last", [P, T + 1])
            prev_col = sb("prev_col", [P, 2])
            carr = sb("carr", [P, 2, P])
            rest = sb("rest", [P, 4, D])
            rest_lhs = sb("rest_lhs", [D, P])
            raw = sb("raw", [P, 2, 2, P], I32)
            rowf = sb("rowf", [P, 2, 2, P])
            rown = sb("rown", [P, 2, P])
            bits = sb("bits", [P, 2, T], I32)
            bits_lo = sb("bits_lo", [P, 2, T], I32)
            bits_hi = sb("bits_hi", [P, 2, T], I32)
            bits_j = sb("bits_j", [P, 2, T], I32)
            hot_lo = sb("hot_lo", [P, GROUP, 2, P], F16)
            hot_hi = sb("hot_hi", [P, GROUP, 2, NC], F16)
            idx = sb("idx", [P, RING, GROUP], U32)
            xg = sb("xg", [P, RING, GROUP, D])
            in_cnt = sb("in_cnt", [P, NC])
            ends = sb("ends", [P, NC])
            nodes = sb("nodes", [P, NC])
            per_p = sb("per_p", [P, NBLK])
            base = sb("base", [P, NBLK])
            upto = sb("upto", [P, NBLK + 1])
            xin = sb("xin", [P, RING, 2, J, D])
            xT = sb("xT", [P, RING, 2, 4 * P])
            sq = sb("sq", [P, RING, 2, J * D])
            var = sb("var", [P, RING, 2 * J])
            sd = sb("sd", [P, RING, 2 * J])
            rs = sb("rs", [P, RING, 2 * J])
            rsio = sb("rsio", [P, RING, 2 * J])
            arow = sb("arow", [P, RING, 2, J, AROW])
            bank = [ph.enter_context(nc.psum_tensor(f"bank1_{k}", [P, 512], F32)) for k in range(8)]

            s_pace = sem("s_pace")
            with nc.Block() as block:
                @block.sync
                def _(sp):
                    for s in (s_xt, s_xtc, s_cen, s_sq, s_var, s_sd, s_rs, s_rsio, s_hs):
                        sp.sem_inc(s, RING)
                    sp.sem_inc(s_hist, GROUP)
                    sp.wait_ge(s_padded, 1)
                    for a, v in enumerate((src, dst)):
                        sp.dma_start(raw[:, a, 0, :], v[0:P * P].rearrange("(t p) -> t p", p=P)).then_inc(s_raw, 16)
                        sp.dma_start(raw[0:TL - 1, a, 1, :],
                                     v[P * P:(T - 1) * P].rearrange("(t p) -> t p", p=P)).then_inc(s_raw, 16)
                        sp.dma_start(raw[TL - 1:TL, a, 1, 0:EL],
                                     v[(T - 1) * P:E].rearrange("(t p) -> t p", t=1)).then_inc(s_raw, 16)
                    sp.wait_ge(s_rowf, 1)
                    r = dst_rows[0]
                    sp.dma_start(r[0:P * P].rearrange("(t p) -> t p", p=P), rowf[:, 1, 0, :]).then_inc(s_rows, 16)
                    sp.dma_start(r[P * P:SLOTS + P].rearrange("(t p) -> t p", p=P),
                                 rowf[0:TL + 1, 1, 1, :]).then_inc(s_rows, 16)
                    sp.wait_ge(s_rows, 32)
                    sp.dma_start(rown[:, 0, :], r[1:P * P + 1].rearrange("(t p) -> t p", p=P)).then_inc(s_next, 16)
                    sp.dma_start(rown[0:TL, 1, :],
                                 r[P * P + 1:SLOTS + 1].rearrange("(t p) -> t p", p=P)).then_inc(s_next, 16)
                    sp.dma_start(prev_col[1:P, 0:1], r[0:P * P].rearrange("(t p) -> t p", p=P)[0:P - 1, P - 1:P],
                                 allow_slow_non_contiguous=True).then_inc(s_prev, 16)
                    sp.dma_start(prev_col[0:TL, 1:2],
                                 r[(P - 1) * P:(T - 1) * P].rearrange("(t p) -> t p", p=P)[:, P - 1:P],
                                 allow_slow_non_contiguous=True).then_inc(s_prev, 16)
                    sp.dma_start(carried.rearrange("g t c -> (g t) c").rearrange("(p a) c -> p a c", a=2),
                                 sq[0:T // 2, 0]).then_inc(s_carz, 16)
                    sp.wait_ge(s_const, 2)
                    loads = 0
                    for to, w in ((gW1_2[0:D, 0:D], gW1), (gW1_2[D:P, D:P], gW1), (gW2_2[0:D, 0:D], gW2),
                                  (gW2_2[D:P, D:P], gW2), (sW4_2[0:D, 0:D], sW4), (sW4_2[D:P, D:P], sW4),
                                  (gW1_a[0:D, 0:D], gW1), (sW3_a[0:D, 0:D], sW3), (gW2_s[:], gW2),
                                  (sW1_s[:], sW1), (sW2_s[:], sW2)):
                        sp.dma_start(to, w).then_inc(s_w, 16)
                        loads += 1
                    for row, b, n in ((b1_rows, gb1, J), (b2_rows, gb2, J), (sb1_row, sb1, 1), (sb2_rows, sb2, GROUP),
                                      (sb4_rows, sb4, GROUP)):
                        sp.dma_start(row[:].rearrange("o (n d) -> o n d", d=D),
                                     b.rearrange("(o n d) -> o n d", o=1, n=1).broadcast_to([1, n, D])).then_inc(s_w, 16)
                        loads += 1
                    for full, b in ((b1_all, gb1), (b2_all, gb2), (sb3_all, sb3)):
                        sp.dma_start(full[:], b.rearrange("(o d) -> o d", o=1).broadcast_to([P, D])).then_inc(s_w, 16)
                        loads += 1
                    sp.dma_start(sb3_col[:], sb3.rearrange("(d o) -> d o", o=1),
                                 allow_slow_non_contiguous=True).then_inc(s_w, 16)
                    loads += 1

                    sp.wait_ge(s_carr, 1)
                    flat = carried_rows.rearrange("g t p -> (g t) p")
                    sp.dma_start(flat[0:P, :], carr[:, 0, :]).then_inc(s_carw, 16)
                    sp.dma_start(flat[P:T, :], carr[0:TL, 1, :]).then_inc(s_carw, 16)
                    sp.wait_ge(s_carw, 32)
                    sp.wait_ge(s_carz, 16)
                    for t in range(GROUP):
                        sp.dma_start(carried[:, t, t * P:(t + 1) * P], carried_rows[:, t, :]).then_inc(s_carc, 16)

                    def fetch(g, u):
                        if not (isinstance(g, int) and g < RING):
                            sp.wait_ge(s_xt, freed(g))
                        for k in range(2):
                            rows = PL if isinstance(g, int) and 2 * g + k == NBLK - 1 else P
                            sp.dma_start(xin[0:rows, u, k].rearrange("p j d -> p (j d)"), blocks(x, 2 * g + k, rows)).then_inc(s_x[u], 16)

                    def store(g, u, turn):
                        sp.wait_ge(s_hs, done(g))
                        for k in range(2):
                            rows = PL if isinstance(g, int) and 2 * g + k == NBLK - 1 else P
                            sp.dma_start(blocks(table_a, 2 * g + k, rows), arow[0:rows, u, k].rearrange("p j d -> p (j d)")).then_inc(s_a[u], 16)

                    each_group_ahead(sp, NG, fetch, store)
                    sp.wait_ge(s_w, 16 * loads)
                    sp.wait_ge(s_carc, 16 * GROUP)
                    sp.wait_ge(s_a[0], 32 * (PAIRS + 1))
                    sp.wait_ge(s_a[1], 32 * PAIRS)

                @block.gpsimd
                def _(pool):
                    max_node = pool.to_reg(N - 1)
                    max_row = pool.to_reg(SLOTS + N - 1)
                    pool.memset(ident[:], 0.0)
                    pool.memset(before[:], 0.0)
                    pool.memset(last_row[:], 0.0)
                    pool.memset(ones[:], 1.0)
                    pool.iota(iota_hi[:], pattern=[[1, NC]], base=0, channel_multiplier=0,
                              allow_small_or_imprecise_dtypes=True)
                    pool.iota(iota_lo[:], pattern=[[1, P]], base=0, channel_multiplier=0,
                              allow_small_or_imprecise_dtypes=True)
                    pool.iota(nodes[:].rearrange("p (b j) -> p b j", j=J), pattern=[[BLOCK, NBLK], [1, J]],
                              base=SLOTS, channel_multiplier=J,
                              allow_small_or_imprecise_dtypes=True).then_inc(s_chain, 1)
                    pool.wait_ge(s_chain, 1)
                    pool.affine_select(out=ident[:], in_=ident[:], compare_op=ALU.not_equal, fill=1.0, base=0,
                                       pattern=[[-1, P]], channel_multiplier=1)
                    pool.affine_select(out=before[:], in_=before[:], compare_op=ALU.is_ge, fill=1.0, base=0,
                                       pattern=[[-1, P]], channel_multiplier=1)
                    pool.affine_select(out=last_row[:], in_=last_row[:], compare_op=ALU.not_equal, fill=1.0,
                                       base=-(P - 1), pattern=[[0, P]], channel_multiplier=1).then_inc(s_const, 1)
                    pool.wait_ge(s_idx, 1)

                    def gather(g, u, turn):
                        pool.tensor_copy(idx[:, u, :], dst_u[:, bass.ds(g * GROUP, GROUP)]).then_inc(s_staged, 1)
                        pool.wait_ge(s_staged, g + 1)
                        pool.wait_ge(s_xs[u], 16 * turn)
                        pool.sem_inc(s_pace, 1)
                        for t in range(GROUP):
                            pool.indirect_dma_start(
                                xg[:, u, t, :], None, x, bass.IndirectOffsetOnAxis(ap=idx[:, u, t:t + 1], axis=0),
                                bounds_check=max_node, oob_is_err=False).then_inc(s_xg[u], 16)

                    def store(g, u, turn):
                        pool.wait_ge(s_xg[u], 16 * GROUP * (turn + 1))
                        pool.dma_start(x_dst[bass.ds(g * GC, GC), :].rearrange("(t p) d -> p t d", p=P),
                                       xg[:, u]).then_inc(s_xs[u], 16)

                    each_group_lead(pool, NG, gather, store)
                    pool.wait_ge(s_xs[0], 16 * (PAIRS + 1))
                    pool.wait_ge(s_xs[1], 16 * PAIRS)

                @block.tensor
                def _(pe):
                    pe.wait_ge(s_const, 2)
                    pe.wait_ge(s_rowf, 1)
                    for a in range(2):
                        pe.transpose(bank[4 + a][:, 0:P], rowf[:, a, 0, :], ident[:])
                        last = pe.transpose(bank[4 + a][:, P:T], rowf[0:TL, a, 1, :], ident[0:TL, 0:TL])
                    last.then_inc(s_turned, 1)
                    pe.wait_ge(s_next, 32)
                    pe.wait_ge(s_const, 2)
                    pe.transpose(bank[6][:, 0:P], rown[:, 0, :], ident[:])
                    pe.transpose(bank[6][:, P:T], rown[0:TL, 1, :], ident[0:TL, 0:TL]).then_inc(s_turned, 1)
                    pe.wait_ge(s_slots, 1)
                    pe.matmul(bank[7][:, 0:T], last_row[:], dst_f[:], start=True, stop=True).then_inc(s_last, 1)
                    pe.wait_ge(s_rest_v, 1)
                    pe.matmul(bank[5][:, 0:D], rest_lhs[:], sW4_2[0:D, 0:D], start=True, stop=False)
                    pe.matmul(bank[5][:, 0:D], ones[0:1, :], sb4_rows[:, 0:D], start=False, stop=True).then_inc(s_rest_p, 1)
                    for b in range(4):
                        pe.matmul(bank[b][:, 0:HC], zeros[:, 0:P], zeros[:], start=True, stop=False)
                    with pe.Fori(0, NG) as i:
                        for t in range(GROUP):
                            pe.wait_ge(s_hot, GROUP * i + t + 1)
                            for b in range(4):
                                last = pe.matmul(bank[b][:, 0:HC], hot_lo[:, t, b // 2, :],
                                                 hot_hi[:, t, b // 2, (b % 2) * HC:(b % 2 + 1) * HC],
                                                 start=False, stop=False)
                            last.then_inc(s_hist, 1)
                    for b in range(4):
                        last = pe.matmul(bank[b][:, 0:HC], zeros[:, 0:P], zeros[:], start=False, stop=True)
                    last.then_inc(s_hist_end, 1)
                    pe.wait_ge(s_pp, 1)
                    pe.matmul(bank[4][:, 0:NBLK], before[:], per_p[:], start=True, stop=True)
                    pe.matmul(bank[5][:, 0:NBLK], ones[:], per_p[:], start=True, stop=True).then_inc(s_pre, 1)
                    pe.wait_ge(s_extra, 1)

                    def turn_x(g, u, turn):
                        pe.wait_ge(s_x[u], 32 * (turn + 1))
                        pe.wait_ge(s_xtc, freed(g))
                        for k in range(2):
                            for q in range(4):
                                last = pe.transpose(bank[4 * u + 2 * k][:, q * P:(q + 1) * P],
                                                    xin[:, u, k, 2 * q:2 * q + 2, :].rearrange("p j d -> p (j d)"),
                                                    ident[:])
                        last.then_inc(s_xt, 1)

                    def center(g, u, turn):
                        pe.wait_ge(s_xtc, done(g))
                        pe.wait_ge(s_hs, freed(g))
                        for k in range(2):
                            for q in range(4):
                                last = pe.matmul(bank[4 * u + 2 * k + 1][:, q * P:(q + 1) * P],
                                                 xT[:, u, k, q * P:(q + 1) * P], center2[:], start=True, stop=True)
                        last.then_inc(s_cen, 1)

                    each_group_lead(pe, NG, turn_x, center)

                @block.scalar
                def _(act):
                    act.wait_ge(s_w, 16 * 20)
                    act.wait_ge(s_const, 2)

                    def half_softplus(y, r, n):
                        act.activation(r[0], y, ACT.Abs).then_inc(s_rest_a, 1)
                        act.wait_ge(s_rest_a, n + 1)
                        act.activation(r[1], r[0], ACT.Exp, scale=-1.0).then_inc(s_rest_a, 1)
                        act.wait_ge(s_rest_a, n + 2)
                        act.activation(r[0], r[1], ACT.Ln, bias=half_col[0:r[0].shape[0], :],
                                       scale=0.5).then_inc(s_rest_a, 1)

                    half_softplus(sb3_col[:], (rest[0:D, 0, 0:1], rest[0:D, 1, 0:1]), 0)
                    act.wait_ge(s_rest_p, 1)
                    half_softplus(bank[5][:, 0:D], (rest[:, 2, :], rest[:, 3, :]), 3)
                    act.wait_ge(s_hist_end, 1)
                    for b in range(2):
                        last = act.activation(ends[:, b * HC:(b + 1) * HC], bank[2 + b][:, 0:HC], ACT.Sqrt, bias=1.0)
                    last.then_inc(s_root, 1)

                    def square(g, u, turn):
                        act.wait_ge(s_xt, done(g))
                        act.wait_ge(s_cen, freed(g))
                        for k in range(2):
                            last = act.activation(xT[:, u, k, :], bank[4 * u + 2 * k][:], ACT.Copy)
                        last.then_inc(s_xtc, 1)
                        act.wait_ge(s_cen, done(g))
                        act.wait_ge(s_var, freed(g))
                        for k in range(2):
                            last = act.activation(sq[:, u, k, :], bank[4 * u + 2 * k + 1][:], ACT.Square, scale=0.125)
                        last.then_inc(s_sq, 1)

                    def deviation(g, u, turn):
                        act.wait_ge(s_var, done(g))
                        act.wait_ge(s_rs, freed(g))
                        act.activation(sd[:, u, :], var[:, u, :], ACT.Sqrt, bias=eps_col[:]).then_inc(s_sd, 1)

                    each_group_lead(act, NG, square, deviation)

                @block.vector
                def _(dve):
                    links = [0]

                    def link(ins):
                        links[0] += 1
                        ins.then_inc(s_chain2, 1)
                        dve.wait_ge(s_chain2, links[0])

                    dve.memset(raw[:], SKIP).then_inc(s_padded, 1)
                    for z in (gW1_2, gW2_2, sW4_2, gW1_a, sW3_a, center2):
                        dve.memset(z[:], 0.0)
                    dve.memset(arow[:], 1.0)
                    dve.memset(xin[:], 0.0)
                    dve.memset(sq[:], 0.0)
                    dve.memset(prev_col[:], -1.0)
                    dve.memset(half_col[:], 0.5)
                    dve.memset(upto[:, 0:1], 0.0)
                    dve.memset(eps_col[:], EPS)
                    dve.memset(ones_row[:], 1.0)
                    link(dve.memset(zeros[:], 0.0))
                    dve.memset(gW1_a[D:D + 1, D:D + 1], 1.0)
                    dve.memset(sW3_a[D:D + 1, D:D + 1], 1.0)
                    dve.memset(center2[0:D, 0:D], -1.0 / D)
                    dve.memset(dst_last[:, 0:1], -1.0)
                    link(dve.memset(center2[D:P, D:P], -1.0 / D))
                    dve.wait_ge(s_const, 1)
                    dve.tensor_tensor(center2[:], center2[:], ident[:], ALU.add).then_inc(s_const, 1)
                    dve.wait_ge(s_raw, 96)
                    dve.tensor_copy(rowf[:], raw[:]).then_inc(s_rowf, 1)
                    dve.wait_ge(s_turned, 1)
                    dve.tensor_copy(src_f[:], bank[4][:, 0:T])
                    dve.tensor_copy(dst_f[:], bank[5][:, 0:T]).then_inc(s_slots, 1)
                    dve.wait_ge(s_slots, 1)
                    link(dve.tensor_copy(dst_u[:], dst_f[:]))
                    dve.tensor_copy(src_u[:], src_f[:]).then_inc(s_idx, 1)
                    link(dve.tensor_tensor(keep[:], src_f[:], dst_f[:], ALU.not_equal))
                    link(dve.scalar_tensor_tensor(dst_kept[:], dst_f[:], 1.0, keep[:], ALU.add, ALU.mult))
                    dve.tensor_scalar(dst_kept[:], dst_kept[:], -1.0, None, ALU.add)
                    dve.tensor_copy(bits[:, 0, :], src_f[:])
                    link(dve.tensor_copy(bits[:, 1, :], dst_f[:]))
                    dve.tensor_scalar(bits_lo[:], bits[:], 3, P - 1, ALU.logical_shift_right, ALU.bitwise_and)
                    dve.tensor_scalar(bits_hi[:], bits[:], 10, 3, ALU.logical_shift_right, ALU.logical_shift_left)
                    link(dve.tensor_scalar(bits_j[:], bits[:], J - 1, None, ALU.bitwise_and))
                    link(dve.tensor_tensor(bits_hi[:], bits_hi[:], bits_j[:], ALU.bitwise_or))
                    dve.tensor_copy(src_lo[:], bits_lo[:, 0, :])
                    dve.tensor_copy(dst_lo[:], bits_lo[:, 1, :])
                    dve.tensor_copy(src_hi[:], bits_hi[:, 0, :])
                    link(dve.tensor_copy(dst_hi[:], bits_hi[:, 1, :]))
                    dve.wait_ge(s_rest_a, 3)
                    link(dve.scalar_tensor_tensor(rest[0:D, 1, 0:1], sb3_col[:], 0.0, rest[0:D, 0, 0:1], ALU.max,
                                                  ALU.add))
                    dve.tensor_scalar(rest_lhs[:], ones[0:D, :], rest[0:D, 1, 0:1], None,
                                      ALU.mult).then_inc(s_rest_v, 1)
                    dve.wait_ge(s_rest_a, 6)
                    dve.scalar_tensor_tensor(rest_row[:], bank[5][:, 0:D], 0.0, rest[:, 2, :], ALU.max, ALU.add)
                    dve.wait_ge(s_last, 1)
                    link(dve.tensor_copy(dst_last[:, 1:T + 1], bank[7][:, 0:T]))
                    dve.tensor_tensor(goes_on[:], dst_last[:, 1:T + 1], dst_last[:, 0:T], ALU.is_equal)
                    dve.wait_ge(s_prev, 32)
                    dve.tensor_scalar(carr[:, 0, :], rowf[:, 1, 0, :], prev_col[:, 0:1], None, ALU.is_equal)
                    dve.tensor_scalar(carr[0:TL, 1, :], rowf[0:TL, 1, 1, :], prev_col[0:TL, 1:2], None,
                                      ALU.is_equal).then_inc(s_carr, 1)
                    dve.wait_ge(s_turned, 2)
                    link(dve.tensor_tensor(next_f[:], bank[6][:, 0:T], dst_f[:], ALU.is_equal))
                    link(dve.scalar_tensor_tensor(next_f[:], next_f[:], float(SKIP), dst_f[:], ALU.mult, ALU.add))
                    link(dve.tensor_copy(out_u[:], next_f[:]))
                    with dve.Fori(0, NG) as i:
                        for t in range(GROUP):
                            n = GROUP * i + t
                            dve.wait_ge(s_hist, n + 1)
                            dve.tensor_scalar(hot_lo[:, t, 0, :], iota_lo[:], dst_lo[:, bass.ds(n, 1)], None,
                                              ALU.is_equal)
                            dve.tensor_scalar(hot_lo[:, t, 1, :], iota_lo[:], src_lo[:, bass.ds(n, 1)],
                                              keep[:, bass.ds(n, 1)], ALU.is_equal, ALU.mult)
                            dve.tensor_scalar(hot_hi[:, t, 0, :], iota_hi[:], dst_hi[:, bass.ds(n, 1)], None,
                                              ALU.is_equal)
                            dve.tensor_scalar(hot_hi[:, t, 1, :], iota_hi[:], src_hi[:, bass.ds(n, 1)], None,
                                              ALU.is_equal).then_inc(s_hot, 1)
                    dve.wait_ge(s_hist_end, 1)
                    for b in range(2):
                        half = slice(b * HC, (b + 1) * HC)
                        link(dve.tensor_copy(in_cnt[:, half], bank[b][:, 0:HC]))
                    dve.wait_ge(s_root, 1)
                    link(dve.reciprocal(out_scale[:], ends[:]))
                    dve.tensor_reduce(per_p[:], in_cnt[:].rearrange("p (b j) -> p b j", j=J), AX_X,
                                      ALU.add).then_inc(s_pp, 1)
                    dve.wait_ge(s_pre, 1)
                    link(dve.tensor_tensor_scan(upto[:, 1:NBLK + 1], ones[:, 0:NBLK], bank[5][:, 0:NBLK], 0.0,
                                                ALU.mult, ALU.add))
                    link(dve.tensor_tensor(base[:], bank[4][:, 0:NBLK], upto[:, 0:NBLK], ALU.add))
                    ends_v = ends[:].rearrange("p (b j) -> p b j", j=J)
                    cnt_v = in_cnt[:].rearrange("p (b j) -> p b j", j=J)
                    for j in range(J):
                        link(dve.tensor_tensor(ends_v[:, :, j], cnt_v[:, :, j],
                                               base[:] if j == 0 else ends_v[:, :, j - 1], ALU.add))
                    link(dve.scalar_tensor_tensor(ends[:], ends[:], -1.0, nodes[:], ALU.add, ALU.subtract))
                    link(dve.scalar_tensor_tensor(ends[:], in_cnt[:], 0.0, ends[:], ALU.is_gt, ALU.mult))
                    dve.tensor_tensor(code[:], ends[:], nodes[:], ALU.add).then_inc(s_extra, 1)
                    dve.wait_ge(s_extra, 1)

                    def variance(g, u, turn):
                        dve.wait_ge(s_sq, done(g))
                        dve.wait_ge(s_sd, freed(g))
                        dve.tensor_reduce(var[:, u, :], sq[:, u].rearrange("p k (j d) -> p (k j) d", d=D), AX_X,
                                          ALU.add).then_inc(s_var, 1)

                    def scale(g, u, turn):
                        dve.wait_ge(s_sd, done(g))
                        dve.reciprocal(rs[:, u, :], sd[:, u, :]).then_inc(s_rs, 1)
                        dve.wait_ge(s_rs, done(g))
                        dve.tensor_tensor(rsio[:, u, :], rs[:, u, :], out_scale[:, bass.ds(g * 2 * J, 2 * J)],
                                          ALU.mult).then_inc(s_rsio, 1)
                        dve.wait_ge(s_a[u], 32 * turn)
                        dve.tensor_copy(arow[:, u, :, :, D + 1].rearrange("p k j -> p (k j)"),
                                        code[:, bass.ds(g * 2 * J, 2 * J)])
                        dve.wait_ge(s_rsio, done(g))
                        for k in range(2):
                            last = dve.scalar_tensor_tensor(
                                arow[:, u, k, :, 0:D], bank[4 * u + 2 * k + 1][:].rearrange("p (j d) -> p j d", d=D),
                                0.0, rsio[:, u, k * J:(k + 1) * J].unsqueeze(2).broadcast_to([P, J, D]),
                                ALU.max, ALU.mult)
                        last.then_inc(s_hs, 1)

                    each_group_lead(dve, NG, variance, scale)

        nc.clear_and_free_semaphores(signals)
        nc.all_engine_barrier()


        z_slot = ctx.enter_context(nc.sbuf_tensor("z_slot", [P, T, D + 1], F32))
        self_slot = ctx.enter_context(nc.sbuf_tensor("self_slot", [P, T, D], F32))
        signals = []
        with ExitStack() as ph:
            def sb(name, shape, dt=F32):
                return ph.enter_context(nc.sbuf_tensor(f"p2_{name}", shape, dt))

            def sem(name):
                signals.append(nc.alloc_semaphore(name))
                return signals[-1]

            bank_names = ("agg", "z", "slots", "xd", "t0", "z0", "t1", "z1")
            agg, zb, slots_b, xb, t0, z0, t1, z1 = [
                ph.enter_context(nc.psum_tensor(f"bank2_{n}", [P, 512], F32)) for n in bank_names]
            tb, zbk = (t0, t1), (z0, z1)

            idx = sb("idx", [P, RING, GROUP], U32)
            msg = sb("msg", [P, RING, GROUP, AROW])
            rows = sb("rows", [P, RING, GC])
            car = sb("car", [GROUP, RING, GC])
            seg = sb("seg", [P, RING, GROUP, P])
            carry = sb("carry", [D + 1, RING, GROUP + 1])
            crow = sb("crow", [GROUP, RING, D + 1])
            aggs = sb("aggs", [D + 1, RING, GC])
            code_i = sb("code_i", [P, RING, 3, GROUP], I32)
            code_f = sb("code_f", [P, RING, 2, GROUP])
            shot_lo = sb("shot_lo", [P, RING, GROUP, P], F16)
            shot_hi = sb("shot_hi", [P, RING, GROUP, T], F16)
            iota_t = sb("iota_t", [P, T], F16)
            hin = sb("hin", [P, RING, 2, J, D])
            xin = sb("xin", [P, RING, 2, J * D])
            hT = sb("hT", [P, 2, 4 * P])
            h1 = sb("h1", [P, RING, 2, J * D])
            rel = sb("rel", [P, 2, J * D])
            x1 = sb("x1", [P, RING, 2, J * D])
            res = sb("res", [P, RING, 2, J * D])
            xd = sb("xd", [P, RING, GROUP, D])
            xdT = sb("xdT", [P, 2 * P])
            xvar = sb("xvar", [P, GROUP])
            xsd = sb("xsd", [P, GROUP])
            xrs = sb("xrs", [P, GROUP])
            xh = sb("xh", [P, GROUP * D])
            xhT = sb("xhT", [P, 2 * P])

            s_iota2 = sem("s_iota2")
            s_staged = sem("s2_staged")
            s_msg = [sem(f"s2_msg{u}") for u in range(RING)]
            s_in = [sem(f"s2_in{u}") for u in range(RING)]
            s_nd = [sem(f"s2_nd{u}") for u in range(RING)]
            s_xd = [sem(f"s2_xd{u}") for u in range(RING)]
            s_st = [sem(f"s2_st{u}") for u in range(RING)]
            s_so = [sem(f"s2_so{u}") for u in range(RING)]
            stages = {n: sem("s2_" + n) for n in (
                "seg", "agg", "scan", "crT", "crow", "carried", "aggs", "z", "zs", "codei", "codes", "hot", "slot", "hotf",
                "t1", "t1c", "w1", "y", "h1", "t2", "t2c", "w2", "rel", "h2", "x1", "res",
                "xt", "xtc", "xcen", "xsq", "xvar", "xsd", "xrs", "xh", "xt2", "xt2c", "xw", "xws")}
            S = stages
            s_link, s_link2 = sem("s2_link"), sem("s2_link2")

            s_pace = sem("s2_pace")
            with nc.Block() as block:
                @block.sync
                def _(sp):
                    for s in S.values():
                        sp.sem_inc(s, RING)

                    def fetch(g, u):
                        last = isinstance(g, int) and g == NG - 1
                        if not (isinstance(g, int) and g < RING):
                            sp.wait_ge(S["carried"], freed(g))
                            sp.wait_ge(S["seg"], freed(g))
                        sp.dma_start(rows[:, u], dst_rows[:, bass.ds(g * GC, GC)].broadcast_to([P, GC])).then_inc(s_in[u], 16)
                        sp.dma_start(car[:, u], carried[bass.ds(g, 1)].rearrange("o t c -> (o t) c")).then_inc(s_in[u], 16)
                        if not (isinstance(g, int) and g < RING):
                            sp.wait_ge(S["t1"], freed(g))
                            sp.wait_ge(S["x1"], freed(g))
                        for k, n in ((0, P), (1, PL if last else P)):
                            sp.dma_start(hin[0:n, u, k], table_a[bass.ds((2 * g + k) * BLOCK, n * J), 0:D].rearrange(
                                "(p j) d -> p j d", j=J)).then_inc(s_nd[u], 16)
                            sp.dma_start(xin[0:n, u, k], blocks(x, 2 * g + k, n)).then_inc(s_nd[u], 16)
                        if not (isinstance(g, int) and g < RING):
                            sp.wait_ge(S["xt"], freed(g))
                        sp.dma_start(xd[:, u], tiles(x_dst, g)).then_inc(s_xd[u], 16)

                    def store(g, u, turn):
                        sp.wait_ge(S["h1"], done(g))
                        sp.dma_start(both(local_h, g), h1[:, u]).then_inc(s_st[u], 16)
                        sp.wait_ge(S["res"], done(g))
                        sp.dma_start(both(local_x, g), x1[:, u]).then_inc(s_st[u], 16)
                        if isinstance(g, int) and g == NG - 1:
                            sp.dma_start(blocks(out, 2 * g, P), res[:, u, 0]).then_inc(s_so[u], 16)
                            sp.dma_start(blocks(out, 2 * g + 1, PL), res[0:PL, u, 1]).then_inc(s_so[u], 16)
                        else:
                            sp.dma_start(both(out, g), res[:, u]).then_inc(s_so[u], 16)

                    each_group_ahead(sp, NG, fetch, store)
                    sp.wait_ge(s_st[0], 32 * (PAIRS + 1))
                    sp.wait_ge(s_st[1], 32 * PAIRS)
                    sp.wait_ge(s_so[0], 16 * (PAIRS + 2))
                    sp.wait_ge(s_so[1], 16 * PAIRS)

                @block.gpsimd
                def _(pool):
                    max_node = pool.to_reg(N - 1)
                    pool.iota(iota_t[:], pattern=[[1, T]], base=0, channel_multiplier=0,
                              allow_small_or_imprecise_dtypes=True).then_inc(s_iota2, 1)

                    def gather(g, u):
                        if not (isinstance(g, int) and g < RING):
                            pool.wait_ge(S["agg"], freed(g))
                            pool.wait_ge(S["codei"], freed(g))
                        pool.tensor_copy(idx[:, u, :], src_u[:, bass.ds(g * GROUP, GROUP)]).then_inc(s_staged, 1)
                        pool.wait_ge(s_staged, g + 1)
                        pool.sem_inc(s_pace, 1)
                        for t in range(GROUP):
                            pool.indirect_dma_start(
                                msg[:, u, t, :], None, table_a,
                                bass.IndirectOffsetOnAxis(ap=idx[:, u, t:t + 1], axis=0),
                                bounds_check=max_node, oob_is_err=False).then_inc(s_msg[u], 16)

                    def add_rest(g, u, turn):
                        pool.wait_ge(S["x1"], done(g))
                        pool.wait_ge(s_so[u], 16 * turn)
                        for k in range(2):
                            last = pool.tensor_tensor(
                                res[:, u, k].rearrange("p (j d) -> p j d", d=D),
                                x1[:, u, k].rearrange("p (j d) -> p j d", d=D),
                                rest_row[:].unsqueeze(1).broadcast_to([P, J, D]), ALU.add)
                        last.then_inc(S["res"], 1)

                    each_group_ahead(pool, NG, gather, add_rest)

                @block.tensor
                def _(pe):
                    pe.matmul(slots_b[:, 0:T], zeros[:, 0:P], zeros[:, 0:T], start=True, stop=False)

                    def group(g, u, turn):
                        pe.wait_ge(s_nd[u], 64 * (turn + 1))
                        pe.wait_ge(S["t2c"], done(g - 1))
                        for k in range(2):
                            for q in range(4):
                                last = pe.transpose(tb[k][:, q * P:(q + 1) * P], 
                                                    hin[:, u, k, 2 * q:2 * q + 2, :].rearrange("p j d -> p (j d)"), ident[:])
                        last.then_inc(S["t1"], 1)
                        pe.wait_ge(s_xd[u], 16 * (turn + 1))
                        pe.wait_ge(S["xws"], done(g - 1))
                        for q in range(2):
                            last = pe.transpose(xb[:, q * P:(q + 1) * P],
                                                xd[:, u, 2 * q:2 * q + 2, :].rearrange("p t d -> p (t d)"), ident[:])
                        last.then_inc(S["xt"], 1)
                        pe.wait_ge(s_msg[u], 16 * GROUP * (turn + 1))
                        pe.wait_ge(S["seg"], done(g))
                        pe.wait_ge(S["aggs"], done(g - 1))
                        for t in range(GROUP):
                            last = pe.matmul(agg[0:D + 1, t * P:(t + 1) * P], msg[:, u, t, 0:D + 1], seg[:, u, t, :],
                                             start=(t == 0), stop=False, skip_group_check=True)
                        last.then_inc(S["agg"], 1)
                        pe.wait_ge(S["t1c"], done(g))
                        pe.wait_ge(S["rel"], done(g - 1))
                        pe.wait_ge(S["h2"], done(g - 1))
                        for k in range(2):
                            for q in range(4):
                                pe.matmul(zbk[k][:, q * P:(q + 1) * P], hT[:, k, q * P:(q + 1) * P], gW1_2[:],
                                          start=(q == 0), stop=False, skip_group_check=True)
                            last = pe.matmul(zbk[k][:], ones[0:1, :], b1_rows[:], start=False, stop=True,
                                             skip_group_check=True)
                        last.then_inc(S["w1"], 1)
                        pe.wait_ge(S["xtc"], done(g))
                        for q in range(2):
                            last = pe.matmul(xb[:, (2 + q) * P:(3 + q) * P], xdT[:, q * P:(q + 1) * P], center2[:],
                                             start=True, stop=True)
                        last.then_inc(S["xcen"], 1)
                        pe.wait_ge(S["scan"], done(g))
                        pe.wait_ge(S["zs"], done(g - 1))
                        pe.transpose(zb[0:GROUP, 0:D + 1], carry[:, u, 0:GROUP],
                                     ident[0:D + 1, 0:D + 1]).then_inc(S["crT"], 1)
                        pe.wait_ge(S["hot"], done(g))
                        for t in range(GROUP):
                            last = pe.matmul(slots_b[:, 0:T], shot_lo[:, u, t, :], shot_hi[:, u, t, :],
                                             start=False, stop=False)
                        last.then_inc(S["slot"], 1)
                        pe.wait_ge(S["h1"], done(g))
                        for k in range(2):
                            for q in range(4):
                                last = pe.transpose(tb[k][:, q * P:(q + 1) * P], h1[:, u, k, q * P:(q + 1) * P], ident[:])
                        last.then_inc(S["t2"], 1)
                        pe.wait_ge(S["crow"], done(g))
                        pe.wait_ge(s_in[u], 32 * (turn + 1))
                        pe.matmul(agg[0:D + 1, :], crow[:, u, :], car[:, u, :], start=False, stop=True,
                                  skip_group_check=True).then_inc(S["carried"], 1)
                        pe.wait_ge(S["xh"], done(g))
                        for q in range(2):
                            last = pe.transpose(xb[:, q * P:(q + 1) * P], xh[:, q * P:(q + 1) * P], ident[:])
                        last.then_inc(S["xt2"], 1)
                        pe.wait_ge(S["t2c"], done(g))
                        for k in range(2):
                            for q in range(4):
                                pe.matmul(zbk[k][:, q * P:(q + 1) * P], hT[:, k, q * P:(q + 1) * P], gW2_2[:],
                                          start=(q == 0), stop=False, skip_group_check=True)
                            last = pe.matmul(zbk[k][:], ones[0:1, :], b2_rows[:], start=False, stop=True,
                                             skip_group_check=True)
                        last.then_inc(S["w2"], 1)
                        pe.wait_ge(S["aggs"], done(g))
                        for t in range(GROUP):
                            last = pe.matmul(zb[:, t * (D + 1):(t + 1) * (D + 1)], aggs[:, u, t * P:(t + 1) * P], gW1_a[:],
                                             start=True, stop=True)
                        last.then_inc(S["z"], 1)
                        pe.wait_ge(S["xt2c"], done(g))
                        for q in range(2):
                            last = pe.matmul(xb[:, (2 + q) * P:(3 + q) * P], xhT[:, q * P:(q + 1) * P], gW1_2[:],
                                             start=True, stop=True)
                        last.then_inc(S["xw"], 1)

                    each_group(pe, NG, group)
                    pe.matmul(slots_b[:, 0:T], zeros[:, 0:P], zeros[:, 0:T], start=False, stop=True).then_inc(s_link, 1)

                @block.scalar
                def _(act):
                    def group(g, u, turn):
                        act.wait_ge(S["t1"], done(g))
                        act.wait_ge(S["w2"], done(g - 1))
                        for k in range(2):
                            last = act.activation(hT[:, k], tb[k][:], ACT.Copy)
                        last.then_inc(S["t1c"], 1)
                        act.wait_ge(S["xt"], done(g))
                        act.wait_ge(S["xcen"], done(g - 1))
                        act.activation(xdT[:], xb[:, 0:2 * P], ACT.Copy).then_inc(S["xtc"], 1)
                        act.wait_ge(S["xcen"], done(g))
                        act.wait_ge(S["xt2"], done(g - 1))
                        act.activation(xh[:], xb[:, 2 * P:4 * P], ACT.Square, scale=0.125).then_inc(S["xsq"], 1)
                        act.wait_ge(S["xvar"], done(g))
                        act.wait_ge(S["xrs"], done(g - 1))
                        act.activation(xsd[:], xvar[:], ACT.Sqrt, bias=eps_col[:]).then_inc(S["xsd"], 1)
                        act.wait_ge(S["t2"], done(g))
                        act.wait_ge(S["w1"], done(g))
                        for k in range(2):
                            last = act.activation(hT[:, k], tb[k][:], ACT.Copy)
                        last.then_inc(S["t2c"], 1)
                        act.wait_ge(S["carried"], done(g))
                        act.wait_ge(S["z"], freed(g))
                        act.activation(aggs[:, u], agg[0:D + 1, :], ACT.Copy).then_inc(S["aggs"], 1)
                        act.wait_ge(S["xt2"], done(g))
                        act.wait_ge(S["xw"], done(g - 1))
                        act.activation(xhT[:], xb[:, 0:2 * P], ACT.Copy).then_inc(S["xt2c"], 1)
                        act.wait_ge(S["w2"], done(g))
                        act.wait_ge(S["h2"], done(g - 1))
                        for k in range(2):
                            last = act.activation(rel[:, k], zbk[k][:], ACT.Relu, scale=1.0 - SLOPE)
                        last.then_inc(S["rel"], 1)
                        act.wait_ge(S["z"], done(g))
                        act.activation(z_slot[:, bass.ds(g * GROUP, GROUP), :],
                                       zb[:, 0:GROUP * (D + 1)].rearrange("p (t d) -> p t d", d=D + 1),
                                       ACT.Copy).then_inc(S["zs"], 1)
                        act.wait_ge(S["xw"], done(g))
                        act.activation(self_slot[:, bass.ds(g * GROUP, GROUP), :],
                                       xb[:, 2 * P:4 * P].rearrange("p (t d) -> p t d", d=D),
                                       ACT.Copy).then_inc(S["xws"], 1)

                    each_group(act, NG, group)

                @block.vector
                def _(dve):
                    dve.memset(carry[:], 0.0).then_inc(s_link2, 1)
                    dve.wait_ge(s_link2, 1)
                    dve.wait_ge(s_iota2, 1)

                    def group(g, u, turn):
                        cols = bass.ds(g * GROUP, GROUP)
                        dve.wait_ge(s_in[u], 32 * (turn + 1))
                        dve.wait_ge(S["agg"], freed(g))
                        dve.tensor_tensor(seg[:, u], rows[:, u].rearrange("p (t i) -> p t i", i=P),
                                          dst_kept[:, cols].unsqueeze(2).broadcast_to([P, GROUP, P]),
                                          ALU.is_equal).then_inc(S["seg"], 1)
                        dve.wait_ge(s_msg[u], 16 * GROUP * (turn + 1))
                        dve.wait_ge(S["codes"], freed(g))
                        dve.tensor_copy(code_u[:, cols], msg[:, u, :, D + 1])
                        dve.tensor_copy(code_i[:, u, 0], msg[:, u, :, D + 1]).then_inc(S["codei"], 1)
                        dve.wait_ge(S["codei"], done(g))
                        dve.tensor_scalar(code_i[:, u, 1], code_i[:, u, 0], P - 1, None, ALU.bitwise_and)
                        dve.tensor_scalar(code_i[:, u, 2], code_i[:, u, 0], 7, None,
                                          ALU.logical_shift_right).then_inc(S["codes"], 1)
                        dve.wait_ge(S["w1"], done(g))
                        dve.wait_ge(s_st[u], 32 * turn)
                        dve.wait_ge(S["t2"], freed(g))
                        for k in range(2):
                            last = dve.tensor_tensor(
                                h1[:, u, k].rearrange("p (j d) -> p j d", d=D),
                                zbk[k][:].rearrange("p (j d) -> p j d", d=D),
                                out_scale[:, bass.ds(g * 2 * J + k * J, J)].unsqueeze(2).broadcast_to([P, J, D]),
                                ALU.mult)
                        last.then_inc(S["y"], 1)
                        dve.wait_ge(S["agg"], done(g))
                        dve.wait_ge(S["crT"], freed(g))
                        dve.wait_ge(S["scan"], done(g - 1))
                        dve.tensor_copy(carry[:, u, 0:1], carry[:, 1 - u, GROUP:GROUP + 1])
                        dve.tensor_tensor_scan(carry[:, u, 1:GROUP + 1], goes_on[0:D + 1, cols],
                                               agg[0:D + 1].rearrange("p (t i) -> p t i", i=P)[:, :, P - 1],
                                               carry[:, 1 - u, GROUP:GROUP + 1], ALU.mult,
                                               ALU.add).then_inc(S["scan"], 1)
                        dve.wait_ge(S["codes"], done(g))
                        dve.wait_ge(S["hotf"], freed(g))
                        dve.tensor_copy(code_f[:, u], code_i[:, u, 1:3]).then_inc(S["hotf"], 1)
                        dve.wait_ge(S["y"], done(g))
                        for k in range(2):
                            last = dve.scalar_tensor_tensor(h1[:, u, k], h1[:, u, k], SLOPE, h1[:, u, k],
                                                            ALU.mult, ALU.max)
                        last.then_inc(S["h1"], 1)
                        dve.wait_ge(S["crT"], done(g))
                        dve.wait_ge(S["carried"], freed(g))
                        dve.tensor_copy(crow[:, u], zb[0:GROUP, 0:D + 1]).then_inc(S["crow"], 1)
                        dve.wait_ge(S["xsq"], done(g))
                        dve.wait_ge(S["xsd"], done(g - 1))
                        dve.tensor_reduce(xvar[:], xh[:].rearrange("p (t d) -> p t d", d=D), AX_X,
                                          ALU.add).then_inc(S["xvar"], 1)
                        dve.wait_ge(S["hotf"], done(g))
                        dve.wait_ge(S["slot"], freed(g))
                        for t in range(GROUP):
                            dve.tensor_scalar(shot_lo[:, u, t], iota_lo[:], code_f[:, u, 0, t:t + 1],
                                              keep[:, bass.ds(g * GROUP + t, 1)], ALU.is_equal, ALU.mult)
                            last = dve.tensor_scalar(shot_hi[:, u, t], iota_t[:], code_f[:, u, 1, t:t + 1], None,
                                                     ALU.is_equal)
                        last.then_inc(S["hot"], 1)
                        dve.wait_ge(S["xsd"], done(g))
                        dve.reciprocal(xrs[:], xsd[:]).then_inc(S["xrs"], 1)
                        dve.wait_ge(S["xrs"], done(g))
                        dve.wait_ge(S["xt2"], done(g - 1))
                        dve.scalar_tensor_tensor(xh[:].rearrange("p (t d) -> p t d", d=D),
                                                 xb[:, 2 * P:4 * P].rearrange("p (t d) -> p t d", d=D), 0.0,
                                                 xrs[:].unsqueeze(2).broadcast_to([P, GROUP, D]), ALU.max,
                                                 ALU.mult).then_inc(S["xh"], 1)
                        dve.wait_ge(S["rel"], done(g))
                        for k in range(2):
                            last = dve.scalar_tensor_tensor(rel[:, k], zbk[k][:], SLOPE, rel[:, k], ALU.mult, ALU.add)
                        last.then_inc(S["h2"], 1)
                        dve.wait_ge(S["h2"], done(g))
                        dve.wait_ge(S["res"], freed(g))
                        dve.wait_ge(s_st[u], 32 * turn)
                        for k in range(2):
                            last = dve.tensor_tensor(x1[:, u, k], rel[:, k], xin[:, u, k], ALU.add)
                        last.then_inc(S["x1"], 1)

                    each_group(dve, NG, group)
                    dve.wait_ge(s_link, 1)
                    dve.tensor_copy(io_slot[:], slots_b[:, 0:T]).then_inc(s_link2, 1)
                    dve.wait_ge(s_link2, 2)

        nc.clear_and_free_semaphores(signals)
        nc.all_engine_barrier()


        CH = T // 7
        assert T == 7 * CH
        signals = []
        with ExitStack() as ph:
            def sb(name, shape, dt=F32):
                return ph.enter_context(nc.sbuf_tensor(f"p3_{name}", shape, dt))

            def sem(name):
                signals.append(nc.alloc_semaphore(name))
                return signals[-1]

            root = sb("root", [P, 2, T])
            s_root, s_inv, s_io, s_sum, s_ii, s_b, s_leak, s_h, s_st3 = (
                sem("s3_root"), sem("s3_inv"), sem("s3_io"), sem("s3_sum"), sem("s3_ii"), sem("s3_b"),
                sem("s3_leak"), sem("s3_h"), sem("s3_st"))

            with nc.Block() as block:
                def wide(col, c):
                    return col[:, bass.ds(c * CH, CH)].unsqueeze(2).broadcast_to([P, CH, D])

                @block.scalar
                def _(act):
                    act.activation(root[:, 0], io_slot[:], ACT.Sqrt, bias=1.0)
                    act.activation(root[:, 1], z_slot[:, :, D], ACT.Sqrt, bias=1.0).then_inc(s_root, 1)

                @block.gpsimd
                def _(pool):
                    pool.wait_ge(s_inv, 1)
                    with pool.Fori(0, 7) as c:
                        h = self_slot[:, bass.ds(c * CH, CH), :]
                        pool.tensor_tensor(h, h, wide(io_slot, c), ALU.mult).then_inc(s_io, 1)
                    with pool.Fori(0, 7) as c:
                        h = self_slot[:, bass.ds(c * CH, CH), :]
                        pool.wait_ge(s_leak, c + 1)
                        pool.tensor_tensor(h, h, wide(io_slot, c), ALU.mult).then_inc(s_h, 1)

                @block.vector
                def _(dve):
                    dve.wait_ge(s_root, 1)
                    dve.reciprocal(io_slot[:], root[:, 0])
                    dve.reciprocal(ii_slot[:], root[:, 1]).then_inc(s_inv, 1)
                    dve.wait_ge(s_inv, 1)
                    with dve.Fori(0, 7) as c:
                        h = self_slot[:, bass.ds(c * CH, CH), :]
                        dve.wait_ge(s_io, c + 1)
                        dve.tensor_tensor(h, h, z_slot[:, bass.ds(c * CH, CH), 0:D], ALU.add).then_inc(s_sum, 1)
                        dve.wait_ge(s_sum, c + 1)
                        dve.tensor_tensor(h, h, wide(ii_slot, c), ALU.mult).then_inc(s_ii, 1)
                        dve.wait_ge(s_ii, c + 1)
                        dve.tensor_tensor(h, h, b1_all[:].unsqueeze(1).broadcast_to([P, CH, D]),
                                          ALU.add).then_inc(s_b, 1)
                        dve.wait_ge(s_b, c + 1)
                        dve.scalar_tensor_tensor(h, h, SLOPE, h, ALU.mult, ALU.max).then_inc(s_leak, 1)

                @block.sync
                def _(sp):
                    with sp.Fori(0, 7) as c:
                        sp.wait_ge(s_h, c + 1)
                        sp.dma_start(table_h[bass.ds(c * CH * P, CH * P), :].rearrange("(t p) d -> p t d", p=P),
                                     self_slot[:, bass.ds(c * CH, CH), :]).then_inc(s_st3, 16)
                    sp.wait_ge(s_st3, 16 * 7)

        nc.clear_and_free_semaphores(signals)
        nc.all_engine_barrier()


        signals = []
        with ExitStack() as ph:
            def sb(name, shape, dt=F32):
                return ph.enter_context(nc.sbuf_tensor(f"p4_{name}", shape, dt))

            def sem(name):
                signals.append(nc.alloc_semaphore(name))
                return signals[-1]

            agg, zb, hdb, etb, e1b, e2b = [
                ph.enter_context(nc.psum_tensor(f"bank4_{n}", [P, 512], F32))
                for n in ("agg", "z", "hd", "et", "e1", "e2")]
            idx = sb("idx", [P, RING, GROUP], U32)
            msg = sb("msg", [P, RING, GROUP, D])
            rows = sb("rows", [P, RING, GC])
            car = sb("car", [GROUP, RING, GC])
            seg = sb("seg", [P, RING, GROUP, P])
            carry = sb("carry", [D + 1, RING, GROUP + 1])
            crow = sb("crow", [GROUP, RING, D])
            aggs = sb("aggs", [D, RING, GC])
            hd = sb("hd", [P, RING, GROUP, D])
            hdT = sb("hdT", [P, RING, 2 * P])
            xd = sb("xd", [P, RING, GROUP, D])
            y = sb("y", [P, 3, GROUP * D])
            x1 = sb("x1", [P, RING, GROUP, D])
            er = sb("er", [P, RING, GROUP, R])
            eh = sb("eh", [P, RING, GROUP, D])
            erT = sb("erT", [P, GC])
            pa = sb("pa", [D, 2, GC])
            w1 = sb("w1", [D, GC])
            pb_ = sb("pb_", [P, 2, GROUP * D])
            w2 = sb("w2", [P, GROUP * D])

            s_staged = sem("s4_staged")
            s_msg = [sem(f"s4_msg{u}") for u in range(RING)]
            s_in = [sem(f"s4_in{u}") for u in range(RING)]
            s_sl = [sem(f"s4_sl{u}") for u in range(RING)]
            s_ed = [sem(f"s4_ed{u}") for u in range(RING)]
            s_st = [sem(f"s4_st{u}") for u in range(RING)]
            s_link = sem("s4_link")
            S = {n: sem("s4_" + n) for n in (
                "seg", "agg", "scan", "crT", "crow", "carried", "aggs", "hd", "hdT", "z", "y0", "y1", "y2", "x1",
                "et", "etc", "e1", "e1a", "e1e", "e1l", "w1", "e2", "e2a", "e2e", "e2l", "w2", "w")}

            s_pace = sem("s4_pace")
            with nc.Block() as block:
                @block.sync
                def _(sp):
                    for s in S.values():
                        sp.sem_inc(s, RING)

                    def fetch(g, u):
                        first = isinstance(g, int) and g < RING
                        if not first:
                            sp.wait_ge(S["carried"], freed(g))
                            sp.wait_ge(S["seg"], freed(g))
                        sp.dma_start(rows[:, u], dst_rows[:, bass.ds(g * GC, GC)].broadcast_to([P, GC])).then_inc(s_in[u], 16)
                        sp.dma_start(car[:, u], carried[bass.ds(g, 1)].rearrange("o t c -> (o t) c")).then_inc(s_in[u], 16)
                        if not first:
                            sp.wait_ge(S["hd"], freed(g))
                            sp.wait_ge(S["x1"], freed(g))
                        sp.dma_start(hd[:, u], tiles(table_h, g)).then_inc(s_sl[u], 16)
                        sp.dma_start(xd[:, u], tiles(x_dst, g)).then_inc(s_sl[u], 16)
                        if not first:
                            sp.wait_ge(S["et"], freed(g))
                            sp.wait_ge(S["w"], freed(g))
                        if isinstance(g, int) and g == NG - 1:
                            full, at = GROUP - 1, (T - 1) * P
                            for to, v in ((er, radial), (eh, edge_h)):
                                sp.dma_start(to[:, u, 0:full], v[g * GC:at, :].rearrange("(t p) d -> p t d", p=P)).then_inc(s_ed[u], 16)
                                sp.dma_start(to[0:EL, u, full], v[at:E, :]).then_inc(s_ed[u], 16)
                        else:
                            sp.dma_start(er[:, u], tiles(radial, g)).then_inc(s_ed[u], 16)
                            sp.dma_start(eh[:, u], tiles(edge_h, g)).then_inc(s_ed[u], 16)

                    def store(g, u, turn):
                        sp.wait_ge(S["x1"], done(g))
                        sp.dma_start(tiles(table_x, g), x1[:, u]).then_inc(s_st[u], 16)

                    each_group_ahead(sp, NG, fetch, store)
                    sp.wait_ge(s_st[0], 16 * (PAIRS + 1))
                    sp.wait_ge(s_st[1], 16 * PAIRS)

                @block.gpsimd
                def _(pool):
                    max_row = pool.to_reg(SLOTS + N - 1)
                    def gather(g, u, turn):
                        pool.wait_ge(S["agg"], freed(g))
                        pool.tensor_copy(idx[:, u, :], code_u[:, bass.ds(g * GROUP, GROUP)]).then_inc(s_staged, 1)
                        pool.wait_ge(s_staged, g + 1)
                        pool.sem_inc(s_pace, 1)
                        for t in range(GROUP):
                            pool.indirect_dma_start(
                                msg[:, u, t, :], None, table_h,
                                bass.IndirectOffsetOnAxis(ap=idx[:, u, t:t + 1], axis=0),
                                bounds_check=max_row, oob_is_err=False).then_inc(s_msg[u], 16)

                    each_group(pool, NG, gather)

                @block.tensor
                def _(pe):
                    def group(g, u, turn):
                        pe.wait_ge(s_ed[u], 32 * turn + (64 if isinstance(g, int) and g == NG - 1 else 32))
                        pe.wait_ge(S["etc"], done(g - 1))
                        for t in range(GROUP):
                            last = pe.transpose(etb[:, t * P:(t + 1) * P], er[:, u, t], ident[:])
                        last.then_inc(S["et"], 1)
                        pe.wait_ge(s_sl[u], 32 * (turn + 1))
                        pe.wait_ge(S["hdT"], done(g - 1))
                        for q in range(2):
                            last = pe.transpose(hdb[:, q * P:(q + 1) * P],
                                                hd[:, u, 2 * q:2 * q + 2].rearrange("p t d -> p (t d)"), ident[:])
                        last.then_inc(S["hd"], 1)
                        pe.wait_ge(S["etc"], done(g))
                        pe.wait_ge(S["w1"], done(g - 1))
                        pe.matmul(e1b[0:D, :], sW1_s[:], erT[:], start=True, stop=False)
                        pe.matmul(e1b[0:D, :], sb1_row[:], ones_row[:], start=False, stop=True).then_inc(S["e1"], 1)
                        pe.wait_ge(s_msg[u], 16 * GROUP * (turn + 1))
                        pe.wait_ge(S["seg"], done(g))
                        pe.wait_ge(S["aggs"], done(g - 1))
                        for t in range(GROUP):
                            last = pe.matmul(agg[0:D, t * P:(t + 1) * P], msg[:, u, t, :], seg[:, u, t, :],
                                             start=(t == 0), stop=False, skip_group_check=True)
                        last.then_inc(S["agg"], 1)
                        pe.wait_ge(S["scan"], done(g))
                        pe.wait_ge(S["y0"], done(g - 1))
                        pe.transpose(zb[0:GROUP, 256:256 + D + 1], carry[:, u, 0:GROUP],
                                     ident[0:D + 1, 0:D + 1]).then_inc(S["crT"], 1)
                        pe.wait_ge(S["w1"], done(g))
                        pe.wait_ge(S["w2"], done(g - 1))
                        for t in range(GROUP):
                            pe.matmul(e2b[:, t * D:(t + 1) * D], w1[:, t * P:(t + 1) * P], sW2_s[:], start=(t == 0),
                                      stop=False, skip_group_check=True)
                        pe.matmul(e2b[:, 0:GROUP * D], ones[0:1, :], sb2_rows[:], start=False, stop=True,
                                  skip_group_check=True).then_inc(S["e2"], 1)
                        pe.wait_ge(S["crow"], done(g))
                        pe.matmul(agg[0:D, :], crow[:, u, :], car[:, u, :], start=False, stop=True,
                                  skip_group_check=True).then_inc(S["carried"], 1)
                        pe.wait_ge(S["hdT"], done(g))
                        pe.wait_ge(S["aggs"], done(g))
                        for q in range(2):
                            last = pe.matmul(zb[:, q * P:(q + 1) * P], hdT[:, u, q * P:(q + 1) * P], gW2_2[:],
                                             start=(q == 0), stop=False, skip_group_check=True)
                            for t in (2 * q, 2 * q + 1):
                                last = pe.matmul(zb[:, t * D:(t + 1) * D], aggs[:, u, t * P:(t + 1) * P], gW2_s[:],
                                                 start=False, stop=(t == GROUP - 1), skip_group_check=True)
                        last.then_inc(S["z"], 1)

                    each_group(pe, NG, group)

                @block.scalar
                def _(act):
                    def group(g, u, turn):
                        act.wait_ge(S["et"], done(g))
                        act.wait_ge(S["e1"], done(g - 1))
                        act.activation(erT[:], etb[:], ACT.Copy).then_inc(S["etc"], 1)
                        act.wait_ge(S["hd"], done(g))
                        act.wait_ge(S["z"], freed(g))
                        act.activation(hdT[:, u], hdb[:, 0:2 * P], ACT.Copy).then_inc(S["hdT"], 1)
                        act.wait_ge(S["e1"], done(g))
                        act.wait_ge(S["w1"], done(g - 1))
                        act.activation(pa[:, 0], e1b[0:D, :], ACT.Abs).then_inc(S["e1a"], 1)
                        act.wait_ge(S["e1a"], done(g))
                        act.activation(pa[:, 1], pa[:, 0], ACT.Exp, scale=-1.0).then_inc(S["e1e"], 1)
                        act.wait_ge(S["e1e"], done(g))
                        act.activation(pa[:, 0], pa[:, 1], ACT.Ln, bias=half_col[0:D, :],
                                       scale=0.5).then_inc(S["e1l"], 1)
                        act.wait_ge(S["e2"], done(g))
                        act.wait_ge(S["w2"], done(g - 1))
                        act.activation(pb_[:, 0], e2b[:, 0:GROUP * D], ACT.Abs).then_inc(S["e2a"], 1)
                        act.wait_ge(S["e2a"], done(g))
                        act.activation(pb_[:, 1], pb_[:, 0], ACT.Exp, scale=-1.0).then_inc(S["e2e"], 1)
                        act.wait_ge(S["e2e"], done(g))
                        act.activation(pb_[:, 0], pb_[:, 1], ACT.Ln, bias=half_col[:], scale=0.5).then_inc(S["e2l"], 1)
                        act.wait_ge(S["carried"], done(g))
                        act.wait_ge(S["z"], freed(g))
                        act.activation(aggs[:, u], agg[0:D, :], ACT.Copy).then_inc(S["aggs"], 1)

                    each_group(act, NG, group)

                @block.vector
                def _(dve):
                    dve.memset(carry[:], 0.0).then_inc(s_link, 1)
                    dve.wait_ge(s_link, 1)

                    def group(g, u, turn):
                        cols = bass.ds(g * GROUP, GROUP)
                        dve.wait_ge(s_in[u], 32 * (turn + 1))
                        dve.wait_ge(S["agg"], freed(g))
                        dve.tensor_tensor(seg[:, u], rows[:, u].rearrange("p (t i) -> p t i", i=P),
                                          dst_kept[:, cols].unsqueeze(2).broadcast_to([P, GROUP, P]),
                                          ALU.is_equal).then_inc(S["seg"], 1)
                        dve.wait_ge(S["e1l"], done(g))
                        dve.wait_ge(S["e2"], done(g - 1))
                        dve.scalar_tensor_tensor(w1[:], e1b[0:D, :], 0.0, pa[:, 0], ALU.max,
                                                 ALU.add).then_inc(S["w1"], 1)
                        dve.wait_ge(S["agg"], done(g))
                        dve.wait_ge(S["crT"], freed(g))
                        dve.wait_ge(S["scan"], done(g - 1))
                        dve.tensor_copy(carry[:, u, 0:1], carry[:, 1 - u, GROUP:GROUP + 1])
                        dve.tensor_tensor_scan(carry[0:D, u, 1:GROUP + 1], goes_on[0:D, cols],
                                               agg[0:D].rearrange("p (t i) -> p t i", i=P)[:, :, P - 1],
                                               carry[0:D, 1 - u, GROUP:GROUP + 1], ALU.mult,
                                               ALU.add).then_inc(S["scan"], 1)
                        dve.wait_ge(S["crT"], done(g))
                        dve.wait_ge(S["carried"], freed(g))
                        dve.tensor_copy(crow[:, u], zb[0:GROUP, 256:256 + D]).then_inc(S["crow"], 1)
                        dve.wait_ge(S["e2l"], done(g))
                        dve.wait_ge(S["w"], done(g - 1))
                        dve.scalar_tensor_tensor(w2[:], e2b[:, 0:GROUP * D], 0.0, pb_[:, 0], ALU.max,
                                                 ALU.add).then_inc(S["w2"], 1)
                        dve.wait_ge(S["w2"], done(g))
                        dve.wait_ge(s_ed[u], 32 * turn + (64 if isinstance(g, int) and g == NG - 1 else 32))
                        dve.tensor_tensor(self_slot[:, cols, :], w2[:].rearrange("p (t d) -> p t d", d=D), eh[:, u],
                                          ALU.mult).then_inc(S["w"], 1)
                        dve.wait_ge(S["z"], done(g))
                        y0, y1, y2 = [y[:, n].rearrange("p (t d) -> p t d", d=D) for n in range(3)]
                        dve.tensor_tensor(y0, zb[:, 0:GROUP * D].rearrange("p (t d) -> p t d", d=D),
                                          ii_slot[:, cols].unsqueeze(2).broadcast_to([P, GROUP, D]),
                                          ALU.mult).then_inc(S["y0"], 1)
                        dve.wait_ge(S["y0"], done(g))
                        dve.tensor_tensor(y1, y0, b2_all[:].unsqueeze(1).broadcast_to([P, GROUP, D]),
                                          ALU.add).then_inc(S["y1"], 1)
                        dve.wait_ge(S["y1"], done(g))
                        dve.scalar_tensor_tensor(y2, y1, SLOPE, y1, ALU.mult, ALU.max).then_inc(S["y2"], 1)
                        dve.wait_ge(S["y2"], done(g))
                        dve.wait_ge(s_sl[u], 32 * (turn + 1))
                        dve.wait_ge(s_st[u], 16 * turn)
                        dve.tensor_tensor(x1[:, u], y2, xd[:, u], ALU.add).then_inc(S["x1"], 1)

                    each_group(dve, NG, group)

        nc.clear_and_free_semaphores(signals)
        nc.all_engine_barrier()


        signals = []
        with ExitStack() as ph:
            def sb(name, shape, dt=F32):
                return ph.enter_context(nc.sbuf_tensor(f"p5_{name}", shape, dt))

            def sem(name):
                signals.append(nc.alloc_semaphore(name))
                return signals[-1]

            agg, zb, xb, sb_, qb = [
                ph.enter_context(nc.psum_tensor(f"bank5_{n}", [P, 512], F32))
                for n in ("agg", "z", "x", "s", "q")]
            idx = sb("idx", [P, RING, GROUP], U32)
            oidx = sb("oidx", [P, RING, GROUP], U32)
            xg = sb("xg", [P, RING, GROUP, D])
            rows = sb("rows", [P, RING, GC])
            car = sb("car", [GROUP, RING, GC])
            seg = sb("seg", [P, RING, GROUP, P])
            carry = sb("carry", [D + 1, RING, GROUP + 1])
            crow = sb("crow", [GROUP, RING, D + 1])
            aggs = sb("aggs", [D + 1, RING, GC])
            xT = sb("xT", [P, 2 * P])
            sq = sb("sq", [P, GROUP * D])
            var = sb("var", [P, GROUP])
            lnv = sb("lnv", [P, GROUP])
            rs = sb("rs", [P, 4, GROUP])
            xh = sb("xh", [P, GROUP, D])
            msg = sb("msg", [P, RING, GROUP, D + 1])
            cnt = sb("cnt", [P, 2, GROUP])
            y = sb("y", [P, 2, GROUP * D])
            pa = sb("pa", [P, 2, GROUP * D])
            s1 = sb("s1", [P, GROUP * D])
            s1T = sb("s1T", [P, 2 * P])
            pc = sb("pc", [P, 2, GROUP * D])
            f = sb("f", [P, GROUP * D])
            x1 = sb("x1", [P, RING, GROUP, D])
            res = sb("res", [P, RING, GROUP, D])

            s_staged, s_ostaged = sem("s5_staged"), sem("s5_ostaged")
            s_xg = [sem(f"s5_xg{u}") for u in range(RING)]
            s_in = [sem(f"s5_in{u}") for u in range(RING)]
            s_sl = [sem(f"s5_sl{u}") for u in range(RING)]
            s_sc = [sem(f"s5_sc{u}") for u in range(RING)]
            s_link = sem("s5_link")
            S = {n: sem("s5_" + n) for n in (
                "xt", "xtc", "cen", "sq", "var", "lnv", "r0", "r1", "r2", "rs", "xh", "msg",
                "seg", "agg", "scan", "crT", "crow", "carried", "aggs", "z", "cnt", "rc", "y0", "y1",
                "ya", "ye", "yl", "s1", "st", "stc", "q", "qa", "qe", "ql", "f", "res")}

            s_pace = sem("s5_pace")
            with nc.Block() as block:
                @block.sync
                def _(sp):
                    for s in S.values():
                        sp.sem_inc(s, RING)

                    def fetch(g, u, turn):
                        sp.wait_ge(S["carried"], freed(g))
                        sp.wait_ge(S["seg"], freed(g))
                        sp.dma_start(rows[:, u], dst_rows[:, bass.ds(g * GC, GC)].broadcast_to([P, GC])).then_inc(s_in[u], 16)
                        sp.dma_start(car[:, u], carried[bass.ds(g, 1)].rearrange("o t c -> (o t) c")).then_inc(s_in[u], 16)
                        sp.wait_ge(S["res"], freed(g))
                        sp.dma_start(x1[:, u], tiles(table_x, g)).then_inc(s_sl[u], 16)

                    each_group(sp, NG, fetch)
                    sp.wait_ge(s_sc[0], 16 * GROUP * (PAIRS + 1))
                    sp.wait_ge(s_sc[1], 16 * GROUP * PAIRS)

                @block.gpsimd
                def _(pool):
                    max_node = pool.to_reg(N - 1)
                    max_row = pool.to_reg(SLOTS + N - 1)
                    def gather(g, u):
                        if not (isinstance(g, int) and g < RING):
                            pool.wait_ge(S["xt"], freed(g))
                        pool.tensor_copy(idx[:, u, :], code_u[:, bass.ds(g * GROUP, GROUP)]).then_inc(s_staged, 1)
                        pool.wait_ge(s_staged, g + 1)
                        pool.sem_inc(s_pace, 1)
                        for t in range(GROUP):
                            pool.indirect_dma_start(
                                xg[:, u, t, :], None, table_x,
                                bass.IndirectOffsetOnAxis(ap=idx[:, u, t:t + 1], axis=0),
                                bounds_check=max_row, oob_is_err=False).then_inc(s_xg[u], 16)

                    def scatter(g, u, turn):
                        pool.wait_ge(s_sc[u], 16 * GROUP * turn)
                        pool.tensor_copy(oidx[:, u, :], out_u[:, bass.ds(g * GROUP, GROUP)]).then_inc(s_ostaged, 1)
                        pool.wait_ge(s_ostaged, g + 1)
                        pool.wait_ge(S["res"], done(g))
                        pool.sem_inc(s_pace, 1)
                        for t in range(GROUP):
                            pool.indirect_dma_start(
                                out, bass.IndirectOffsetOnAxis(ap=oidx[:, u, t:t + 1], axis=0),
                                res[:, u, t, :], None,
                                bounds_check=max_node, oob_is_err=False).then_inc(s_sc[u], 16)

                    each_group_ahead(pool, NG, gather, scatter)

                @block.tensor
                def _(pe):
                    def normed(g, u, turn):
                        pe.wait_ge(s_xg[u], 16 * GROUP * (turn + 1))
                        pe.wait_ge(S["xh"], done(g - 1))
                        for q in range(2):
                            last = pe.transpose(xb[:, q * P:(q + 1) * P],
                                                xg[:, u, 2 * q:2 * q + 2, :].rearrange("p t d -> p (t d)"), ident[:])
                        last.then_inc(S["xt"], 1)
                        pe.wait_ge(S["xtc"], done(g))
                        for q in range(2):
                            last = pe.matmul(xb[:, (2 + q) * P:(3 + q) * P], xT[:, q * P:(q + 1) * P], center2[:],
                                             start=True, stop=True)
                        last.then_inc(S["cen"], 1)
                        pe.wait_ge(S["msg"], done(g))
                        pe.wait_ge(S["seg"], done(g))
                        pe.wait_ge(S["aggs"], done(g - 1))
                        for t in range(GROUP):
                            last = pe.matmul(agg[0:D + 1, t * P:(t + 1) * P], msg[:, u, t, :], seg[:, u, t, :],
                                             start=(t == 0), stop=False, skip_group_check=True)
                        last.then_inc(S["agg"], 1)

                    def layer(g, u, turn):
                        pe.wait_ge(S["scan"], done(g))
                        pe.wait_ge(S["y0"], done(g - 1))
                        pe.wait_ge(S["cnt"], done(g - 1))
                        pe.transpose(zb[0:GROUP, 320:320 + D + 1], carry[:, u, 0:GROUP],
                                     ident[0:D + 1, 0:D + 1]).then_inc(S["crT"], 1)
                        pe.wait_ge(S["crow"], done(g))
                        pe.matmul(agg[0:D + 1, :], crow[:, u, :], car[:, u, :], start=False, stop=True,
                                  skip_group_check=True).then_inc(S["carried"], 1)
                        pe.wait_ge(S["aggs"], done(g))
                        for t in range(GROUP):
                            last = pe.matmul(zb[:, t * (D + 1):(t + 1) * (D + 1)], aggs[:, u, t * P:(t + 1) * P],
                                             sW3_a[:], start=True, stop=True)
                        last.then_inc(S["z"], 1)
                        pe.wait_ge(S["s1"], done(g))
                        pe.wait_ge(S["stc"], done(g - 1))
                        for q in range(2):
                            last = pe.transpose(sb_[:, q * P:(q + 1) * P], s1[:, q * P:(q + 1) * P], ident[:])
                        last.then_inc(S["st"], 1)
                        pe.wait_ge(S["stc"], done(g))
                        pe.wait_ge(S["f"], done(g - 1))
                        for q in range(2):
                            pe.matmul(qb[:, q * P:(q + 1) * P], s1T[:, q * P:(q + 1) * P], sW4_2[:], start=(q == 0),
                                      stop=False, skip_group_check=True)
                        pe.matmul(qb[:, 0:2 * P], ones[0:1, :], sb4_rows[:], start=False, stop=True,
                                  skip_group_check=True).then_inc(S["q"], 1)

                    def group(g, u, turn):
                        normed(g, u, turn)
                        layer(g, u, turn)

                    each_group(pe, NG, group)

                @block.scalar
                def _(act):
                    def group(g, u, turn):
                        act.wait_ge(S["xt"], done(g))
                        act.wait_ge(S["cen"], done(g - 1))
                        act.activation(xT[:], xb[:, 0:2 * P], ACT.Copy).then_inc(S["xtc"], 1)
                        act.wait_ge(S["cen"], done(g))
                        act.wait_ge(S["var"], done(g - 1))
                        act.activation(sq[:], xb[:, 2 * P:4 * P], ACT.Square, scale=0.125).then_inc(S["sq"], 1)
                        act.wait_ge(S["var"], done(g))
                        act.activation(lnv[:], var[:], ACT.Ln, bias=eps_col[:]).then_inc(S["lnv"], 1)
                        act.wait_ge(S["lnv"], done(g))
                        act.wait_ge(S["rs"], done(g - 1))
                        act.activation(rs[:, 0], lnv[:], ACT.Exp, scale=-0.5).then_inc(S["r0"], 1)
                        act.wait_ge(S["carried"], done(g))
                        act.wait_ge(S["z"], freed(g))
                        act.activation(aggs[:, u], agg[0:D + 1, :], ACT.Copy).then_inc(S["aggs"], 1)
                        act.wait_ge(S["y1"], done(g))
                        act.wait_ge(S["s1"], done(g - 1))
                        act.activation(pa[:, 0], y[:, 1], ACT.Abs).then_inc(S["ya"], 1)
                        act.wait_ge(S["ya"], done(g))
                        act.activation(pa[:, 1], pa[:, 0], ACT.Exp, scale=-1.0).then_inc(S["ye"], 1)
                        act.wait_ge(S["ye"], done(g))
                        act.activation(pa[:, 0], pa[:, 1], ACT.Ln, bias=half_col[:], scale=0.5).then_inc(S["yl"], 1)
                        act.wait_ge(S["st"], done(g))
                        act.wait_ge(S["q"], done(g - 1))
                        act.activation(s1T[:], sb_[:, 0:2 * P], ACT.Copy).then_inc(S["stc"], 1)
                        act.wait_ge(S["q"], done(g))
                        act.wait_ge(S["f"], done(g - 1))
                        act.activation(pc[:, 0], qb[:, 0:2 * P], ACT.Abs).then_inc(S["qa"], 1)
                        act.wait_ge(S["qa"], done(g))
                        act.activation(pc[:, 1], pc[:, 0], ACT.Exp, scale=-1.0).then_inc(S["qe"], 1)
                        act.wait_ge(S["qe"], done(g))
                        act.activation(pc[:, 0], pc[:, 1], ACT.Ln, bias=half_col[:], scale=0.5).then_inc(S["ql"], 1)

                    each_group(act, NG, group)

                @block.vector
                def _(dve):
                    dve.memset(msg[:], 1.0)
                    dve.memset(carry[:], 0.0).then_inc(s_link, 1)
                    dve.wait_ge(s_link, 1)

                    def group(g, u, turn):
                        cols = bass.ds(g * GROUP, GROUP)
                        dve.wait_ge(s_in[u], 32 * (turn + 1))
                        dve.wait_ge(S["agg"], freed(g))
                        dve.tensor_tensor(seg[:, u], rows[:, u].rearrange("p (t i) -> p t i", i=P),
                                          dst_f[:, cols].unsqueeze(2).broadcast_to([P, GROUP, P]),
                                          ALU.is_equal).then_inc(S["seg"], 1)
                        dve.wait_ge(S["sq"], done(g))
                        dve.wait_ge(S["rs"], done(g - 1))
                        dve.tensor_reduce(var[:], sq[:].rearrange("p (t d) -> p t d", d=D), AX_X,
                                          ALU.add).then_inc(S["var"], 1)
                        dve.wait_ge(S["r0"], done(g))
                        dve.scalar_tensor_tensor(rs[:, 1], var[:], EPS, rs[:, 0], ALU.add, ALU.mult).then_inc(S["r1"], 1)
                        dve.wait_ge(S["r1"], done(g))
                        dve.scalar_tensor_tensor(rs[:, 2], rs[:, 1], -0.5, rs[:, 0], ALU.mult,
                                                 ALU.mult).then_inc(S["r2"], 1)
                        dve.wait_ge(S["r2"], done(g))
                        dve.wait_ge(S["xh"], done(g - 1))
                        dve.scalar_tensor_tensor(rs[:, 3], rs[:, 2], 1.5, rs[:, 0], ALU.add, ALU.mult).then_inc(S["rs"], 1)
                        dve.wait_ge(S["rs"], done(g))
                        dve.wait_ge(S["msg"], done(g - 1))
                        dve.scalar_tensor_tensor(xh[:], xb[:, 2 * P:4 * P].rearrange("p (t d) -> p t d", d=D), 0.0,
                                                 rs[:, 3].unsqueeze(2).broadcast_to([P, GROUP, D]), ALU.max,
                                                 ALU.mult).then_inc(S["xh"], 1)
                        dve.wait_ge(S["xh"], done(g))
                        dve.tensor_tensor(msg[:, u, :, 0:D], xh[:], self_slot[:, cols, :], ALU.mult).then_inc(S["msg"], 1)
                        dve.wait_ge(S["agg"], done(g))
                        dve.wait_ge(S["crT"], freed(g))
                        dve.wait_ge(S["scan"], done(g - 1))
                        dve.tensor_copy(carry[:, u, 0:1], carry[:, 1 - u, GROUP:GROUP + 1])
                        dve.tensor_tensor_scan(carry[:, u, 1:GROUP + 1], goes_on[0:D + 1, cols],
                                               agg[0:D + 1].rearrange("p (t i) -> p t i", i=P)[:, :, P - 1],
                                               carry[:, 1 - u, GROUP:GROUP + 1], ALU.mult,
                                               ALU.add).then_inc(S["scan"], 1)
                        dve.wait_ge(S["crT"], done(g))
                        dve.wait_ge(S["carried"], freed(g))
                        dve.tensor_copy(crow[:, u], zb[0:GROUP, 320:320 + D + 1]).then_inc(S["crow"], 1)
                        dve.wait_ge(S["z"], done(g))
                        zv = zb[:, 0:GROUP * (D + 1)].rearrange("p (t d) -> p t d", d=D + 1)
                        y0, y1 = [y[:, n].rearrange("p (t d) -> p t d", d=D) for n in range(2)]
                        dve.tensor_scalar(cnt[:, 0], zv[:, :, D], 1.0, None, ALU.max).then_inc(S["cnt"], 1)
                        dve.wait_ge(S["cnt"], done(g))
                        dve.reciprocal(cnt[:, 1], cnt[:, 0]).then_inc(S["rc"], 1)
                        dve.wait_ge(S["rc"], done(g))
                        dve.tensor_tensor(y0, zv[:, :, 0:D], cnt[:, 1].unsqueeze(2).broadcast_to([P, GROUP, D]),
                                          ALU.mult).then_inc(S["y0"], 1)
                        dve.wait_ge(S["y0"], done(g))
                        dve.tensor_tensor(y1, y0, sb3_all[:].unsqueeze(1).broadcast_to([P, GROUP, D]),
                                          ALU.add).then_inc(S["y1"], 1)
                        dve.wait_ge(S["yl"], done(g))
                        dve.wait_ge(S["st"], done(g - 1))
                        dve.scalar_tensor_tensor(s1[:], y[:, 1], 0.0, pa[:, 0], ALU.max, ALU.add).then_inc(S["s1"], 1)
                        dve.wait_ge(S["ql"], done(g))
                        dve.scalar_tensor_tensor(f[:], qb[:, 0:2 * P], 0.0, pc[:, 0], ALU.max, ALU.add).then_inc(S["f"], 1)
                        dve.wait_ge(S["f"], done(g))
                        dve.wait_ge(s_sl[u], 16 * (turn + 1))
                        dve.wait_ge(s_sc[u], 16 * GROUP * turn)
                        dve.tensor_tensor(res[:, u], f[:].rearrange("p (t d) -> p t d", d=D), x1[:, u],
                                          ALU.add).then_inc(S["res"], 1)

                    each_group(dve, NG, group)


_INS = ['x', 'src', 'dst', 'edge_attr_128', 'edge_attr_64', 'L0_gnn_W1', 'L0_gnn_b1', 'L0_gnn_W2', 'L0_gnn_b2',
        'L1_gnn_W1', 'L1_gnn_b1', 'L1_gnn_W2', 'L1_gnn_b2', 'L1_gnn_W3', 'L1_gnn_b3', 'L1_gnn_W4', 'L1_gnn_b4']
_OUTS = [((100000, 64), 'float32')]


def kernel(**inputs):
    import numpy as _np
    import concourse.bacc as _bacc
    from concourse import mybir as _mybir
    from concourse.bass_utils import run_bass_kernel_spmd as _run

    nc = _bacc.Bacc("TRN2", target_bir_lowering=False, num_devices=1)
    arrays, args = {}, []
    for name in _INS:
        a = _np.ascontiguousarray(inputs[name])
        arrays[f"in_{name}_dram"] = a
        args.append(nc.dram_tensor(f"in_{name}_dram", a.shape, _mybir.dt.from_np(a.dtype), kind="ExternalInput").ap())
    for i, (shape, dtype) in enumerate(_OUTS):
        dt = _mybir.dt.from_np(_np.dtype(dtype))
        args.append(nc.dram_tensor(f"out_{i}_dram", shape, dt, kind="ExternalOutput").ap())
    gnn_kernel(nc, *args)
    r = _run(nc, [arrays], core_ids=[0])
    got = tuple(r.results[0][f"out_{i}_dram"] for i in range(len(_OUTS)))
    return got[0]
```

```python
import concourse.bass as bass
from concourse import mybir
from contextlib import ExitStack

ALU = mybir.AluOpType
ACT = mybir.ActivationFunctionType
AX_X = mybir.AxisListType.X
F32 = mybir.dt.float32
F16 = mybir.dt.float16
BF16 = mybir.dt.bfloat16
I32 = mybir.dt.int32
U32 = mybir.dt.uint32

P = 128
J = 8
BLOCK = P * J
GROUP = 4
SKIP = 131071
AROW = 66
RING = 2
EPS = 1e-5
SLOPE = 0.01


def done(g):
    return g + 1 + RING


def freed(g):
    return g + 1


def early(g):
    return isinstance(g, int) and g < RING


def each_group(eng, count, body, peel=0):
    for g in range(2 * peel):
        body(g, g % 2, g // 2)
    with eng.Fori(peel, count // 2) as i:
        body(2 * i, 0, i)
        body(2 * i + 1, 1, i)
    body(count - 1, 0, count // 2)


def each_group_lead(eng, count, first, then, peel=0):
    def two(i):
        first(2 * i + 1, 1, i)
        then(2 * i, 0, i)
        first(2 * i + 2, 0, i + 1)
        then(2 * i + 1, 1, i)

    first(0, 0, 0)
    for i in range(peel):
        two(i)
    with eng.Fori(peel, count // 2) as i:
        two(i)
    then(count - 1, 0, count // 2)


def each_group_ahead(eng, count, fetch, body, peel=0):
    def two(i):
        for u in range(2):
            fetch(2 * i + u + 2, u)
            body(2 * i + u, u, i)

    fetch(0, 0)
    fetch(1, 1)
    for i in range(peel):
        two(i)
    with eng.Fori(peel, count // 2 - 1) as i:
        two(i)
    fetch(count - 1, 0)
    for g in range(count - 3, count):
        body(g, g % 2, g // 2)


def each_group_staged(eng, count, *stages):
    most = max(lag for lag, _ in stages)
    first = -(-(most + RING) // 2) * 2
    last = count // 2 * 2

    def peeled(i):
        for lag, step in stages:
            g = i - lag
            if 0 <= g < count:
                step(g, g % 2, g // 2)

    for i in range(first):
        peeled(i)
    with eng.Fori(first // 2, last // 2) as r:
        for s in range(2):
            for lag, step in stages:
                k = s - lag
                step(2 * r + k, k % 2, r + k // 2)
    for i in range(last, count + most):
        peeled(i)


def gnn_kernel(nc, x, src, dst, radial, edge_h, gW1, gb1, gW2, gb2,
               sW1, sb1, sW2, sb2, sW3, sb3, sW4, sb4, out):
    N, D = x.shape
    E = src.shape[0]
    R = radial.shape[1]
    T = -(-E // P)
    SLOTS = T * P
    EL = E - (T - 1) * P
    NG = T // GROUP
    NBLK = -(-N // BLOCK)
    PL = (N - (NBLK - 1) * BLOCK) // J
    NC = NBLK * J
    HC = NC // 2
    assert T == NG * GROUP and NBLK == 2 * NG and NG % 2 == 1 and D == 64 and R == P
    assert (N - (NBLK - 1) * BLOCK) % J == 0 and HC <= 512 and N < SKIP
    PAIRS = NG // 2
    GC = GROUP * P
    TL = T - P

    B3 = 65
    EP, EC = 125, E // 125
    PIECE = 25
    assert E == EP * EC and EC % PIECE == 0

    src_sorted = nc.dram_tensor("src_sorted", [E, 1], I32, kind="Internal").ap()
    dst_sorted = nc.dram_tensor("dst_sorted", [E, 1], I32, kind="Internal").ap()
    rank_d = nc.dram_tensor("rank_d", [EP, EC], U32, kind="Internal").ap()
    w_given = nc.dram_tensor("w_given", [SLOTS, D], F32, kind="Internal").ap()
    w_sorted = nc.dram_tensor("w_sorted", [SLOTS, D], F32, kind="Internal").ap()
    dst_rows = nc.dram_tensor("dst_rows", [1, SLOTS + P], F32, kind="Internal").ap()
    table_a = nc.dram_tensor("table_a", [N, AROW], F32, kind="Internal").ap()
    x_dst = nc.dram_tensor("x_dst", [SLOTS, D], F32, kind="Internal").ap()
    carried = nc.dram_tensor("carried", [NG, GROUP, GC], F32, kind="Internal").ap()
    carried_rows = nc.dram_tensor("carried_rows", [NG, GROUP, P], F32, kind="Internal").ap()
    table_h = nc.dram_tensor("table_h", [SLOTS + NBLK * BLOCK, D], F32, kind="Internal").ap()
    table_x = nc.dram_tensor("table_x", [SLOTS + NBLK * BLOCK, D], F32, kind="Internal").ap()

    local_h, local_x = table_h[SLOTS:, :], table_x[SLOTS:, :]

    def both(t, g):
        return t[bass.ds(g * 2 * BLOCK, 2 * BLOCK), :].rearrange("(k p j) d -> p k (j d)", p=P, j=J)

    def tiles(t, g):
        return t[bass.ds(g * GC, GC), :].rearrange("(t p) d -> p t d", p=P)

    def blocks(t, b, rows=P):
        return t[bass.ds(b * BLOCK, rows * J), :].rearrange("(p j) d -> p (j d)", j=J)

    with ExitStack() as ctx:
        def sb(name, shape, dt=F32):
            return ctx.enter_context(nc.sbuf_tensor(name, shape, dt))

        def sem(name):
            return ctx.enter_context(nc.semaphore(name))

        ident = sb("ident", [P, P])
        ones = sb("ones", [P, P])
        center2 = sb("center2", [P, P])
        gW1_2 = sb("gW1_2", [P, P])
        gW2_2 = sb("gW2_2", [P, P])
        sW4_2 = sb("sW4_2", [P, P])
        gW1_a = sb("gW1_a", [D + 1, D + 1])
        sW3_a = sb("sW3_a", [D + 1, D + 1])
        gW2_s = sb("gW2_s", [D, D])
        sW1_s = sb("sW1_s", [P, D])
        sW2_s = sb("sW2_s", [D, D])
        b1_rows = sb("b1_rows", [1, J * D])
        b2_rows = sb("b2_rows", [1, J * D])
        sb2_rows = sb("sb2_rows", [1, GROUP * D])
        sb4_rows = sb("sb4_rows", [1, GROUP * D])
        b1_all = sb("b1_all", [P, D])
        b2_all = sb("b2_all", [P, D])
        sb3_all = sb("sb3_all", [P, D])
        sb1_row = sb("sb1_row", [1, D])
        b1_3 = sb("b1_3", [B3, J * D], BF16)
        b2_3 = sb("b2_3", [B3, J * D], BF16)
        sb1_3 = sb("sb1_3", [B3, D], BF16)
        sb2_3 = sb("sb2_3", [B3, GROUP * D], BF16)
        sb4_3 = sb("sb4_3", [B3, GROUP * D], BF16)
        ones_3 = sb("ones_3", [B3, GROUP * P], BF16)
        sb3_col = sb("sb3_col", [D, 1])
        rest_row = sb("rest_row", [P, D])
        eps_col = sb("eps_col", [P, 1])
        iota_lo = sb("iota_lo", [P, P], F16)
        zeros = sb("zeros", [P, HC], F16)
        half_col = sb("half_col", [P, 1])
        code_u = sb("code_u", [P, T], U32)
        io_slot = sb("io_slot", [P, T])
        ii_slot = sb("ii_slot", [P, T])
        dst_f = sb("dst_f", [P, T])
        src_u = sb("src_u", [P, T], U32)
        dst_u = sb("dst_u", [P, T], U32)
        out_u = sb("out_u", [P, T], U32)
        keep = sb("keep", [P, T])
        goes_on = sb("goes_on", [P, T])
        dst_kept = sb("dst_kept", [P, T])
        out_scale = sb("out_scale", [P, NC])
        code = sb("code", [P, NC])

        unsorted = sb("unsorted", [1, 1], I32)

        s_const = sem("s_const")
        s_w = sem("s_w")

        signals = []
        with ExitStack() as ph:
            def sb(name, shape, dt=F32):
                return ph.enter_context(nc.sbuf_tensor(f"p0_{name}", shape, dt))

            def sem(name):
                signals.append(nc.alloc_semaphore(name))
                return signals[-1]

            bank0 = ph.enter_context(nc.psum_tensor("bank0_count", [P, 512], F32))
            given = sb("given", [EP, 2, EC], I32)
            first_next = sb("first_next", [EP, 1], I32)
            dst_e = sb("dst_e", [EP, EC + 1])
            falls = sb("falls", [EP, EC])
            fall = sb("fall", [EP, 1])
            one = sb("one", [EP, 1])
            col = sb("col", [EP, EC])
            later = sb("later", [EP, EP])
            row_i = sb("row_i", [EP, EC], I32)
            row = sb("row", [EP, EC])
            dst_up = sb("dst_up", [EP, EC])
            less = sb("less", [EP, PIECE, EC], F16)
            add = sb("add", [EP, EC])
            before = sb("before", [EP, EC])
            same = sb("same", [EP, EC])
            rank = sb("rank", [EP, EC])
            rank_u = sb("rank_u", [EP, EC], U32)
            idx = sb("idx", [EP, 1], U32)
            pay = sb("pay", [EP, 2], I32)

            s_given, s_next, s_copied, s_count, s_flag = (
                sem("s0_given"), sem("s0_next"), sem("s0_copied"), sem("s0_count"), sem("s0_flag"))
            s_v, s_aid, s_row, s_row_used, s_ranked, s_rank_st = (
                sem("s0_v"), sem("s0_aid"), sem("s0_row"), sem("s0_row_used"), sem("s0_ranked"), sem("s0_rank_st"))
            s_rv, s_tie, s_staged, s_pace, s_sc = (
                sem("s0_rv"), sem("s0_tie"), sem("s0_staged"), sem("s0_pace"), sem("s0_sc"))

            with nc.Block() as block:
                @block.sync
                def _(sp):
                    sp.dma_start(given[:, 1], dst.rearrange("(p c) -> p c", c=EC)).then_inc(s_given, 16)
                    sp.wait_ge(s_v, 1)
                    sp.dma_start(first_next[0:EP - 1, :], dst.rearrange("(p c) -> p c", c=EC)[1:EP, 0:1],
                                 allow_slow_non_contiguous=True).then_inc(s_next, 16)
                    sp.dma_start(src_sorted.rearrange("(p c) o -> p (c o)", c=EC),
                                 src.rearrange("(p c) -> p c", c=EC)).then_inc(s_copied, 16)
                    sp.dma_start(dst_sorted.rearrange("(p c) o -> p (c o)", c=EC),
                                 dst.rearrange("(p c) -> p c", c=EC)).then_inc(s_copied, 16)
                    sp.wait_ge(s_copied, 32)
                    sp.wait_ge(s_flag, 1)
                    with sp.If(sp.value_load(unsorted[:]) > 0):
                        sp.dma_start(given[:, 0], src.rearrange("(p c) -> p c", c=EC)).then_inc(s_given, 16)

                        def load_row(c):
                            sp.dma_start(row_i[:], dst.rearrange("(p c) -> p c", c=EC)[bass.ds(c, 1), :].broadcast_to(
                                [EP, EC])).then_inc(s_row, 16)

                        load_row(0)
                        with sp.Fori(1, EP) as c:
                            sp.wait_ge(s_row_used, c)
                            load_row(c)
                        sp.wait_ge(s_ranked, 1)
                        sp.dma_start(rank_d, rank_u[:]).then_inc(s_rank_st, 16)
                        sp.wait_ge(s_rank_st, 16)
                        sp.wait_ge(s_sc, 32 * EC)

                @block.gpsimd
                def _(pool):
                    pool.wait_ge(s_flag, 1)
                    with pool.If(pool.value_load(unsorted[:]) > 0):
                        max_edge = pool.to_reg(E - 1)
                        pool.iota(col[:], pattern=[[1, EC]], base=0, channel_multiplier=0,
                                  allow_small_or_imprecise_dtypes=True).then_inc(s_aid, 1)
                        pool.memset(later[:], 0.5).then_inc(s_aid, 1)
                        pool.wait_ge(s_aid, 2)
                        pool.affine_select(later[:], later[:], pattern=[[-1, EP]], compare_op=ALU.is_gt, fill=0.0,
                                           base=0, channel_multiplier=1).then_inc(s_aid, 1)
                        pool.wait_ge(s_given, 32)
                        pool.wait_ge(s_copied, 32)
                        pool.wait_ge(s_ranked, 1)
                        with pool.Fori(0, EC) as t:
                            pool.tensor_copy(idx[:], rank_u[:, bass.ds(t, 1)]).then_inc(s_staged, 1)
                            pool.tensor_copy(pay[:, 0:1], given[:, 0, bass.ds(t, 1)]).then_inc(s_staged, 1)
                            pool.tensor_copy(pay[:, 1:2], given[:, 1, bass.ds(t, 1)]).then_inc(s_staged, 1)
                            pool.wait_ge(s_staged, 3 * t + 3)
                            pool.sem_inc(s_pace, 1)
                            for a, to in enumerate((src_sorted, dst_sorted)):
                                pool.indirect_dma_start(
                                    to, bass.IndirectOffsetOnAxis(ap=idx[:], axis=0), pay[:, a:a + 1], None,
                                    bounds_check=max_edge, oob_is_err=False).then_inc(s_sc, 16)
                            pool.wait_ge(s_sc, 32 * t + 32)

                @block.tensor
                def _(pe):
                    pe.wait_ge(s_count, 1)
                    pe.matmul(bank0[0:1, 0:1], fall[:], one[:], start=True, stop=True).then_inc(s_count, 1)

                @block.vector
                def _(dve):
                    dve.memset(first_next[:], N).then_inc(s_v, 1)
                    dve.memset(one[:], 1.0)
                    dve.wait_ge(s_given, 16)
                    dve.tensor_copy(dst_e[:, 0:EC], given[:, 1])
                    dve.wait_ge(s_next, 16)
                    dve.tensor_copy(dst_e[:, EC:EC + 1], first_next[:]).then_inc(s_v, 1)
                    dve.wait_ge(s_v, 2)
                    dve.tensor_tensor(falls[:], dst_e[:, 1:EC + 1], dst_e[:, 0:EC], ALU.is_lt).then_inc(s_v, 1)
                    dve.wait_ge(s_v, 3)
                    dve.tensor_reduce(fall[:], falls[:], AX_X, ALU.add).then_inc(s_count, 1)
                    dve.wait_ge(s_count, 2)
                    dve.tensor_copy(unsorted[:], bank0[0:1, 0:1]).then_inc(s_flag, 1)
                    dve.wait_ge(s_flag, 1)
                    with dve.If(dve.value_load(unsorted[:]) > 0):
                        dve.wait_ge(s_aid, 3)
                        with dve.Fori(0, EC) as t:
                            dve.tensor_scalar(before[:], col[:], col[:, bass.ds(t, 1)], None,
                                              ALU.is_lt).then_inc(s_tie, 1)
                            dve.wait_ge(s_tie, 3 * t + 1)
                            dve.scalar_tensor_tensor(same[:], dst_e[:, 0:EC], dst_e[:, bass.ds(t, 1)], before[:],
                                                     ALU.is_equal, ALU.mult).then_inc(s_tie, 1)
                            dve.wait_ge(s_tie, 3 * t + 2)
                            dve.tensor_reduce(rank[:, bass.ds(t, 1)], same[:], AX_X, ALU.add).then_inc(s_tie, 1)
                            dve.wait_ge(s_tie, 3 * t + 3)
                        steps = 2 * (EC // PIECE) + 2
                        with dve.Fori(0, EP) as c:
                            dve.wait_ge(s_row, 16 * c + 16)
                            dve.tensor_copy(row[:], row_i[:]).then_inc(s_row_used, 1)
                            dve.wait_ge(s_row_used, c + 1)
                            dve.tensor_scalar(dst_up[:], dst_e[:, 0:EC], later[:, bass.ds(c, 1)], None,
                                              ALU.add).then_inc(s_rv, 1)
                            dve.wait_ge(s_rv, steps * c + 1)
                            for k in range(EC // PIECE):
                                cols = slice(k * PIECE, (k + 1) * PIECE)
                                dve.tensor_tensor(less[:], row[:].unsqueeze(1).broadcast_to([EP, PIECE, EC]),
                                                  dst_up[:, cols].unsqueeze(2).broadcast_to([EP, PIECE, EC]),
                                                  ALU.is_lt).then_inc(s_rv, 1)
                                dve.wait_ge(s_rv, steps * c + 2 + 2 * k)
                                dve.tensor_reduce(add[:, cols], less[:], AX_X, ALU.add).then_inc(s_rv, 1)
                                dve.wait_ge(s_rv, steps * c + 3 + 2 * k)
                            dve.tensor_tensor(rank[:], rank[:], add[:], ALU.add).then_inc(s_rv, 1)
                            dve.wait_ge(s_rv, steps * c + steps)
                        dve.tensor_copy(rank_u[:], rank[:]).then_inc(s_ranked, 1)

        nc.clear_and_free_semaphores(signals)
        nc.all_engine_barrier()


        signals = []
        with ExitStack() as ph:
            def sb(name, shape, dt=F32):
                return ph.enter_context(nc.sbuf_tensor(f"p1_{name}", shape, dt))

            def sem(name):
                signals.append(nc.alloc_semaphore(name))
                return signals[-1]

            s_padded, s_raw, s_rowf, s_rows, s_next = (
                sem("s_padded"), sem("s_raw"), sem("s_rowf"), sem("s_rows"), sem("s_next"))
            s_turned, s_slots, s_last, s_idx, s_chain, s_chain2 = (
                sem("s_turned"), sem("s_slots"), sem("s_last"), sem("s_idx"), sem("s_chain"), sem("s_chain2"))
            s_hot, s_hist, s_hist_end = sem("s_hot"), sem("s_hist"), sem("s_hist_end")
            s_pp, s_pre, s_root, s_extra = sem("s_pp"), sem("s_pre"), sem("s_root"), sem("s_extra")
            s_staged = sem("s_staged")
            s_prev, s_carr, s_carz, s_carw, s_carc = (
                sem("s_prev"), sem("s_carr"), sem("s_carz"), sem("s_carw"), sem("s_carc"))
            s_rest_a, s_rest_v, s_rest_p = sem("s_rest_a"), sem("s_rest_v"), sem("s_rest_p")
            s_xg = [sem(f"s_xg{u}") for u in range(RING)]
            s_xs = [sem(f"s_xs{u}") for u in range(RING)]
            s_x = [sem(f"s_x{u}") for u in range(RING)]
            s_a = [sem(f"s_a{u}") for u in range(RING)]
            s_xt, s_xtc, s_cen, s_sq = sem("s_xt"), sem("s_xtc"), sem("s_cen"), sem("s_sq")
            s_var, s_sd, s_rs, s_rsio, s_hs = sem("s_var"), sem("s_sd"), sem("s_rs"), sem("s_rsio"), sem("s_hs")

            iota_hi = sb("iota_hi", [P, NC], F16)
            before = sb("before", [P, P])
            last_row = sb("last_row", [P, P])
            src_f = sb("src_f", [P, T])
            next_f = sb("next_f", [P, T])
            part_r = sb("part_r", [1, J * D])
            part_s = sb("part_s", [1, J * D])
            part_b = sb("part_b", [1, J * D], BF16)
            src_lo = sb("src_lo", [P, T])
            src_hi = sb("src_hi", [P, T])
            dst_lo = sb("dst_lo", [P, T])
            dst_hi = sb("dst_hi", [P, T])
            dst_last = sb("dst_last", [P, T + 1])
            prev_col = sb("prev_col", [P, 2])
            carr = sb("carr", [P, 2, P])
            rest = sb("rest", [P, 4, D])
            rest_lhs = sb("rest_lhs", [D, P])
            raw = sb("raw", [P, 2, 2, P], I32)
            rowf = sb("rowf", [P, 2, 2, P])
            rown = sb("rown", [P, 2, P])
            bits = sb("bits", [P, 2, T], I32)
            bits_lo = sb("bits_lo", [P, 2, T], I32)
            bits_hi = sb("bits_hi", [P, 2, T], I32)
            bits_j = sb("bits_j", [P, 2, T], I32)
            hot_lo = sb("hot_lo", [P, GROUP, 2, P], F16)
            hot_hi = sb("hot_hi", [P, GROUP, 2, NC], F16)
            idx = sb("idx", [P, RING, GROUP], U32)
            xg = sb("xg", [P, RING, GROUP, D])
            in_cnt = sb("in_cnt", [P, NC])
            ends = sb("ends", [P, NC])
            nodes = sb("nodes", [P, NC])
            per_p = sb("per_p", [P, NBLK])
            base = sb("base", [P, NBLK])
            upto = sb("upto", [P, NBLK + 1])
            xin = sb("xin", [P, RING, 2, J, D])
            xT = sb("xT", [P, RING, 2, 4 * P])
            sq = sb("sq", [P, RING, 2, J * D])
            var = sb("var", [P, RING, 2 * J])
            sd = sb("sd", [P, RING, 2 * J])
            rs = sb("rs", [P, RING, 2 * J])
            rsio = sb("rsio", [P, RING, 2 * J])
            arow = sb("arow", [P, RING, 2, J, AROW])
            bank = [ph.enter_context(nc.psum_tensor(f"bank1_{k}", [P, 512], F32)) for k in range(8)]

            s_pace = sem("s_pace")
            with nc.Block() as block:
                @block.sync
                def _(sp):
                    for s in (s_xt, s_xtc, s_cen, s_sq, s_var, s_sd, s_rs, s_rsio, s_hs):
                        sp.sem_inc(s, RING)
                    for u in range(RING):
                        sp.sem_inc(s_a[u], 32)
                    sp.sem_inc(s_hist, GROUP)
                    sp.wait_ge(s_padded, 1)
                    for a, v in enumerate((src_sorted[:, 0], dst_sorted[:, 0])):
                        sp.dma_start(raw[:, a, 0, :], v[0:P * P].rearrange("(t p) -> t p", p=P)).then_inc(s_raw, 16)
                        sp.dma_start(raw[0:TL - 1, a, 1, :],
                                     v[P * P:(T - 1) * P].rearrange("(t p) -> t p", p=P)).then_inc(s_raw, 16)
                        sp.dma_start(raw[TL - 1:TL, a, 1, 0:EL],
                                     v[(T - 1) * P:E].rearrange("(t p) -> t p", t=1)).then_inc(s_raw, 16)
                    sp.wait_ge(s_rowf, 1)
                    r = dst_rows[0]
                    sp.dma_start(r[0:P * P].rearrange("(t p) -> t p", p=P), rowf[:, 1, 0, :]).then_inc(s_rows, 16)
                    sp.dma_start(r[P * P:SLOTS + P].rearrange("(t p) -> t p", p=P),
                                 rowf[0:TL + 1, 1, 1, :]).then_inc(s_rows, 16)
                    sp.wait_ge(s_rows, 32)
                    sp.dma_start(rown[:, 0, :], r[1:P * P + 1].rearrange("(t p) -> t p", p=P)).then_inc(s_next, 16)
                    sp.dma_start(rown[0:TL, 1, :],
                                 r[P * P + 1:SLOTS + 1].rearrange("(t p) -> t p", p=P)).then_inc(s_next, 16)
                    sp.dma_start(prev_col[1:P, 0:1], r[0:P * P].rearrange("(t p) -> t p", p=P)[0:P - 1, P - 1:P],
                                 allow_slow_non_contiguous=True).then_inc(s_prev, 16)
                    sp.dma_start(prev_col[0:TL, 1:2],
                                 r[(P - 1) * P:(T - 1) * P].rearrange("(t p) -> t p", p=P)[:, P - 1:P],
                                 allow_slow_non_contiguous=True).then_inc(s_prev, 16)
                    sp.dma_start(carried.rearrange("g t c -> (g t) c").rearrange("(p a) c -> p a c", a=2),
                                 sq[0:T // 2, 0]).then_inc(s_carz, 16)
                    sp.wait_ge(s_const, 2)
                    loads = 0
                    for to, w in ((gW1_2[0:D, 0:D], gW1), (gW1_2[D:P, D:P], gW1), (gW2_2[0:D, 0:D], gW2),
                                  (gW2_2[D:P, D:P], gW2), (sW4_2[0:D, 0:D], sW4), (sW4_2[D:P, D:P], sW4),
                                  (gW1_a[0:D, 0:D], gW1), (sW3_a[0:D, 0:D], sW3), (gW2_s[:], gW2),
                                  (sW1_s[:], sW1), (sW2_s[:], sW2)):
                        sp.dma_start(to, w).then_inc(s_w, 16)
                        loads += 1
                    for row, b, n in ((b1_rows, gb1, J), (b2_rows, gb2, J), (sb1_row, sb1, 1), (sb2_rows, sb2, GROUP),
                                      (sb4_rows, sb4, GROUP)):
                        sp.dma_start(row[:].rearrange("o (n d) -> o n d", d=D),
                                     b.rearrange("(o n d) -> o n d", o=1, n=1).broadcast_to([1, n, D])).then_inc(s_w, 16)
                        loads += 1
                    for full, b in ((b1_all, gb1), (b2_all, gb2), (sb3_all, sb3)):
                        sp.dma_start(full[:], b.rearrange("(o d) -> o d", o=1).broadcast_to([P, D])).then_inc(s_w, 16)
                        loads += 1
                    sp.dma_start(sb3_col[:], sb3.rearrange("(d o) -> d o", o=1),
                                 allow_slow_non_contiguous=True).then_inc(s_w, 16)
                    loads += 1

                    sp.wait_ge(s_carr, 1)
                    flat = carried_rows.rearrange("g t p -> (g t) p")
                    sp.dma_start(flat[0:P, :], carr[:, 0, :]).then_inc(s_carw, 16)
                    sp.dma_start(flat[P:T, :], carr[0:TL, 1, :]).then_inc(s_carw, 16)
                    sp.wait_ge(s_carw, 32)
                    sp.wait_ge(s_carz, 16)
                    for t in range(GROUP):
                        sp.dma_start(carried[:, t, t * P:(t + 1) * P], carried_rows[:, t, :]).then_inc(s_carc, 16)

                    def fetch(g, u):
                        if not early(g):
                            sp.wait_ge(s_xt, freed(g))
                        for k in range(2):
                            rows = PL if isinstance(g, int) and 2 * g + k == NBLK - 1 else P
                            sp.dma_start(xin[0:rows, u, k].rearrange("p j d -> p (j d)"), blocks(x, 2 * g + k, rows)).then_inc(s_x[u], 16)

                    def store(g, u, turn):
                        sp.wait_ge(s_hs, done(g))
                        for k in range(2):
                            rows = PL if isinstance(g, int) and 2 * g + k == NBLK - 1 else P
                            sp.dma_start(blocks(table_a, 2 * g + k, rows), arow[0:rows, u, k].rearrange("p j d -> p (j d)")).then_inc(s_a[u], 16)

                    each_group_ahead(sp, NG, fetch, store)
                    sp.wait_ge(s_w, 16 * loads)
                    sp.wait_ge(s_carc, 16 * GROUP)
                    sp.wait_ge(s_a[0], 32 * (PAIRS + 2))
                    sp.wait_ge(s_a[1], 32 * (PAIRS + 1))

                @block.gpsimd
                def _(pool):
                    max_node = pool.to_reg(N - 1)
                    max_row = pool.to_reg(SLOTS + N - 1)
                    pool.memset(ident[:], 0.0)
                    pool.memset(before[:], 0.0)
                    pool.memset(last_row[:], 0.0)
                    pool.memset(ones[:], 1.0)
                    pool.iota(iota_hi[:], pattern=[[1, NC]], base=0, channel_multiplier=0,
                              allow_small_or_imprecise_dtypes=True)
                    pool.iota(iota_lo[:], pattern=[[1, P]], base=0, channel_multiplier=0,
                              allow_small_or_imprecise_dtypes=True)
                    pool.iota(nodes[:].rearrange("p (b j) -> p b j", j=J), pattern=[[BLOCK, NBLK], [1, J]],
                              base=SLOTS, channel_multiplier=J,
                              allow_small_or_imprecise_dtypes=True).then_inc(s_chain, 1)
                    pool.wait_ge(s_chain, 1)
                    pool.affine_select(out=ident[:], in_=ident[:], compare_op=ALU.not_equal, fill=1.0, base=0,
                                       pattern=[[-1, P]], channel_multiplier=1)
                    pool.affine_select(out=before[:], in_=before[:], compare_op=ALU.is_ge, fill=1.0, base=0,
                                       pattern=[[-1, P]], channel_multiplier=1)
                    pool.affine_select(out=last_row[:], in_=last_row[:], compare_op=ALU.not_equal, fill=1.0,
                                       base=-(P - 1), pattern=[[0, P]], channel_multiplier=1).then_inc(s_const, 1)
                    pool.wait_ge(s_idx, 1)

                    def gather(g, u, turn):
                        pool.tensor_copy(idx[:, u, :], dst_u[:, bass.ds(g * GROUP, GROUP)]).then_inc(s_staged, 1)
                        pool.wait_ge(s_staged, g + 1)
                        if not early(g):
                            pool.wait_ge(s_xs[u], 16 * turn)
                        pool.sem_inc(s_pace, 1)
                        for t in range(GROUP):
                            pool.indirect_dma_start(
                                xg[:, u, t, :], None, x, bass.IndirectOffsetOnAxis(ap=idx[:, u, t:t + 1], axis=0),
                                bounds_check=max_node, oob_is_err=False).then_inc(s_xg[u], 16)

                    def store(g, u, turn):
                        pool.wait_ge(s_xg[u], 16 * GROUP * (turn + 1))
                        pool.dma_start(x_dst[bass.ds(g * GC, GC), :].rearrange("(t p) d -> p t d", p=P),
                                       xg[:, u]).then_inc(s_xs[u], 16)

                    each_group_lead(pool, NG, gather, store, peel=1)
                    pool.wait_ge(s_xs[0], 16 * (PAIRS + 1))
                    pool.wait_ge(s_xs[1], 16 * PAIRS)

                @block.tensor
                def _(pe):
                    pe.wait_ge(s_const, 2)
                    pe.wait_ge(s_rowf, 1)
                    for a in range(2):
                        pe.transpose(bank[4 + a][:, 0:P], rowf[:, a, 0, :], ident[:])
                        last = pe.transpose(bank[4 + a][:, P:T], rowf[0:TL, a, 1, :], ident[0:TL, 0:TL])
                    last.then_inc(s_turned, 1)
                    pe.wait_ge(s_next, 32)
                    pe.wait_ge(s_const, 2)
                    pe.transpose(bank[6][:, 0:P], rown[:, 0, :], ident[:])
                    pe.transpose(bank[6][:, P:T], rown[0:TL, 1, :], ident[0:TL, 0:TL]).then_inc(s_turned, 1)
                    pe.wait_ge(s_slots, 1)
                    pe.matmul(bank[7][:, 0:T], last_row[:], dst_f[:], start=True, stop=True).then_inc(s_last, 1)
                    pe.wait_ge(s_rest_v, 1)
                    pe.matmul(bank[5][:, 0:D], rest_lhs[:], sW4_2[0:D, 0:D], start=True, stop=False)
                    pe.matmul(bank[5][:, 0:D], ones[0:1, :], sb4_rows[:, 0:D], start=False, stop=True).then_inc(s_rest_p, 1)
                    for b in range(4):
                        pe.matmul(bank[b][:, 0:HC], zeros[:, 0:P], zeros[:], start=True, stop=False)
                    with pe.Fori(0, NG) as i:
                        for t in range(GROUP):
                            pe.wait_ge(s_hot, GROUP * i + t + 1)
                            for b in range(4):
                                last = pe.matmul(bank[b][:, 0:HC], hot_lo[:, t, b // 2, :],
                                                 hot_hi[:, t, b // 2, (b % 2) * HC:(b % 2 + 1) * HC],
                                                 start=False, stop=False)
                            last.then_inc(s_hist, 1)
                    for b in range(4):
                        last = pe.matmul(bank[b][:, 0:HC], zeros[:, 0:P], zeros[:], start=False, stop=True)
                    last.then_inc(s_hist_end, 1)
                    pe.wait_ge(s_pp, 1)
                    pe.matmul(bank[4][:, 0:NBLK], before[:], per_p[:], start=True, stop=True)
                    pe.matmul(bank[5][:, 0:NBLK], ones[:], per_p[:], start=True, stop=True).then_inc(s_pre, 1)
                    pe.wait_ge(s_extra, 1)

                    def turn_x(g, u, turn):
                        pe.wait_ge(s_x[u], 32 * (turn + 1))
                        pe.wait_ge(s_xtc, freed(g))
                        for k in range(2):
                            for q in range(4):
                                last = pe.transpose(bank[4 * u + 2 * k][:, q * P:(q + 1) * P],
                                                    xin[:, u, k, 2 * q:2 * q + 2, :].rearrange("p j d -> p (j d)"),
                                                    ident[:])
                        last.then_inc(s_xt, 1)

                    def center(g, u, turn):
                        pe.wait_ge(s_xtc, done(g))
                        pe.wait_ge(s_hs, freed(g))
                        for k in range(2):
                            for q in range(4):
                                last = pe.matmul(bank[4 * u + 2 * k + 1][:, q * P:(q + 1) * P],
                                                 xT[:, u, k, q * P:(q + 1) * P], center2[:], start=True, stop=True)
                        last.then_inc(s_cen, 1)

                    each_group_lead(pe, NG, turn_x, center)

                @block.scalar
                def _(act):
                    act.wait_ge(s_w, 16 * 20)
                    act.wait_ge(s_const, 2)

                    def half_softplus(y, r, n):
                        act.activation(r[0], y, ACT.Abs).then_inc(s_rest_a, 1)
                        act.wait_ge(s_rest_a, n + 1)
                        act.activation(r[1], r[0], ACT.Exp, scale=-1.0).then_inc(s_rest_a, 1)
                        act.wait_ge(s_rest_a, n + 2)
                        act.activation(r[0], r[1], ACT.Ln, bias=half_col[0:r[0].shape[0], :],
                                       scale=0.5).then_inc(s_rest_a, 1)

                    half_softplus(sb3_col[:], (rest[0:D, 0, 0:1], rest[0:D, 1, 0:1]), 0)
                    act.wait_ge(s_rest_p, 1)
                    half_softplus(bank[5][:, 0:D], (rest[:, 2, :], rest[:, 3, :]), 3)
                    act.wait_ge(s_hist_end, 1)
                    for b in range(2):
                        last = act.activation(ends[:, b * HC:(b + 1) * HC], bank[2 + b][:, 0:HC], ACT.Sqrt, bias=1.0)
                    last.then_inc(s_root, 1)

                    def square(g, u, turn):
                        act.wait_ge(s_xt, done(g))
                        act.wait_ge(s_cen, freed(g))
                        for k in range(2):
                            last = act.activation(xT[:, u, k, :], bank[4 * u + 2 * k][:], ACT.Copy)
                        last.then_inc(s_xtc, 1)
                        act.wait_ge(s_cen, done(g))
                        act.wait_ge(s_var, freed(g))
                        for k in range(2):
                            last = act.activation(sq[:, u, k, :], bank[4 * u + 2 * k + 1][:], ACT.Square, scale=0.125)
                        last.then_inc(s_sq, 1)

                    def deviation(g, u, turn):
                        act.wait_ge(s_var, done(g))
                        act.wait_ge(s_rs, freed(g))
                        act.activation(sd[:, u, :], var[:, u, :], ACT.Sqrt, bias=eps_col[:]).then_inc(s_sd, 1)

                    each_group_lead(act, NG, square, deviation)

                @block.vector
                def _(dve):
                    links = [0]

                    def link(ins):
                        links[0] += 1
                        ins.then_inc(s_chain2, 1)
                        dve.wait_ge(s_chain2, links[0])

                    dve.memset(raw[:], SKIP).then_inc(s_padded, 1)
                    for z in (gW1_2, gW2_2, sW4_2, gW1_a, sW3_a, center2):
                        dve.memset(z[:], 0.0)
                    dve.memset(arow[:], 1.0)
                    dve.memset(xin[:], 0.0)
                    dve.memset(sq[:], 0.0)
                    dve.memset(prev_col[:], -1.0)
                    dve.memset(half_col[:], 0.5)
                    dve.memset(upto[:, 0:1], 0.0)
                    dve.memset(eps_col[:], EPS)
                    dve.memset(ones_3[:], 1.0)
                    for parts in (b1_3, b2_3, sb1_3, sb2_3, sb4_3):
                        dve.memset(parts[:], 0.0)
                    link(dve.memset(zeros[:], 0.0))
                    dve.memset(gW1_a[D:D + 1, D:D + 1], 1.0)
                    dve.memset(sW3_a[D:D + 1, D:D + 1], 1.0)
                    dve.memset(center2[0:D, 0:D], -1.0 / D)
                    dve.memset(dst_last[:, 0:1], -1.0)
                    link(dve.memset(center2[D:P, D:P], -1.0 / D))
                    dve.wait_ge(s_const, 1)
                    dve.tensor_tensor(center2[:], center2[:], ident[:], ALU.add).then_inc(s_const, 1)
                    dve.wait_ge(s_raw, 96)
                    dve.tensor_copy(rowf[:], raw[:]).then_inc(s_rowf, 1)
                    dve.wait_ge(s_turned, 1)
                    dve.tensor_copy(src_f[:], bank[4][:, 0:T])
                    dve.tensor_copy(dst_f[:], bank[5][:, 0:T]).then_inc(s_slots, 1)
                    dve.wait_ge(s_slots, 1)
                    link(dve.tensor_copy(dst_u[:], dst_f[:]))
                    dve.tensor_copy(src_u[:], src_f[:]).then_inc(s_idx, 1)
                    link(dve.tensor_tensor(keep[:], src_f[:], dst_f[:], ALU.not_equal))
                    link(dve.scalar_tensor_tensor(dst_kept[:], dst_f[:], 1.0, keep[:], ALU.add, ALU.mult))
                    dve.tensor_scalar(dst_kept[:], dst_kept[:], -1.0, None, ALU.add)
                    dve.tensor_copy(bits[:, 0, :], src_f[:])
                    link(dve.tensor_copy(bits[:, 1, :], dst_f[:]))
                    dve.tensor_scalar(bits_lo[:], bits[:], 3, P - 1, ALU.logical_shift_right, ALU.bitwise_and)
                    dve.tensor_scalar(bits_hi[:], bits[:], 10, 3, ALU.logical_shift_right, ALU.logical_shift_left)
                    link(dve.tensor_scalar(bits_j[:], bits[:], J - 1, None, ALU.bitwise_and))
                    link(dve.tensor_tensor(bits_hi[:], bits_hi[:], bits_j[:], ALU.bitwise_or))
                    dve.tensor_copy(src_lo[:], bits_lo[:, 0, :])
                    dve.tensor_copy(dst_lo[:], bits_lo[:, 1, :])
                    dve.tensor_copy(src_hi[:], bits_hi[:, 0, :])
                    link(dve.tensor_copy(dst_hi[:], bits_hi[:, 1, :]))
                    dve.wait_ge(s_w, 16 * 20)
                    for b, parts in ((b1_rows, b1_3), (b2_rows, b2_3), (sb1_row, sb1_3), (sb2_rows, sb2_3),
                                     (sb4_rows, sb4_3)):
                        n = b.shape[1]
                        link(dve.tensor_copy(parts[0:1, :], b[:]))
                        link(dve.tensor_tensor(part_r[:, 0:n], b[:], parts[0:1, :], ALU.subtract))
                        link(dve.tensor_copy(part_b[:, 0:n], part_r[:, 0:n]))
                        dve.tensor_copy(parts[32:33, :], part_r[:, 0:n])
                        link(dve.tensor_tensor(part_s[:, 0:n], part_r[:, 0:n], part_b[:, 0:n], ALU.subtract))
                        link(dve.tensor_copy(parts[64:65, :], part_s[:, 0:n]))
                    dve.wait_ge(s_rest_a, 3)
                    link(dve.scalar_tensor_tensor(rest[0:D, 1, 0:1], sb3_col[:], 0.0, rest[0:D, 0, 0:1], ALU.max,
                                                  ALU.add))
                    dve.tensor_scalar(rest_lhs[:], ones[0:D, :], rest[0:D, 1, 0:1], None,
                                      ALU.mult).then_inc(s_rest_v, 1)
                    dve.wait_ge(s_rest_a, 6)
                    dve.scalar_tensor_tensor(rest_row[:], bank[5][:, 0:D], 0.0, rest[:, 2, :], ALU.max, ALU.add)
                    dve.wait_ge(s_last, 1)
                    link(dve.tensor_copy(dst_last[:, 1:T + 1], bank[7][:, 0:T]))
                    dve.tensor_tensor(goes_on[:], dst_last[:, 1:T + 1], dst_last[:, 0:T], ALU.is_equal)
                    dve.wait_ge(s_prev, 32)
                    dve.tensor_scalar(carr[:, 0, :], rowf[:, 1, 0, :], prev_col[:, 0:1], None, ALU.is_equal)
                    dve.tensor_scalar(carr[0:TL, 1, :], rowf[0:TL, 1, 1, :], prev_col[0:TL, 1:2], None,
                                      ALU.is_equal).then_inc(s_carr, 1)
                    dve.wait_ge(s_turned, 2)
                    link(dve.tensor_tensor(next_f[:], bank[6][:, 0:T], dst_f[:], ALU.is_equal))
                    link(dve.scalar_tensor_tensor(next_f[:], next_f[:], float(SKIP), dst_f[:], ALU.mult, ALU.add))
                    link(dve.tensor_copy(out_u[:], next_f[:]))
                    with dve.Fori(0, NG) as i:
                        for t in range(GROUP):
                            n = GROUP * i + t
                            dve.wait_ge(s_hist, n + 1)
                            dve.tensor_scalar(hot_lo[:, t, 0, :], iota_lo[:], dst_lo[:, bass.ds(n, 1)], None,
                                              ALU.is_equal)
                            dve.tensor_scalar(hot_lo[:, t, 1, :], iota_lo[:], src_lo[:, bass.ds(n, 1)],
                                              keep[:, bass.ds(n, 1)], ALU.is_equal, ALU.mult)
                            dve.tensor_scalar(hot_hi[:, t, 0, :], iota_hi[:], dst_hi[:, bass.ds(n, 1)], None,
                                              ALU.is_equal)
                            dve.tensor_scalar(hot_hi[:, t, 1, :], iota_hi[:], src_hi[:, bass.ds(n, 1)], None,
                                              ALU.is_equal).then_inc(s_hot, 1)
                    dve.wait_ge(s_hist_end, 1)
                    for b in range(2):
                        half = slice(b * HC, (b + 1) * HC)
                        link(dve.tensor_copy(in_cnt[:, half], bank[b][:, 0:HC]))
                    dve.wait_ge(s_root, 1)
                    link(dve.reciprocal(out_scale[:], ends[:]))
                    dve.tensor_reduce(per_p[:], in_cnt[:].rearrange("p (b j) -> p b j", j=J), AX_X,
                                      ALU.add).then_inc(s_pp, 1)
                    dve.wait_ge(s_pre, 1)
                    link(dve.tensor_tensor_scan(upto[:, 1:NBLK + 1], ones[:, 0:NBLK], bank[5][:, 0:NBLK], 0.0,
                                                ALU.mult, ALU.add))
                    link(dve.tensor_tensor(base[:], bank[4][:, 0:NBLK], upto[:, 0:NBLK], ALU.add))
                    ends_v = ends[:].rearrange("p (b j) -> p b j", j=J)
                    cnt_v = in_cnt[:].rearrange("p (b j) -> p b j", j=J)
                    for j in range(J):
                        link(dve.tensor_tensor(ends_v[:, :, j], cnt_v[:, :, j],
                                               base[:] if j == 0 else ends_v[:, :, j - 1], ALU.add))
                    link(dve.scalar_tensor_tensor(ends[:], ends[:], -1.0, nodes[:], ALU.add, ALU.subtract))
                    link(dve.scalar_tensor_tensor(ends[:], in_cnt[:], 0.0, ends[:], ALU.is_gt, ALU.mult))
                    dve.tensor_tensor(code[:], ends[:], nodes[:], ALU.add).then_inc(s_extra, 1)
                    dve.wait_ge(s_extra, 1)

                    def variance(g, u, turn):
                        dve.wait_ge(s_sq, done(g))
                        dve.wait_ge(s_sd, freed(g))
                        dve.tensor_reduce(var[:, u, :], sq[:, u].rearrange("p k (j d) -> p (k j) d", d=D), AX_X,
                                          ALU.add).then_inc(s_var, 1)

                    def scale(g, u, turn):
                        dve.wait_ge(s_sd, done(g))
                        dve.reciprocal(rs[:, u, :], sd[:, u, :]).then_inc(s_rs, 1)
                        dve.wait_ge(s_rs, done(g))
                        dve.tensor_tensor(rsio[:, u, :], rs[:, u, :], out_scale[:, bass.ds(g * 2 * J, 2 * J)],
                                          ALU.mult).then_inc(s_rsio, 1)
                        dve.wait_ge(s_a[u], 32 * (turn + 1))
                        dve.tensor_copy(arow[:, u, :, :, D + 1].rearrange("p k j -> p (k j)"),
                                        code[:, bass.ds(g * 2 * J, 2 * J)])
                        dve.wait_ge(s_rsio, done(g))
                        for k in range(2):
                            last = dve.scalar_tensor_tensor(
                                arow[:, u, k, :, 0:D], bank[4 * u + 2 * k + 1][:].rearrange("p (j d) -> p j d", d=D),
                                0.0, rsio[:, u, k * J:(k + 1) * J].unsqueeze(2).broadcast_to([P, J, D]),
                                ALU.max, ALU.mult)
                        last.then_inc(s_hs, 1)

                    each_group_lead(dve, NG, variance, scale)

        nc.clear_and_free_semaphores(signals)
        nc.all_engine_barrier()


        z_slot = ctx.enter_context(nc.sbuf_tensor("z_slot", [P, T, D + 1], F32))
        self_slot = ctx.enter_context(nc.sbuf_tensor("self_slot", [P, T, D], F32))
        signals = []
        with ExitStack() as ph:
            def sb(name, shape, dt=F32):
                return ph.enter_context(nc.sbuf_tensor(f"p2_{name}", shape, dt))

            def sem(name):
                signals.append(nc.alloc_semaphore(name))
                return signals[-1]

            bank_names = ("agg", "z", "slots", "xd", "t0", "z0", "t1", "z1")
            agg, zb, slots_b, xb, t0, z0, t1, z1 = [
                ph.enter_context(nc.psum_tensor(f"bank2_{n}", [P, 512], F32)) for n in bank_names]
            tb, zbk = (t0, t1), (z0, z1)

            idx = sb("idx", [P, RING, GROUP], U32)
            msg = sb("msg", [P, RING, GROUP, AROW])
            rows = sb("rows", [P, RING, GC])
            car = sb("car", [GROUP, RING, GC])
            seg = sb("seg", [P, RING, GROUP, P])
            carry = sb("carry", [D + 1, RING, GROUP + 1])
            crow = sb("crow", [GROUP, RING, D + 1])
            aggs = sb("aggs", [D + 1, RING, GC])
            code_i = sb("code_i", [P, RING, 3, GROUP], I32)
            code_f = sb("code_f", [P, RING, 2, GROUP])
            shot_lo = sb("shot_lo", [P, RING, GROUP, P], F16)
            shot_hi = sb("shot_hi", [P, RING, GROUP, T], F16)
            iota_t = sb("iota_t", [P, T], F16)
            hin = sb("hin", [P, RING, 2, J, D])
            xin = sb("xin", [P, RING, 2, J * D])
            hT = sb("hT", [P, 2, 4 * P])
            h1 = sb("h1", [P, RING, 2, J * D])
            rel = sb("rel", [P, 2, J * D])
            x1 = sb("x1", [P, RING, 2, J * D])
            res = sb("res", [P, RING, 2, J * D])
            xd = sb("xd", [P, RING, GROUP, D])
            xdT = sb("xdT", [P, 2 * P])
            xvar = sb("xvar", [P, GROUP])
            xsd = sb("xsd", [P, GROUP])
            xrs = sb("xrs", [P, GROUP])
            xh = sb("xh", [P, GROUP * D])
            xhT = sb("xhT", [P, 2 * P])

            s_iota2 = sem("s_iota2")
            s_staged = sem("s2_staged")
            s_msg = [sem(f"s2_msg{u}") for u in range(RING)]
            s_rows = [sem(f"s2_rows{u}") for u in range(RING)]
            s_in = [sem(f"s2_in{u}") for u in range(RING)]
            s_nd = [sem(f"s2_nd{u}") for u in range(RING)]
            s_nx = [sem(f"s2_nx{u}") for u in range(RING)]
            s_xd = [sem(f"s2_xd{u}") for u in range(RING)]
            s_sth = [sem(f"s2_sth{u}") for u in range(RING)]
            s_st = [sem(f"s2_st{u}") for u in range(RING)]
            s_so = [sem(f"s2_so{u}") for u in range(RING)]
            stages = {n: sem("s2_" + n) for n in (
                "seg", "agg", "scan", "crT", "crow", "carried", "aggs", "z", "zs", "codei", "codes", "hot", "slot", "hotf",
                "t1", "t1c", "w1", "y", "h1", "t2", "t2c", "w2", "rel", "h2", "x1", "res",
                "xt", "xtc", "xcen", "xsq", "xvar", "xsd", "xrs", "xh", "xt2", "xt2c", "xw", "xws")}
            S = stages
            s_link, s_link2 = sem("s2_link"), sem("s2_link2")

            s_pace = sem("s2_pace")
            s_paced = sem("s2_paced")
            with nc.Block() as block:
                @block.sync
                def _(sp):
                    for s in S.values():
                        sp.sem_inc(s, RING)
                    for u in range(RING):
                        sp.sem_inc(s_sth[u], 16)
                        sp.sem_inc(s_st[u], 16)
                        sp.sem_inc(s_so[u], 16)

                    def fetch_rows(g, u, turn):
                        sp.wait_ge(S["seg"], freed(g))
                        sp.dma_start(rows[:, u], dst_rows[:, bass.ds(g * GC, GC)].broadcast_to([P, GC])).then_inc(s_rows[u], 16)

                    def fetch_car(g, u, turn):
                        sp.wait_ge(S["carried"], freed(g))
                        sp.dma_start(car[:, u], carried[bass.ds(g, 1)].rearrange("o t c -> (o t) c")).then_inc(s_in[u], 16)

                    def lens(g):
                        return (0, P), (1, PL if isinstance(g, int) and g == NG - 1 else P)

                    def fetch_hs(g, u, turn):
                        sp.wait_ge(S["t1"], freed(g))
                        for k, n in lens(g):
                            sp.dma_start(hin[0:n, u, k], table_a[bass.ds((2 * g + k) * BLOCK, n * J), 0:D].rearrange(
                                "(p j) d -> p j d", j=J)).then_inc(s_nd[u], 16)

                    def fetch_x(g, u, turn):
                        sp.wait_ge(S["x1"], freed(g))
                        for k, n in lens(g):
                            sp.dma_start(xin[0:n, u, k], blocks(x, 2 * g + k, n)).then_inc(s_nx[u], 16)

                    def fetch_x_dst(g, u, turn):
                        sp.wait_ge(S["xt"], freed(g))
                        sp.dma_start(xd[:, u], tiles(x_dst, g)).then_inc(s_xd[u], 16)

                    def store_h(g, u, turn):
                        sp.wait_ge(S["h1"], done(g))
                        sp.dma_start(both(local_h, g), h1[:, u]).then_inc(s_sth[u], 16)

                    def store_x(g, u, turn):
                        sp.wait_ge(S["res"], done(g))
                        sp.sem_inc(s_paced, 1)
                        if isinstance(g, int) and g == NG - 1:
                            sp.dma_start(blocks(out, 2 * g, P), res[:, u, 0]).then_inc(s_so[u], 16)
                            sp.dma_start(blocks(out, 2 * g + 1, PL), res[0:PL, u, 1]).then_inc(s_so[u], 16)
                        else:
                            sp.dma_start(both(out, g), res[:, u]).then_inc(s_so[u], 16)
                        sp.dma_start(both(local_x, g), x1[:, u]).then_inc(s_st[u], 16)

                    each_group_staged(sp, NG, (0, fetch_rows), (0, fetch_x_dst), (0, fetch_hs), (0, fetch_car),
                                      (2, store_h), (1, fetch_x), (3, store_x))
                    sp.wait_ge(s_sth[0], 16 * (PAIRS + 2))
                    sp.wait_ge(s_sth[1], 16 * (PAIRS + 1))
                    sp.wait_ge(s_st[0], 16 * (PAIRS + 2))
                    sp.wait_ge(s_st[1], 16 * (PAIRS + 1))
                    sp.wait_ge(s_so[0], 16 * (PAIRS + 3))
                    sp.wait_ge(s_so[1], 16 * (PAIRS + 1))

                @block.gpsimd
                def _(pool):
                    max_node = pool.to_reg(N - 1)
                    pool.iota(iota_t[:], pattern=[[1, T]], base=0, channel_multiplier=0,
                              allow_small_or_imprecise_dtypes=True).then_inc(s_iota2, 1)

                    def gather(g, u, turn):
                        if not early(g):
                            pool.wait_ge(S["agg"], freed(g))
                            pool.wait_ge(S["codei"], freed(g))
                        pool.tensor_copy(idx[:, u, :], src_u[:, bass.ds(g * GROUP, GROUP)]).then_inc(s_staged, 1)
                        pool.wait_ge(s_staged, g + 1)
                        pool.sem_inc(s_pace, 1)
                        for t in range(GROUP):
                            pool.indirect_dma_start(
                                msg[:, u, t, :], None, table_a,
                                bass.IndirectOffsetOnAxis(ap=idx[:, u, t:t + 1], axis=0),
                                bounds_check=max_node, oob_is_err=False).then_inc(s_msg[u], 16)

                    def add_rest(g, u, turn):
                        pool.wait_ge(S["x1"], done(g))
                        pool.wait_ge(s_so[u], 16 * (turn + 1))
                        for k in range(2):
                            last = pool.tensor_tensor(
                                res[:, u, k].rearrange("p (j d) -> p j d", d=D),
                                x1[:, u, k].rearrange("p (j d) -> p j d", d=D),
                                rest_row[:].unsqueeze(1).broadcast_to([P, J, D]), ALU.add)
                        last.then_inc(S["res"], 1)

                    each_group_staged(pool, NG, (0, gather), (3, add_rest))

                @block.tensor
                def _(pe):
                    pe.matmul(slots_b[:, 0:T], zeros[:, 0:P], zeros[:, 0:T], start=True, stop=False)

                    def step_t1(g, u, turn):
                        pe.wait_ge(s_nd[u], 32 * (turn + 1))
                        pe.wait_ge(S["t2c"], done(g - 1))
                        for k in range(2):
                            for q in range(4):
                                last = pe.transpose(tb[k][:, q * P:(q + 1) * P], 
                                                    hin[:, u, k, 2 * q:2 * q + 2, :].rearrange("p j d -> p (j d)"), ident[:])
                        last.then_inc(S["t1"], 1)

                    def step_xt(g, u, turn):
                        pe.wait_ge(s_xd[u], 16 * (turn + 1))
                        pe.wait_ge(S["xws"], done(g - 1))
                        for q in range(2):
                            last = pe.transpose(xb[:, q * P:(q + 1) * P],
                                                xd[:, u, 2 * q:2 * q + 2, :].rearrange("p t d -> p (t d)"), ident[:])
                        last.then_inc(S["xt"], 1)

                    def step_agg(g, u, turn):
                        pe.wait_ge(s_msg[u], 16 * GROUP * (turn + 1))
                        pe.wait_ge(S["seg"], done(g))
                        pe.wait_ge(S["aggs"], done(g - 1))
                        for t in range(GROUP):
                            last = pe.matmul(agg[0:D + 1, t * P:(t + 1) * P], msg[:, u, t, 0:D + 1], seg[:, u, t, :],
                                             start=(t == 0), stop=False, skip_group_check=True)
                        last.then_inc(S["agg"], 1)

                    def step_w1(g, u, turn):
                        pe.wait_ge(S["t1c"], done(g))
                        pe.wait_ge(S["rel"], done(g - 1))
                        pe.wait_ge(S["h2"], done(g - 1))
                        for k in range(2):
                            for q in range(4):
                                pe.matmul(zbk[k][:, q * P:(q + 1) * P], hT[:, k, q * P:(q + 1) * P], gW1_2[:],
                                          start=(q == 0), stop=False, skip_group_check=True)
                            last = pe.matmul(zbk[k][:], ones_3[:, 0:P], b1_3[:], start=False, stop=True,
                                             skip_group_check=True)
                        last.then_inc(S["w1"], 1)

                    def step_xcen(g, u, turn):
                        pe.wait_ge(S["xtc"], done(g))
                        for q in range(2):
                            last = pe.matmul(xb[:, (2 + q) * P:(3 + q) * P], xdT[:, q * P:(q + 1) * P], center2[:],
                                             start=True, stop=True)
                        last.then_inc(S["xcen"], 1)

                    def step_crT(g, u, turn):
                        pe.wait_ge(S["scan"], done(g))
                        pe.wait_ge(S["zs"], done(g - 1))
                        pe.transpose(zb[0:GROUP, 0:D + 1], carry[:, u, 0:GROUP],
                                     ident[0:D + 1, 0:D + 1]).then_inc(S["crT"], 1)

                    def step_slot(g, u, turn):
                        pe.wait_ge(S["hot"], done(g))
                        for t in range(GROUP):
                            last = pe.matmul(slots_b[:, 0:T], shot_lo[:, u, t, :], shot_hi[:, u, t, :],
                                             start=False, stop=False)
                        last.then_inc(S["slot"], 1)

                    def step_t2(g, u, turn):
                        pe.wait_ge(S["h1"], done(g))
                        for k in range(2):
                            for q in range(4):
                                last = pe.transpose(tb[k][:, q * P:(q + 1) * P], h1[:, u, k, q * P:(q + 1) * P], ident[:])
                        last.then_inc(S["t2"], 1)

                    def step_carried(g, u, turn):
                        pe.wait_ge(S["crow"], done(g))
                        pe.wait_ge(s_in[u], 16 * (turn + 1))
                        pe.matmul(agg[0:D + 1, :], crow[:, u, :], car[:, u, :], start=False, stop=True,
                                  skip_group_check=True).then_inc(S["carried"], 1)

                    def step_xt2(g, u, turn):
                        pe.wait_ge(S["xh"], done(g))
                        for q in range(2):
                            last = pe.transpose(xb[:, q * P:(q + 1) * P], xh[:, q * P:(q + 1) * P], ident[:])
                        last.then_inc(S["xt2"], 1)

                    def step_w2(g, u, turn):
                        pe.wait_ge(S["t2c"], done(g))
                        for k in range(2):
                            for q in range(4):
                                pe.matmul(zbk[k][:, q * P:(q + 1) * P], hT[:, k, q * P:(q + 1) * P], gW2_2[:],
                                          start=(q == 0), stop=False, skip_group_check=True)
                            last = pe.matmul(zbk[k][:], ones_3[:, 0:P], b2_3[:], start=False, stop=True,
                                             skip_group_check=True)
                        last.then_inc(S["w2"], 1)

                    def step_z(g, u, turn):
                        pe.wait_ge(S["aggs"], done(g))
                        for t in range(GROUP):
                            last = pe.matmul(zb[:, t * (D + 1):(t + 1) * (D + 1)], aggs[:, u, t * P:(t + 1) * P], gW1_a[:],
                                             start=True, stop=True)
                        last.then_inc(S["z"], 1)

                    def step_xw(g, u, turn):
                        pe.wait_ge(S["xt2c"], done(g))
                        for q in range(2):
                            last = pe.matmul(xb[:, (2 + q) * P:(3 + q) * P], xhT[:, q * P:(q + 1) * P], gW1_2[:],
                                             start=True, stop=True)
                        last.then_inc(S["xw"], 1)

                    each_group_staged(pe, NG, (1, step_t2), (1, step_xw), (0, step_xt), (0, step_t1),
                                      (1, step_w2), (0, step_agg), (1, step_z), (0, step_xcen), (0, step_crT),
                                      (0, step_w1), (0, step_slot), (0, step_carried), (0, step_xt2))
                    pe.matmul(slots_b[:, 0:T], zeros[:, 0:P], zeros[:, 0:T], start=False, stop=True).then_inc(s_link, 1)

                @block.scalar
                def _(act):
                    def step_t1c(g, u, turn):
                        act.wait_ge(S["t1"], done(g))
                        act.wait_ge(S["w2"], done(g - 1))
                        for k in range(2):
                            last = act.activation(hT[:, k], tb[k][:], ACT.Copy)
                        last.then_inc(S["t1c"], 1)

                    def step_xtc(g, u, turn):
                        act.wait_ge(S["xt"], done(g))
                        act.wait_ge(S["xcen"], done(g - 1))
                        act.activation(xdT[:], xb[:, 0:2 * P], ACT.Copy).then_inc(S["xtc"], 1)

                    def step_xsq(g, u, turn):
                        act.wait_ge(S["xcen"], done(g))
                        act.wait_ge(S["xt2"], done(g - 1))
                        act.activation(xh[:], xb[:, 2 * P:4 * P], ACT.Square, scale=0.125).then_inc(S["xsq"], 1)

                    def step_xsd(g, u, turn):
                        act.wait_ge(S["xvar"], done(g))
                        act.wait_ge(S["xrs"], done(g - 1))
                        act.activation(xsd[:], xvar[:], ACT.Sqrt, bias=eps_col[:]).then_inc(S["xsd"], 1)

                    def step_t2c(g, u, turn):
                        act.wait_ge(S["t2"], done(g))
                        act.wait_ge(S["w1"], done(g))
                        for k in range(2):
                            last = act.activation(hT[:, k], tb[k][:], ACT.Copy)
                        last.then_inc(S["t2c"], 1)

                    def step_aggs(g, u, turn):
                        act.wait_ge(S["carried"], done(g))
                        act.wait_ge(S["z"], freed(g))
                        act.activation(aggs[:, u], agg[0:D + 1, :], ACT.Copy).then_inc(S["aggs"], 1)

                    def step_xt2c(g, u, turn):
                        act.wait_ge(S["xt2"], done(g))
                        act.wait_ge(S["xw"], done(g - 1))
                        act.activation(xhT[:], xb[:, 0:2 * P], ACT.Copy).then_inc(S["xt2c"], 1)

                    def step_rel(g, u, turn):
                        act.wait_ge(S["w2"], done(g))
                        act.wait_ge(S["x1"], done(g - 1))
                        for k in range(2):
                            last = act.activation(rel[:, k], zbk[k][:], ACT.Relu, scale=1.0 - SLOPE)
                        last.then_inc(S["rel"], 1)

                    def step_zs(g, u, turn):
                        act.wait_ge(S["z"], done(g))
                        act.activation(z_slot[:, bass.ds(g * GROUP, GROUP), :],
                                       zb[:, 0:GROUP * (D + 1)].rearrange("p (t d) -> p t d", d=D + 1),
                                       ACT.Copy).then_inc(S["zs"], 1)

                    def step_xws(g, u, turn):
                        act.wait_ge(S["xw"], done(g))
                        act.activation(self_slot[:, bass.ds(g * GROUP, GROUP), :],
                                       xb[:, 2 * P:4 * P].rearrange("p (t d) -> p t d", d=D),
                                       ACT.Copy).then_inc(S["xws"], 1)

                    each_group_staged(act, NG, (1, step_t2c), (1, step_xws), (0, step_xtc), (0, step_t1c),
                                      (1, step_rel), (1, step_zs), (0, step_xsq), (0, step_xsd), (0, step_aggs),
                                      (0, step_xt2c))

                @block.vector
                def _(dve):
                    dve.memset(carry[:], 0.0).then_inc(s_link2, 1)
                    dve.wait_ge(s_link2, 1)
                    dve.wait_ge(s_iota2, 1)

                    def step_seg(g, u, turn):
                        cols = bass.ds(g * GROUP, GROUP)
                        dve.wait_ge(s_rows[u], 16 * (turn + 1))
                        dve.wait_ge(S["agg"], freed(g))
                        dve.tensor_tensor(seg[:, u], rows[:, u].rearrange("p (t i) -> p t i", i=P),
                                          dst_kept[:, cols].unsqueeze(2).broadcast_to([P, GROUP, P]),
                                          ALU.is_equal).then_inc(S["seg"], 1)

                    def step_codei(g, u, turn):
                        cols = bass.ds(g * GROUP, GROUP)
                        dve.wait_ge(s_msg[u], 16 * GROUP * (turn + 1))
                        dve.wait_ge(S["codes"], freed(g))
                        dve.tensor_copy(code_u[:, cols], msg[:, u, :, D + 1])
                        dve.tensor_copy(code_i[:, u, 0], msg[:, u, :, D + 1]).then_inc(S["codei"], 1)

                    def step_codes(g, u, turn):
                        dve.wait_ge(S["codei"], done(g))
                        dve.tensor_scalar(code_i[:, u, 1], code_i[:, u, 0], P - 1, None, ALU.bitwise_and)
                        dve.tensor_scalar(code_i[:, u, 2], code_i[:, u, 0], 7, None,
                                          ALU.logical_shift_right).then_inc(S["codes"], 1)

                    def step_y(g, u, turn):
                        dve.wait_ge(S["w1"], done(g))
                        dve.wait_ge(s_sth[u], 16 * (turn + 1))
                        dve.wait_ge(S["t2"], freed(g))
                        for k in range(2):
                            last = dve.tensor_tensor(
                                h1[:, u, k].rearrange("p (j d) -> p j d", d=D),
                                zbk[k][:].rearrange("p (j d) -> p j d", d=D),
                                out_scale[:, bass.ds(g * 2 * J + k * J, J)].unsqueeze(2).broadcast_to([P, J, D]),
                                ALU.mult)
                        last.then_inc(S["y"], 1)

                    def step_scan(g, u, turn):
                        cols = bass.ds(g * GROUP, GROUP)
                        dve.wait_ge(S["agg"], done(g))
                        dve.wait_ge(S["crT"], freed(g))
                        dve.wait_ge(S["scan"], done(g - 1))
                        dve.tensor_copy(carry[:, u, 0:1], carry[:, 1 - u, GROUP:GROUP + 1])
                        dve.tensor_tensor_scan(carry[:, u, 1:GROUP + 1], goes_on[0:D + 1, cols],
                                               agg[0:D + 1].rearrange("p (t i) -> p t i", i=P)[:, :, P - 1],
                                               carry[:, 1 - u, GROUP:GROUP + 1], ALU.mult,
                                               ALU.add).then_inc(S["scan"], 1)

                    def step_hotf(g, u, turn):
                        dve.wait_ge(S["codes"], done(g))
                        dve.wait_ge(S["hotf"], freed(g))
                        dve.tensor_copy(code_f[:, u], code_i[:, u, 1:3]).then_inc(S["hotf"], 1)

                    def step_h1(g, u, turn):
                        dve.wait_ge(S["y"], done(g))
                        for k in range(2):
                            last = dve.scalar_tensor_tensor(h1[:, u, k], h1[:, u, k], SLOPE, h1[:, u, k],
                                                            ALU.mult, ALU.max)
                        last.then_inc(S["h1"], 1)

                    def step_crow(g, u, turn):
                        dve.wait_ge(S["crT"], done(g))
                        dve.wait_ge(S["carried"], freed(g))
                        dve.tensor_copy(crow[:, u], zb[0:GROUP, 0:D + 1]).then_inc(S["crow"], 1)

                    def step_xvar(g, u, turn):
                        dve.wait_ge(S["xsq"], done(g))
                        dve.wait_ge(S["xsd"], done(g - 1))
                        dve.tensor_reduce(xvar[:], xh[:].rearrange("p (t d) -> p t d", d=D), AX_X,
                                          ALU.add).then_inc(S["xvar"], 1)

                    def step_hot(g, u, turn):
                        dve.wait_ge(S["hotf"], done(g))
                        dve.wait_ge(S["slot"], freed(g))
                        for t in range(GROUP):
                            dve.tensor_scalar(shot_lo[:, u, t], iota_lo[:], code_f[:, u, 0, t:t + 1],
                                              keep[:, bass.ds(g * GROUP + t, 1)], ALU.is_equal, ALU.mult)
                            last = dve.tensor_scalar(shot_hi[:, u, t], iota_t[:], code_f[:, u, 1, t:t + 1], None,
                                                     ALU.is_equal)
                        last.then_inc(S["hot"], 1)

                    def step_xrs(g, u, turn):
                        dve.wait_ge(S["xsd"], done(g))
                        dve.reciprocal(xrs[:], xsd[:]).then_inc(S["xrs"], 1)

                    def step_xh(g, u, turn):
                        dve.wait_ge(S["xrs"], done(g))
                        dve.wait_ge(S["xt2"], done(g - 1))
                        dve.scalar_tensor_tensor(xh[:].rearrange("p (t d) -> p t d", d=D),
                                                 xb[:, 2 * P:4 * P].rearrange("p (t d) -> p t d", d=D), 0.0,
                                                 xrs[:].unsqueeze(2).broadcast_to([P, GROUP, D]), ALU.max,
                                                 ALU.mult).then_inc(S["xh"], 1)

                    def step_h2(g, u, turn):
                        dve.wait_ge(S["rel"], done(g))
                        for k in range(2):
                            last = dve.scalar_tensor_tensor(rel[:, k], zbk[k][:], SLOPE, rel[:, k], ALU.mult, ALU.add)
                        last.then_inc(S["h2"], 1)

                    def step_x1(g, u, turn):
                        dve.wait_ge(S["h2"], done(g))
                        dve.wait_ge(S["res"], freed(g))
                        dve.wait_ge(s_st[u], 16 * (turn + 1))
                        dve.wait_ge(s_nx[u], 32 * (turn + 1))
                        for k in range(2):
                            last = dve.tensor_tensor(x1[:, u, k], rel[:, k], xin[:, u, k], ALU.add)
                        last.then_inc(S["x1"], 1)

                    each_group_staged(dve, NG, (0, step_seg), (0, step_codei), (0, step_scan), (0, step_codes),
                                      (1, step_h2), (0, step_xvar), (0, step_hotf), (0, step_crow), (0, step_y),
                                      (0, step_hot), (0, step_xrs), (0, step_xh), (0, step_h1), (1, step_x1))
                    dve.wait_ge(s_link, 1)
                    dve.tensor_copy(io_slot[:], slots_b[:, 0:T]).then_inc(s_link2, 1)
                    dve.wait_ge(s_link2, 2)

        nc.clear_and_free_semaphores(signals)
        nc.all_engine_barrier()


        CH = T // 7
        assert T == 7 * CH
        signals = []
        with ExitStack() as ph:
            def sb(name, shape, dt=F32):
                return ph.enter_context(nc.sbuf_tensor(f"p3_{name}", shape, dt))

            def sem(name):
                signals.append(nc.alloc_semaphore(name))
                return signals[-1]

            root = sb("root", [P, 2, T])
            s_root, s_inv, s_io, s_sum, s_ii, s_b, s_leak, s_h, s_st3 = (
                sem("s3_root"), sem("s3_inv"), sem("s3_io"), sem("s3_sum"), sem("s3_ii"), sem("s3_b"),
                sem("s3_leak"), sem("s3_h"), sem("s3_st"))

            with nc.Block() as block:
                def wide(col, c):
                    return col[:, bass.ds(c * CH, CH)].unsqueeze(2).broadcast_to([P, CH, D])

                @block.scalar
                def _(act):
                    act.activation(root[:, 0], io_slot[:], ACT.Sqrt, bias=1.0)
                    act.activation(root[:, 1], z_slot[:, :, D], ACT.Sqrt, bias=1.0).then_inc(s_root, 1)

                @block.gpsimd
                def _(pool):
                    pool.wait_ge(s_inv, 1)
                    with pool.Fori(0, 7) as c:
                        h = self_slot[:, bass.ds(c * CH, CH), :]
                        pool.tensor_tensor(h, h, wide(io_slot, c), ALU.mult).then_inc(s_io, 1)
                    with pool.Fori(0, 7) as c:
                        h = self_slot[:, bass.ds(c * CH, CH), :]
                        pool.wait_ge(s_leak, c + 1)
                        pool.tensor_tensor(h, h, wide(io_slot, c), ALU.mult).then_inc(s_h, 1)

                @block.vector
                def _(dve):
                    dve.wait_ge(s_root, 1)
                    dve.reciprocal(io_slot[:], root[:, 0])
                    dve.reciprocal(ii_slot[:], root[:, 1]).then_inc(s_inv, 1)
                    dve.wait_ge(s_inv, 1)
                    with dve.Fori(0, 7) as c:
                        h = self_slot[:, bass.ds(c * CH, CH), :]
                        dve.wait_ge(s_io, c + 1)
                        dve.tensor_tensor(h, h, z_slot[:, bass.ds(c * CH, CH), 0:D], ALU.add).then_inc(s_sum, 1)
                        dve.wait_ge(s_sum, c + 1)
                        dve.tensor_tensor(h, h, wide(ii_slot, c), ALU.mult).then_inc(s_ii, 1)
                        dve.wait_ge(s_ii, c + 1)
                        dve.tensor_tensor(h, h, b1_all[:].unsqueeze(1).broadcast_to([P, CH, D]),
                                          ALU.add).then_inc(s_b, 1)
                        dve.wait_ge(s_b, c + 1)
                        dve.scalar_tensor_tensor(h, h, SLOPE, h, ALU.mult, ALU.max).then_inc(s_leak, 1)

                @block.sync
                def _(sp):
                    with sp.Fori(0, 7) as c:
                        sp.wait_ge(s_h, c + 1)
                        sp.dma_start(table_h[bass.ds(c * CH * P, CH * P), :].rearrange("(t p) d -> p t d", p=P),
                                     self_slot[:, bass.ds(c * CH, CH), :]).then_inc(s_st3, 16)
                    sp.wait_ge(s_st3, 16 * 7)

        nc.clear_and_free_semaphores(signals)
        nc.all_engine_barrier()


        signals = []
        with ExitStack() as ph:
            def sb(name, shape, dt=F32):
                return ph.enter_context(nc.sbuf_tensor(f"p4_{name}", shape, dt))

            def sem(name):
                signals.append(nc.alloc_semaphore(name))
                return signals[-1]

            agg, zb, hdb, etb, e1b, e2b = [
                ph.enter_context(nc.psum_tensor(f"bank4_{n}", [P, 512], F32))
                for n in ("agg", "z", "hd", "et", "e1", "e2")]
            idx = sb("idx", [P, RING, GROUP], U32)
            msg = sb("msg", [P, RING, GROUP, D])
            rows = sb("rows", [P, RING, GC])
            car = sb("car", [GROUP, RING, GC])
            seg = sb("seg", [P, RING, GROUP, P])
            carry = sb("carry", [D + 1, RING, GROUP + 1])
            crow = sb("crow", [GROUP, RING, D])
            aggs = sb("aggs", [D, RING, GC])
            hd = sb("hd", [P, RING, GROUP, D])
            hdT = sb("hdT", [P, RING, 2 * P])
            xd = sb("xd", [P, RING, GROUP, D])
            y = sb("y", [P, 3, GROUP * D])
            x1 = sb("x1", [P, RING, GROUP, D])
            er = sb("er", [P, RING, GROUP, R])
            eh = sb("eh", [P, RING, GROUP, D])
            erT = sb("erT", [P, GC])
            pa = sb("pa", [D, 2, GC])
            w1 = sb("w1", [D, GC])
            pb_ = sb("pb_", [P, 2, GROUP * D])
            w2 = sb("w2", [P, GROUP * D])

            s_staged = sem("s4_staged")
            s_msg = [sem(f"s4_msg{u}") for u in range(RING)]
            s_rows = [sem(f"s4_rows{u}") for u in range(RING)]
            s_in = [sem(f"s4_in{u}") for u in range(RING)]
            s_hd = [sem(f"s4_hd{u}") for u in range(RING)]
            s_sl = [sem(f"s4_sl{u}") for u in range(RING)]
            s_er = [sem(f"s4_er{u}") for u in range(RING)]
            s_eh = [sem(f"s4_eh{u}") for u in range(RING)]
            s_st = [sem(f"s4_st{u}") for u in range(RING)]
            s_link = sem("s4_link")
            S = {n: sem("s4_" + n) for n in (
                "seg", "agg", "scan", "crT", "crow", "carried", "aggs", "hd", "hdT", "z", "y0", "y1", "y2", "x1",
                "et", "etc", "e1", "e1a", "e1e", "e1l", "w1", "e2", "e2a", "e2e", "e2l", "w2", "w")}

            s_pace = sem("s4_pace")
            with nc.Block() as block:
                @block.sync
                def _(sp):
                    for s in S.values():
                        sp.sem_inc(s, RING)
                    for u in range(RING):
                        sp.sem_inc(s_st[u], 16)

                    def fetch_rows(g, u, turn):
                        sp.wait_ge(S["seg"], freed(g))
                        sp.dma_start(rows[:, u], dst_rows[:, bass.ds(g * GC, GC)].broadcast_to([P, GC])).then_inc(s_rows[u], 16)

                    def fetch_car(g, u, turn):
                        sp.wait_ge(S["carried"], freed(g))
                        sp.dma_start(car[:, u], carried[bass.ds(g, 1)].rearrange("o t c -> (o t) c")).then_inc(s_in[u], 16)

                    def fetch_slots(g, u, turn):
                        sp.wait_ge(S["hd"], freed(g))
                        sp.dma_start(hd[:, u], tiles(table_h, g)).then_inc(s_hd[u], 16)

                    def fetch_x(g, u, turn):
                        sp.wait_ge(S["x1"], freed(g))
                        sp.dma_start(xd[:, u], tiles(x_dst, g)).then_inc(s_sl[u], 16)

                    def edges(to, v, s_to, g, u):
                        if isinstance(g, int) and g == NG - 1:
                            full, at = GROUP - 1, (T - 1) * P
                            sp.dma_start(to[:, u, 0:full], v[g * GC:at, :].rearrange("(t p) d -> p t d", p=P)).then_inc(s_to[u], 16)
                            sp.dma_start(to[0:EL, u, full], v[at:E, :]).then_inc(s_to[u], 16)
                        else:
                            sp.dma_start(to[:, u], tiles(v, g)).then_inc(s_to[u], 16)

                    def fetch_radial(g, u, turn):
                        sp.wait_ge(S["et"], freed(g))
                        edges(er, radial, s_er, g, u)

                    def fetch_edge_h(g, u, turn):
                        sp.wait_ge(S["w"], freed(g))
                        edges(eh, edge_h, s_eh, g, u)

                    def store(g, u, turn):
                        sp.wait_ge(S["x1"], done(g))
                        sp.dma_start(tiles(table_x, g), x1[:, u]).then_inc(s_st[u], 16)

                    each_group_staged(sp, NG, (0, fetch_rows), (0, fetch_radial), (0, fetch_slots), (0, fetch_car),
                                      (1, fetch_edge_h), (1, fetch_x), (3, store))
                    sp.wait_ge(s_st[0], 16 * (PAIRS + 2))
                    sp.wait_ge(s_st[1], 16 * (PAIRS + 1))

                @block.gpsimd
                def _(pool):
                    max_row = pool.to_reg(SLOTS + N - 1)
                    def gather(g, u, turn):
                        pool.wait_ge(S["agg"], freed(g))
                        pool.tensor_copy(idx[:, u, :], code_u[:, bass.ds(g * GROUP, GROUP)]).then_inc(s_staged, 1)
                        pool.wait_ge(s_staged, g + 1)
                        pool.sem_inc(s_pace, 1)
                        for t in range(GROUP):
                            pool.indirect_dma_start(
                                msg[:, u, t, :], None, table_h,
                                bass.IndirectOffsetOnAxis(ap=idx[:, u, t:t + 1], axis=0),
                                bounds_check=max_row, oob_is_err=False).then_inc(s_msg[u], 16)

                    each_group(pool, NG, gather)

                @block.tensor
                def _(pe):
                    def step_et(g, u, turn):
                        pe.wait_ge(s_er[u], 16 * turn + (32 if isinstance(g, int) and g == NG - 1 else 16))
                        pe.wait_ge(S["etc"], done(g - 1))
                        for t in range(GROUP):
                            last = pe.transpose(etb[:, t * P:(t + 1) * P], er[:, u, t], ident[:])
                        last.then_inc(S["et"], 1)

                    def step_hd(g, u, turn):
                        pe.wait_ge(s_hd[u], 16 * (turn + 1))
                        pe.wait_ge(S["hdT"], done(g - 1))
                        for q in range(2):
                            last = pe.transpose(hdb[:, q * P:(q + 1) * P],
                                                hd[:, u, 2 * q:2 * q + 2].rearrange("p t d -> p (t d)"), ident[:])
                        last.then_inc(S["hd"], 1)

                    def step_e1(g, u, turn):
                        pe.wait_ge(S["etc"], done(g))
                        pe.wait_ge(S["w1"], done(g - 1))
                        pe.matmul(e1b[0:D, :], sW1_s[:], erT[:], start=True, stop=False)
                        pe.matmul(e1b[0:D, :], sb1_3[:], ones_3[:], start=False, stop=True).then_inc(S["e1"], 1)

                    def step_agg(g, u, turn):
                        pe.wait_ge(s_msg[u], 16 * GROUP * (turn + 1))
                        pe.wait_ge(S["seg"], done(g))
                        pe.wait_ge(S["aggs"], done(g - 1))
                        for t in range(GROUP):
                            last = pe.matmul(agg[0:D, t * P:(t + 1) * P], msg[:, u, t, :], seg[:, u, t, :],
                                             start=(t == 0), stop=False, skip_group_check=True)
                        last.then_inc(S["agg"], 1)

                    def step_crT(g, u, turn):
                        pe.wait_ge(S["scan"], done(g))
                        pe.wait_ge(S["y0"], done(g - 1))
                        pe.transpose(zb[0:GROUP, 256:256 + D + 1], carry[:, u, 0:GROUP],
                                     ident[0:D + 1, 0:D + 1]).then_inc(S["crT"], 1)

                    def step_e2(g, u, turn):
                        pe.wait_ge(S["w1"], done(g))
                        pe.wait_ge(S["w2"], done(g - 1))
                        for t in range(GROUP):
                            pe.matmul(e2b[:, t * D:(t + 1) * D], w1[:, t * P:(t + 1) * P], sW2_s[:], start=(t == 0),
                                      stop=False, skip_group_check=True)
                        pe.matmul(e2b[:, 0:GROUP * D], ones_3[:, 0:P], sb2_3[:], start=False, stop=True,
                                  skip_group_check=True).then_inc(S["e2"], 1)

                    def step_carried(g, u, turn):
                        pe.wait_ge(S["crow"], done(g))
                        pe.wait_ge(s_in[u], 16 * (turn + 1))
                        pe.matmul(agg[0:D, :], crow[:, u, :], car[:, u, :], start=False, stop=True,
                                  skip_group_check=True).then_inc(S["carried"], 1)

                    def step_z(g, u, turn):
                        pe.wait_ge(S["hdT"], done(g))
                        pe.wait_ge(S["aggs"], done(g))
                        for q in range(2):
                            last = pe.matmul(zb[:, q * P:(q + 1) * P], hdT[:, u, q * P:(q + 1) * P], gW2_2[:],
                                             start=(q == 0), stop=False, skip_group_check=True)
                            for t in (2 * q, 2 * q + 1):
                                last = pe.matmul(zb[:, t * D:(t + 1) * D], aggs[:, u, t * P:(t + 1) * P], gW2_s[:],
                                                 start=False, stop=(t == GROUP - 1), skip_group_check=True)
                        last.then_inc(S["z"], 1)

                    each_group_staged(pe, NG, (0, step_et), (1, step_e2), (0, step_agg), (1, step_z),
                                      (0, step_e1), (0, step_crT), (0, step_carried), (0, step_hd))

                @block.scalar
                def _(act):
                    act.preload_act_table_set("natural_log_exp_and_others")

                    def step_etc(g, u, turn):
                        act.wait_ge(S["et"], done(g))
                        act.wait_ge(S["e1"], done(g - 1))
                        act.activation(erT[:], etb[:], ACT.Copy).then_inc(S["etc"], 1)

                    def step_hdT(g, u, turn):
                        act.wait_ge(S["hd"], done(g))
                        act.wait_ge(S["z"], freed(g))
                        act.activation(hdT[:, u], hdb[:, 0:2 * P], ACT.Copy).then_inc(S["hdT"], 1)

                    def step_e1a(g, u, turn):
                        act.wait_ge(S["e1"], done(g))
                        act.wait_ge(S["w1"], done(g - 1))
                        act.activation(pa[:, 0], e1b[0:D, :], ACT.Abs).then_inc(S["e1a"], 1)

                    def step_e1e(g, u, turn):
                        act.wait_ge(S["e1a"], done(g))
                        act.activation(pa[:, 1], pa[:, 0], ACT.Exp, scale=-1.0).then_inc(S["e1e"], 1)

                    def step_e1l(g, u, turn):
                        act.wait_ge(S["e1e"], done(g))
                        act.activation(pa[:, 0], pa[:, 1], ACT.Ln, bias=half_col[0:D, :],
                                       scale=0.5).then_inc(S["e1l"], 1)

                    def step_e2a(g, u, turn):
                        act.wait_ge(S["e2"], done(g))
                        act.wait_ge(S["w2"], done(g - 1))
                        act.activation(pb_[:, 0], e2b[:, 0:GROUP * D], ACT.Abs).then_inc(S["e2a"], 1)

                    def step_e2e(g, u, turn):
                        act.wait_ge(S["e2a"], done(g))
                        act.activation(pb_[:, 1], pb_[:, 0], ACT.Exp, scale=-1.0).then_inc(S["e2e"], 1)

                    def step_e2l(g, u, turn):
                        act.wait_ge(S["e2e"], done(g))
                        act.activation(pb_[:, 0], pb_[:, 1], ACT.Ln, bias=half_col[:], scale=0.5).then_inc(S["e2l"], 1)

                    def step_aggs(g, u, turn):
                        act.wait_ge(S["carried"], done(g))
                        act.wait_ge(S["z"], freed(g))
                        act.activation(aggs[:, u], agg[0:D, :], ACT.Copy).then_inc(S["aggs"], 1)

                    each_group_staged(act, NG, (0, step_etc), (1, step_e2a), (1, step_e2e), (0, step_e1a),
                                      (1, step_e2l), (0, step_e1e), (0, step_hdT), (0, step_e1l), (0, step_aggs))

                @block.vector
                def _(dve):
                    y0, y1, y2 = [y[:, n].rearrange("p (t d) -> p t d", d=D) for n in range(3)]
                    dve.memset(carry[:], 0.0).then_inc(s_link, 1)
                    dve.wait_ge(s_link, 1)

                    def step_seg(g, u, turn):
                        cols = bass.ds(g * GROUP, GROUP)
                        dve.wait_ge(s_rows[u], 16 * (turn + 1))
                        dve.wait_ge(S["agg"], freed(g))
                        dve.tensor_tensor(seg[:, u], rows[:, u].rearrange("p (t i) -> p t i", i=P),
                                          dst_kept[:, cols].unsqueeze(2).broadcast_to([P, GROUP, P]),
                                          ALU.is_equal).then_inc(S["seg"], 1)

                    def step_w1(g, u, turn):
                        dve.wait_ge(S["e1l"], done(g))
                        dve.wait_ge(S["e2"], done(g - 1))
                        dve.scalar_tensor_tensor(w1[:], e1b[0:D, :], 0.0, pa[:, 0], ALU.max,
                                                 ALU.add).then_inc(S["w1"], 1)

                    def step_scan(g, u, turn):
                        cols = bass.ds(g * GROUP, GROUP)
                        dve.wait_ge(S["agg"], done(g))
                        dve.wait_ge(S["crT"], freed(g))
                        dve.wait_ge(S["scan"], done(g - 1))
                        dve.tensor_copy(carry[:, u, 0:1], carry[:, 1 - u, GROUP:GROUP + 1])
                        dve.tensor_tensor_scan(carry[0:D, u, 1:GROUP + 1], goes_on[0:D, cols],
                                               agg[0:D].rearrange("p (t i) -> p t i", i=P)[:, :, P - 1],
                                               carry[0:D, 1 - u, GROUP:GROUP + 1], ALU.mult,
                                               ALU.add).then_inc(S["scan"], 1)

                    def step_crow(g, u, turn):
                        dve.wait_ge(S["crT"], done(g))
                        dve.wait_ge(S["carried"], freed(g))
                        dve.tensor_copy(crow[:, u], zb[0:GROUP, 256:256 + D]).then_inc(S["crow"], 1)

                    def step_w2(g, u, turn):
                        dve.wait_ge(S["e2l"], done(g))
                        dve.wait_ge(S["w"], done(g - 1))
                        dve.scalar_tensor_tensor(w2[:], e2b[:, 0:GROUP * D], 0.0, pb_[:, 0], ALU.max,
                                                 ALU.add).then_inc(S["w2"], 1)

                    def step_w(g, u, turn):
                        cols = bass.ds(g * GROUP, GROUP)
                        dve.wait_ge(S["w2"], done(g))
                        dve.wait_ge(s_eh[u], 16 * turn + (32 if isinstance(g, int) and g == NG - 1 else 16))
                        dve.tensor_tensor(self_slot[:, cols, :], w2[:].rearrange("p (t d) -> p t d", d=D), eh[:, u],
                                          ALU.mult).then_inc(S["w"], 1)

                    def step_y0(g, u, turn):
                        cols = bass.ds(g * GROUP, GROUP)
                        dve.wait_ge(S["z"], done(g))
                        dve.tensor_tensor(y0, zb[:, 0:GROUP * D].rearrange("p (t d) -> p t d", d=D),
                                          ii_slot[:, cols].unsqueeze(2).broadcast_to([P, GROUP, D]),
                                          ALU.mult).then_inc(S["y0"], 1)

                    def step_y1(g, u, turn):
                        dve.wait_ge(S["y0"], done(g))
                        dve.tensor_tensor(y1, y0, b2_all[:].unsqueeze(1).broadcast_to([P, GROUP, D]),
                                          ALU.add).then_inc(S["y1"], 1)

                    def step_y2(g, u, turn):
                        dve.wait_ge(S["y1"], done(g))
                        dve.scalar_tensor_tensor(y2, y1, SLOPE, y1, ALU.mult, ALU.max).then_inc(S["y2"], 1)

                    def step_x1(g, u, turn):
                        dve.wait_ge(S["y2"], done(g))
                        dve.wait_ge(s_sl[u], 16 * (turn + 1))
                        dve.wait_ge(s_st[u], 16 * (turn + 1))
                        dve.tensor_tensor(x1[:, u], y2, xd[:, u], ALU.add).then_inc(S["x1"], 1)

                    each_group_staged(dve, NG, (0, step_seg), (0, step_scan), (1, step_y0), (0, step_crow),
                                      (1, step_y1), (1, step_w2), (1, step_y2), (1, step_w), (1, step_x1),
                                      (0, step_w1))

        nc.clear_and_free_semaphores(signals)
        nc.all_engine_barrier()


        signals = []
        with ExitStack() as ph:
            def sb(name, shape, dt=F32):
                return ph.enter_context(nc.sbuf_tensor(f"pw_{name}", shape, dt))

            def sem(name):
                signals.append(nc.alloc_semaphore(name))
                return signals[-1]

            rank_u = sb("rank_u", [EP, EC], U32)
            idx = sb("idx", [EP, 1], U32)
            w_all = sb("w_all", [EP, EC, D])
            pay = sb("pay", [EP, D])
            s_st, s_ld, s_staged, s_pace, s_sc, s_back = (
                sem("sw_st"), sem("sw_ld"), sem("sw_staged"), sem("sw_pace"), sem("sw_sc"), sem("sw_back"))

            with nc.Block() as block:
                @block.sync
                def _(sp):
                    with sp.If(sp.value_load(unsorted[:]) > 0):
                        sp.dma_start(w_given.rearrange("(t p) d -> p t d", p=P), self_slot[:]).then_inc(s_st, 16)
                        sp.dma_start(rank_u[:], rank_d).then_inc(s_ld, 16)
                        sp.wait_ge(s_st, 16)
                        sp.dma_start(w_all[:], w_given[0:E, :].rearrange("(p c) d -> p c d", c=EC)).then_inc(s_ld, 16)
                        sp.wait_ge(s_sc, 16 * EC)
                        at = (T - 1) * P
                        sp.dma_start(self_slot[:, 0:T - 1, :],
                                     w_sorted[0:at, :].rearrange("(t p) d -> p t d", p=P)).then_inc(s_back, 16)
                        sp.dma_start(self_slot[0:EL, T - 1, :], w_sorted[at:E, :]).then_inc(s_back, 16)
                        sp.wait_ge(s_back, 32)

                @block.gpsimd
                def _(pool):
                    with pool.If(pool.value_load(unsorted[:]) > 0):
                        max_edge = pool.to_reg(E - 1)
                        pool.wait_ge(s_ld, 32)
                        with pool.Fori(0, EC) as t:
                            pool.tensor_copy(idx[:], rank_u[:, bass.ds(t, 1)]).then_inc(s_staged, 1)
                            pool.tensor_copy(pay[:], w_all[:, bass.ds(t, 1), :].rearrange("p c d -> p (c d)")).then_inc(s_staged, 1)
                            pool.wait_ge(s_staged, 2 * t + 2)
                            pool.sem_inc(s_pace, 1)
                            pool.indirect_dma_start(
                                w_sorted, bass.IndirectOffsetOnAxis(ap=idx[:], axis=0), pay[:], None,
                                bounds_check=max_edge, oob_is_err=False).then_inc(s_sc, 16)
                            pool.wait_ge(s_sc, 16 * t + 16)

        nc.clear_and_free_semaphores(signals)
        nc.all_engine_barrier()


        signals = []
        with ExitStack() as ph:
            def sb(name, shape, dt=F32):
                return ph.enter_context(nc.sbuf_tensor(f"p5_{name}", shape, dt))

            def sem(name):
                signals.append(nc.alloc_semaphore(name))
                return signals[-1]

            agg, zb, xb, sb_, qb = [
                ph.enter_context(nc.psum_tensor(f"bank5_{n}", [P, 512], F32))
                for n in ("agg", "z", "x", "s", "q")]
            idx = sb("idx", [P, RING, GROUP], U32)
            oidx = sb("oidx", [P, RING, GROUP], U32)
            xg = sb("xg", [P, RING, GROUP, D])
            rows = sb("rows", [P, RING, GC])
            car = sb("car", [GROUP, RING, GC])
            seg = sb("seg", [P, RING, GROUP, P])
            carry = sb("carry", [D + 1, RING, GROUP + 1])
            crow = sb("crow", [GROUP, RING, D + 1])
            aggs = sb("aggs", [D + 1, RING, GC])
            xT = sb("xT", [P, 2 * P])
            sq = sb("sq", [P, GROUP * D])
            var = sb("var", [P, GROUP])
            lnv = sb("lnv", [P, GROUP])
            rs = sb("rs", [P, 4, GROUP])
            xh = sb("xh", [P, GROUP, D])
            msg = sb("msg", [P, RING, GROUP, D + 1])
            cnt = sb("cnt", [P, 2, GROUP])
            y = sb("y", [P, 2, GROUP * D])
            pa = sb("pa", [P, 2, GROUP * D])
            s1 = sb("s1", [P, GROUP * D])
            s1T = sb("s1T", [P, 2 * P])
            pc = sb("pc", [P, 2, GROUP * D])
            f = sb("f", [P, GROUP * D])
            x1 = sb("x1", [P, RING, GROUP, D])
            res = sb("res", [P, RING, GROUP, D])

            s_staged, s_ostaged = sem("s5_staged"), sem("s5_ostaged")
            s_xg = [sem(f"s5_xg{u}") for u in range(RING)]
            s_rows = [sem(f"s5_rows{u}") for u in range(RING)]
            s_in = [sem(f"s5_in{u}") for u in range(RING)]
            s_sl = [sem(f"s5_sl{u}") for u in range(RING)]
            s_sc = [sem(f"s5_sc{u}") for u in range(RING)]
            s_link = sem("s5_link")
            S = {n: sem("s5_" + n) for n in (
                "xt", "xtc", "cen", "sq", "var", "lnv", "r0", "r1", "r2", "rs", "xh", "msg",
                "seg", "agg", "scan", "crT", "crow", "carried", "aggs", "z", "cnt", "rc", "y0", "y1",
                "ya", "ye", "yl", "s1", "st", "stc", "q", "qa", "qe", "ql", "f", "res")}

            s_pace = sem("s5_pace")
            with nc.Block() as block:
                @block.sync
                def _(sp):
                    for s in S.values():
                        sp.sem_inc(s, RING)

                    def fetch_rows(g, u, turn):
                        sp.wait_ge(S["seg"], freed(g))
                        sp.dma_start(rows[:, u], dst_rows[:, bass.ds(g * GC, GC)].broadcast_to([P, GC])).then_inc(s_rows[u], 16)

                    def fetch_car(g, u, turn):
                        sp.wait_ge(S["carried"], freed(g))
                        sp.dma_start(car[:, u], carried[bass.ds(g, 1)].rearrange("o t c -> (o t) c")).then_inc(s_in[u], 16)

                    def fetch_x1(g, u, turn):
                        sp.wait_ge(S["res"], freed(g))
                        sp.dma_start(x1[:, u], tiles(table_x, g)).then_inc(s_sl[u], 16)

                    each_group_staged(sp, NG, (0, fetch_rows), (1, fetch_car), (2, fetch_x1))
                    sp.wait_ge(s_sc[0], 16 * GROUP * (PAIRS + 1))
                    sp.wait_ge(s_sc[1], 16 * GROUP * PAIRS)

                @block.gpsimd
                def _(pool):
                    max_node = pool.to_reg(N - 1)
                    max_row = pool.to_reg(SLOTS + N - 1)
                    def gather(g, u, turn):
                        if not early(g):
                            pool.wait_ge(S["xt"], freed(g))
                        pool.tensor_copy(idx[:, u, :], code_u[:, bass.ds(g * GROUP, GROUP)]).then_inc(s_staged, 1)
                        pool.wait_ge(s_staged, g + 1)
                        pool.sem_inc(s_pace, 1)
                        for t in range(GROUP):
                            pool.indirect_dma_start(
                                xg[:, u, t, :], None, table_x,
                                bass.IndirectOffsetOnAxis(ap=idx[:, u, t:t + 1], axis=0),
                                bounds_check=max_row, oob_is_err=False).then_inc(s_xg[u], 16)

                    def scatter(g, u, turn):
                        if not early(g):
                            pool.wait_ge(s_sc[u], 16 * GROUP * turn)
                        pool.tensor_copy(oidx[:, u, :], out_u[:, bass.ds(g * GROUP, GROUP)]).then_inc(s_ostaged, 1)
                        pool.wait_ge(s_ostaged, g + 1)
                        pool.wait_ge(S["res"], done(g))
                        pool.sem_inc(s_pace, 1)
                        for t in range(GROUP):
                            pool.indirect_dma_start(
                                out, bass.IndirectOffsetOnAxis(ap=oidx[:, u, t:t + 1], axis=0),
                                res[:, u, t, :], None,
                                bounds_check=max_node, oob_is_err=False).then_inc(s_sc[u], 16)

                    each_group_staged(pool, NG, (0, gather), (4, scatter))

                @block.tensor
                def _(pe):
                    def step_xt(g, u, turn):
                        pe.wait_ge(s_xg[u], 16 * GROUP * (turn + 1))
                        pe.wait_ge(S["xh"], done(g - 1))
                        for q in range(2):
                            last = pe.transpose(xb[:, q * P:(q + 1) * P],
                                                xg[:, u, 2 * q:2 * q + 2, :].rearrange("p t d -> p (t d)"), ident[:])
                        last.then_inc(S["xt"], 1)

                    def step_cen(g, u, turn):
                        pe.wait_ge(S["xtc"], done(g))
                        for q in range(2):
                            last = pe.matmul(xb[:, (2 + q) * P:(3 + q) * P], xT[:, q * P:(q + 1) * P], center2[:],
                                             start=True, stop=True)
                        last.then_inc(S["cen"], 1)

                    def step_agg(g, u, turn):
                        pe.wait_ge(S["msg"], done(g))
                        pe.wait_ge(S["seg"], done(g))
                        pe.wait_ge(S["aggs"], done(g - 1))
                        for t in range(GROUP):
                            last = pe.matmul(agg[0:D + 1, t * P:(t + 1) * P], msg[:, u, t, :], seg[:, u, t, :],
                                             start=(t == 0), stop=False, skip_group_check=True)
                        last.then_inc(S["agg"], 1)

                    def step_crT(g, u, turn):
                        pe.wait_ge(S["scan"], done(g))
                        pe.wait_ge(S["y0"], done(g - 1))
                        pe.wait_ge(S["cnt"], done(g - 1))
                        pe.transpose(zb[0:GROUP, 320:320 + D + 1], carry[:, u, 0:GROUP],
                                     ident[0:D + 1, 0:D + 1]).then_inc(S["crT"], 1)

                    def step_carried(g, u, turn):
                        pe.wait_ge(S["crow"], done(g))
                        pe.wait_ge(s_in[u], 16 * (turn + 1))
                        pe.matmul(agg[0:D + 1, :], crow[:, u, :], car[:, u, :], start=False, stop=True,
                                  skip_group_check=True).then_inc(S["carried"], 1)

                    def step_z(g, u, turn):
                        pe.wait_ge(S["aggs"], done(g))
                        for t in range(GROUP):
                            last = pe.matmul(zb[:, t * (D + 1):(t + 1) * (D + 1)], aggs[:, u, t * P:(t + 1) * P],
                                             sW3_a[:], start=True, stop=True)
                        last.then_inc(S["z"], 1)

                    def step_st(g, u, turn):
                        pe.wait_ge(S["s1"], done(g))
                        pe.wait_ge(S["stc"], done(g - 1))
                        for q in range(2):
                            last = pe.transpose(sb_[:, q * P:(q + 1) * P], s1[:, q * P:(q + 1) * P], ident[:])
                        last.then_inc(S["st"], 1)

                    def step_q(g, u, turn):
                        pe.wait_ge(S["stc"], done(g))
                        pe.wait_ge(S["f"], done(g - 1))
                        for q in range(2):
                            pe.matmul(qb[:, q * P:(q + 1) * P], s1T[:, q * P:(q + 1) * P], sW4_2[:], start=(q == 0),
                                      stop=False, skip_group_check=True)
                        pe.matmul(qb[:, 0:2 * P], ones_3[:, 0:P], sb4_3[:], start=False, stop=True,
                                  skip_group_check=True).then_inc(S["q"], 1)

                    each_group_staged(pe, NG, (0, step_xt), (1, step_agg), (0, step_cen), (1, step_crT),
                                      (1, step_carried), (2, step_st), (1, step_z), (2, step_q))

                @block.scalar
                def _(act):
                    act.preload_act_table_set("natural_log_exp_and_others")

                    def step_xtc(g, u, turn):
                        act.wait_ge(S["xt"], done(g))
                        act.wait_ge(S["cen"], done(g - 1))
                        act.activation(xT[:], xb[:, 0:2 * P], ACT.Copy).then_inc(S["xtc"], 1)

                    def step_sq(g, u, turn):
                        act.wait_ge(S["cen"], done(g))
                        act.wait_ge(S["var"], done(g - 1))
                        act.activation(sq[:], xb[:, 2 * P:4 * P], ACT.Square, scale=0.125).then_inc(S["sq"], 1)

                    def step_lnv(g, u, turn):
                        act.wait_ge(S["var"], done(g))
                        act.activation(lnv[:], var[:], ACT.Ln, bias=eps_col[:]).then_inc(S["lnv"], 1)

                    def step_r0(g, u, turn):
                        act.wait_ge(S["lnv"], done(g))
                        act.wait_ge(S["rs"], done(g - 1))
                        act.activation(rs[:, 0], lnv[:], ACT.Exp, scale=-0.5).then_inc(S["r0"], 1)

                    def step_aggs(g, u, turn):
                        act.wait_ge(S["carried"], done(g))
                        act.wait_ge(S["z"], freed(g))
                        act.activation(aggs[:, u], agg[0:D + 1, :], ACT.Copy).then_inc(S["aggs"], 1)

                    def step_ya(g, u, turn):
                        act.wait_ge(S["y1"], done(g))
                        act.wait_ge(S["s1"], done(g - 1))
                        act.activation(pa[:, 0], y[:, 1], ACT.Abs).then_inc(S["ya"], 1)

                    def step_ye(g, u, turn):
                        act.wait_ge(S["ya"], done(g))
                        act.activation(pa[:, 1], pa[:, 0], ACT.Exp, scale=-1.0).then_inc(S["ye"], 1)

                    def step_yl(g, u, turn):
                        act.wait_ge(S["ye"], done(g))
                        act.activation(pa[:, 0], pa[:, 1], ACT.Ln, bias=half_col[:], scale=0.5).then_inc(S["yl"], 1)

                    def step_stc(g, u, turn):
                        act.wait_ge(S["st"], done(g))
                        act.wait_ge(S["q"], done(g - 1))
                        act.activation(s1T[:], sb_[:, 0:2 * P], ACT.Copy).then_inc(S["stc"], 1)

                    def step_qa(g, u, turn):
                        act.wait_ge(S["q"], done(g))
                        act.wait_ge(S["f"], done(g - 1))
                        act.activation(pc[:, 0], qb[:, 0:2 * P], ACT.Abs).then_inc(S["qa"], 1)

                    def step_qe(g, u, turn):
                        act.wait_ge(S["qa"], done(g))
                        act.activation(pc[:, 1], pc[:, 0], ACT.Exp, scale=-1.0).then_inc(S["qe"], 1)

                    def step_ql(g, u, turn):
                        act.wait_ge(S["qe"], done(g))
                        act.activation(pc[:, 0], pc[:, 1], ACT.Ln, bias=half_col[:], scale=0.5).then_inc(S["ql"], 1)

                    each_group_staged(act, NG, (2, step_ya), (0, step_xtc), (2, step_ye), (0, step_sq),
                                      (2, step_yl), (1, step_aggs), (0, step_lnv), (2, step_stc), (0, step_r0),
                                      (2, step_qa), (2, step_qe), (2, step_ql))

                @block.vector
                def _(dve):
                    zv = zb[:, 0:GROUP * (D + 1)].rearrange("p (t d) -> p t d", d=D + 1)
                    y0, y1 = [y[:, n].rearrange("p (t d) -> p t d", d=D) for n in range(2)]
                    dve.memset(msg[:], 1.0)
                    dve.memset(carry[:], 0.0).then_inc(s_link, 1)
                    dve.wait_ge(s_link, 1)

                    def step_seg(g, u, turn):
                        cols = bass.ds(g * GROUP, GROUP)
                        dve.wait_ge(s_rows[u], 16 * (turn + 1))
                        dve.wait_ge(S["agg"], freed(g))
                        dve.tensor_tensor(seg[:, u], rows[:, u].rearrange("p (t i) -> p t i", i=P),
                                          dst_f[:, cols].unsqueeze(2).broadcast_to([P, GROUP, P]),
                                          ALU.is_equal).then_inc(S["seg"], 1)

                    def step_var(g, u, turn):
                        dve.wait_ge(S["sq"], done(g))
                        dve.wait_ge(S["rs"], done(g - 1))
                        dve.tensor_reduce(var[:], sq[:].rearrange("p (t d) -> p t d", d=D), AX_X,
                                          ALU.add).then_inc(S["var"], 1)

                    def step_r1(g, u, turn):
                        dve.wait_ge(S["r0"], done(g))
                        dve.scalar_tensor_tensor(rs[:, 1], var[:], EPS, rs[:, 0], ALU.add, ALU.mult).then_inc(S["r1"], 1)

                    def step_r2(g, u, turn):
                        dve.wait_ge(S["r1"], done(g))
                        dve.scalar_tensor_tensor(rs[:, 2], rs[:, 1], -0.5, rs[:, 0], ALU.mult,
                                                 ALU.mult).then_inc(S["r2"], 1)

                    def step_rs(g, u, turn):
                        dve.wait_ge(S["r2"], done(g))
                        dve.wait_ge(S["xh"], done(g - 1))
                        dve.scalar_tensor_tensor(rs[:, 3], rs[:, 2], 1.5, rs[:, 0], ALU.add, ALU.mult).then_inc(S["rs"], 1)

                    def step_xh(g, u, turn):
                        dve.wait_ge(S["rs"], done(g))
                        dve.wait_ge(S["msg"], done(g - 1))
                        dve.scalar_tensor_tensor(xh[:], xb[:, 2 * P:4 * P].rearrange("p (t d) -> p t d", d=D), 0.0,
                                                 rs[:, 3].unsqueeze(2).broadcast_to([P, GROUP, D]), ALU.max,
                                                 ALU.mult).then_inc(S["xh"], 1)

                    def step_msg(g, u, turn):
                        cols = bass.ds(g * GROUP, GROUP)
                        dve.wait_ge(S["xh"], done(g))
                        dve.tensor_tensor(msg[:, u, :, 0:D], xh[:], self_slot[:, cols, :], ALU.mult).then_inc(S["msg"], 1)

                    def step_scan(g, u, turn):
                        cols = bass.ds(g * GROUP, GROUP)
                        dve.wait_ge(S["agg"], done(g))
                        dve.wait_ge(S["crT"], freed(g))
                        dve.wait_ge(S["scan"], done(g - 1))
                        dve.tensor_copy(carry[:, u, 0:1], carry[:, 1 - u, GROUP:GROUP + 1])
                        dve.tensor_tensor_scan(carry[:, u, 1:GROUP + 1], goes_on[0:D + 1, cols],
                                               agg[0:D + 1].rearrange("p (t i) -> p t i", i=P)[:, :, P - 1],
                                               carry[:, 1 - u, GROUP:GROUP + 1], ALU.mult,
                                               ALU.add).then_inc(S["scan"], 1)

                    def step_crow(g, u, turn):
                        dve.wait_ge(S["crT"], done(g))
                        dve.wait_ge(S["carried"], freed(g))
                        dve.tensor_copy(crow[:, u], zb[0:GROUP, 320:320 + D + 1]).then_inc(S["crow"], 1)

                    def step_cnt(g, u, turn):
                        dve.wait_ge(S["z"], done(g))
                        dve.tensor_scalar(cnt[:, 0], zv[:, :, D], 1.0, None, ALU.max).then_inc(S["cnt"], 1)

                    def step_rc(g, u, turn):
                        dve.wait_ge(S["cnt"], done(g))
                        dve.reciprocal(cnt[:, 1], cnt[:, 0]).then_inc(S["rc"], 1)

                    def step_y0(g, u, turn):
                        dve.wait_ge(S["rc"], done(g))
                        dve.tensor_tensor(y0, zv[:, :, 0:D], cnt[:, 1].unsqueeze(2).broadcast_to([P, GROUP, D]),
                                          ALU.mult).then_inc(S["y0"], 1)

                    def step_y1(g, u, turn):
                        dve.wait_ge(S["y0"], done(g))
                        dve.tensor_tensor(y1, y0, sb3_all[:].unsqueeze(1).broadcast_to([P, GROUP, D]),
                                          ALU.add).then_inc(S["y1"], 1)

                    def step_s1(g, u, turn):
                        dve.wait_ge(S["yl"], done(g))
                        dve.wait_ge(S["st"], done(g - 1))
                        dve.scalar_tensor_tensor(s1[:], y[:, 1], 0.0, pa[:, 0], ALU.max, ALU.add).then_inc(S["s1"], 1)

                    def step_f(g, u, turn):
                        dve.wait_ge(S["ql"], done(g))
                        dve.scalar_tensor_tensor(f[:], qb[:, 0:2 * P], 0.0, pc[:, 0], ALU.max, ALU.add).then_inc(S["f"], 1)

                    def step_res(g, u, turn):
                        dve.wait_ge(S["f"], done(g))
                        dve.wait_ge(s_sl[u], 16 * (turn + 1))
                        if not early(g):
                            dve.wait_ge(s_sc[u], 16 * GROUP * turn)
                        dve.tensor_tensor(res[:, u], f[:].rearrange("p (t d) -> p t d", d=D), x1[:, u],
                                          ALU.add).then_inc(S["res"], 1)

                    each_group_staged(dve, NG, (0, step_seg), (1, step_scan), (1, step_crow), (0, step_var),
                                      (2, step_s1), (0, step_r1), (1, step_cnt), (0, step_r2), (1, step_rc),
                                      (0, step_rs), (1, step_y0), (0, step_xh), (1, step_y1), (0, step_msg),
                                      (2, step_f), (2, step_res))


_INS = ['x', 'src', 'dst', 'edge_attr_128', 'edge_attr_64', 'L0_gnn_W1', 'L0_gnn_b1', 'L0_gnn_W2', 'L0_gnn_b2',
        'L1_gnn_W1', 'L1_gnn_b1', 'L1_gnn_W2', 'L1_gnn_b2', 'L1_gnn_W3', 'L1_gnn_b3', 'L1_gnn_W4', 'L1_gnn_b4']
_OUTS = [((100000, 64), 'float32')]


def kernel(**inputs):
    import numpy as _np
    import concourse.bacc as _bacc
    from concourse import mybir as _mybir
    from concourse.bass_utils import run_bass_kernel_spmd as _run

    nc = _bacc.Bacc("TRN2", target_bir_lowering=False, num_devices=1)
    arrays, args = {}, []
    for name in _INS:
        a = _np.ascontiguousarray(inputs[name])
        arrays[f"in_{name}_dram"] = a
        args.append(nc.dram_tensor(f"in_{name}_dram", a.shape, _mybir.dt.from_np(a.dtype), kind="ExternalInput").ap())
    for i, (shape, dtype) in enumerate(_OUTS):
        dt = _mybir.dt.from_np(_np.dtype(dtype))
        args.append(nc.dram_tensor(f"out_{i}_dram", shape, dt, kind="ExternalOutput").ap())
    gnn_kernel(nc, *args)
    r = _run(nc, [arrays], core_ids=[0])
    got = tuple(r.results[0][f"out_{i}_dram"] for i in range(len(_OUTS)))
    return got[0]
```

```python
import concourse.bass as bass
from concourse import mybir
from contextlib import ExitStack

ALU = mybir.AluOpType
ACT = mybir.ActivationFunctionType
AX_X = mybir.AxisListType.X
F32 = mybir.dt.float32
F16 = mybir.dt.float16
BF16 = mybir.dt.bfloat16
I32 = mybir.dt.int32
U32 = mybir.dt.uint32

P = 128
J = 8
BLOCK = P * J
GROUP = 4
SKIP = 131071
AROW = 67
RING = 2
EPS = 1e-5
SLOPE = 0.01


def done(g):
    return g + 1 + RING


def freed(g):
    return g + 1


def early(g, ring=RING):
    return isinstance(g, int) and g < ring


def each_group(eng, count, body, peel=0):
    for g in range(2 * peel):
        body(g, g % 2, g // 2)
    with eng.Fori(peel, count // 2) as i:
        body(2 * i, 0, i)
        body(2 * i + 1, 1, i)
    body(count - 1, 0, count // 2)


def each_group_staged(eng, count, *stages, ring=RING):
    most = max(lag for lag, _ in stages)
    first = -(-(most + ring) // ring) * ring
    last = count // ring * ring

    def peeled(i):
        for lag, step in stages:
            g = i - lag
            if 0 <= g < count:
                step(g, g % ring, g // ring)

    for i in range(first):
        peeled(i)
    with eng.Fori(first // ring, last // ring) as r:
        for s in range(ring):
            for lag, step in stages:
                k = s - lag
                step(ring * r + k, k % ring, r + k // ring)
    for i in range(last, count + most):
        peeled(i)


def gnn_kernel(nc, x, src, dst, radial, edge_h, gW1, gb1, gW2, gb2,
               sW1, sb1, sW2, sb2, sW3, sb3, sW4, sb4, out):
    N, D = x.shape
    E = src.shape[0]
    R = radial.shape[1]
    T = -(-E // P)
    SLOTS = T * P
    EL = E - (T - 1) * P
    NG = T // GROUP
    NBLK = -(-N // BLOCK)
    PL = (N - (NBLK - 1) * BLOCK) // J
    NC = NBLK * J
    HC = NC // 2
    assert T == NG * GROUP and NBLK == 2 * NG and NG % 2 == 1 and D == 64 and R == P
    assert (N - (NBLK - 1) * BLOCK) % J == 0 and HC <= 512 and N < SKIP
    PAIRS = NG // 2
    GC = GROUP * P
    TL = T - P

    B3 = 65
    EP, EC = 125, E // 125
    PIECE = 25
    assert E == EP * EC and EC % PIECE == 0

    src_sorted = nc.dram_tensor("src_sorted", [E, 1], I32, kind="Internal").ap()
    dst_sorted = nc.dram_tensor("dst_sorted", [E, 1], I32, kind="Internal").ap()
    rank_d = nc.dram_tensor("rank_d", [EP, EC], U32, kind="Internal").ap()
    w_given = nc.dram_tensor("w_given", [SLOTS, D], F32, kind="Internal").ap()
    w_sorted = nc.dram_tensor("w_sorted", [SLOTS, D], F32, kind="Internal").ap()
    dst_rows = nc.dram_tensor("dst_rows", [1, SLOTS + P], F32, kind="Internal").ap()
    x_dst = nc.dram_tensor("x_dst", [SLOTS, D], F32, kind="Internal").ap()
    table_a = nc.dram_tensor("table_a", [N, AROW], F32, kind="Internal").ap()
    carried = nc.dram_tensor("carried", [NG, GROUP, GC], F32, kind="Internal").ap()
    carried_rows = nc.dram_tensor("carried_rows", [NG, GROUP, P], F32, kind="Internal").ap()
    table_h = nc.dram_tensor("table_h", [SLOTS + NBLK * BLOCK, D], F32, kind="Internal").ap()
    table_x = nc.dram_tensor("table_x", [SLOTS + NBLK * BLOCK, D], F32, kind="Internal").ap()

    local_h, local_x = table_h[SLOTS:, :], table_x[SLOTS:, :]

    def both(t, g):
        return t[bass.ds(g * 2 * BLOCK, 2 * BLOCK), :].rearrange("(k p j) d -> p k (j d)", p=P, j=J)

    def tiles(t, g):
        return t[bass.ds(g * GC, GC), :].rearrange("(t p) d -> p t d", p=P)

    def blocks(t, b, rows=P):
        return t[bass.ds(b * BLOCK, rows * J), :].rearrange("(p j) d -> p (j d)", j=J)

    with ExitStack() as ctx:
        def sb(name, shape, dt=F32):
            return ctx.enter_context(nc.sbuf_tensor(name, shape, dt))

        def sem(name):
            return ctx.enter_context(nc.semaphore(name))

        ident = sb("ident", [P, P])
        ones = sb("ones", [P, P])
        center2 = sb("center2", [P, P])
        gW1_2 = sb("gW1_2", [P, P])
        gW2_2 = sb("gW2_2", [P, P])
        sW4_2 = sb("sW4_2", [P, P])
        gW1_a = sb("gW1_a", [D + 1, D + 1])
        sW3_a = sb("sW3_a", [D + 1, D + 1])
        gW2_s = sb("gW2_s", [D, D])
        sW1_s = sb("sW1_s", [P, D])
        sW2_s = sb("sW2_s", [D, D])
        b1_rows = sb("b1_rows", [1, J * D])
        b2_rows = sb("b2_rows", [1, J * D])
        sb2_rows = sb("sb2_rows", [1, GROUP * D])
        sb4_rows = sb("sb4_rows", [1, GROUP * D])
        b1_all = sb("b1_all", [P, D])
        b2_all = sb("b2_all", [P, D])
        sb3_all = sb("sb3_all", [P, D])
        sb1_row = sb("sb1_row", [1, D])
        b1_3 = sb("b1_3", [B3, J * D], BF16)
        b2_3 = sb("b2_3", [B3, J * D], BF16)
        sb1_3 = sb("sb1_3", [B3, D], BF16)
        sb2_3 = sb("sb2_3", [B3, GROUP * D], BF16)
        sb4_3 = sb("sb4_3", [B3, GROUP * D], BF16)
        ones_3 = sb("ones_3", [B3, GROUP * P], BF16)
        sb3_col = sb("sb3_col", [D, 1])
        rest_row = sb("rest_row", [P, D])
        eps_col = sb("eps_col", [P, 1])
        iota_lo = sb("iota_lo", [P, P], F16)
        zeros = sb("zeros", [P, HC], F16)
        half_col = sb("half_col", [P, 1])
        code_u = sb("code_u", [P, T], U32)
        io_slot = sb("io_slot", [P, T])
        ii_slot = sb("ii_slot", [P, T])
        dst_f = sb("dst_f", [P, T])
        src_u = sb("src_u", [P, T], U32)
        dst_u = sb("dst_u", [P, T], U32)
        out_u = sb("out_u", [P, T], U32)
        keep = sb("keep", [P, T])
        goes_on = sb("goes_on", [P, T])
        dst_kept = sb("dst_kept", [P, T])
        out_scale = sb("out_scale", [P, NC])
        code = sb("code", [P, NC])

        unsorted = sb("unsorted", [1, 1], I32)

        s_const = sem("s_const")
        s_w = sem("s_w")

        signals = []
        with ExitStack() as ph:
            def sb(name, shape, dt=F32):
                return ph.enter_context(nc.sbuf_tensor(f"p0_{name}", shape, dt))

            def sem(name):
                signals.append(nc.alloc_semaphore(name))
                return signals[-1]

            bank0 = ph.enter_context(nc.psum_tensor("bank0_count", [P, 512], F32))
            given = sb("given", [EP, 2, EC], I32)
            first_next = sb("first_next", [EP, 1], I32)
            dst_e = sb("dst_e", [EP, EC + 1])
            falls = sb("falls", [EP, EC])
            fall = sb("fall", [EP, 1])
            one = sb("one", [EP, 1])
            col = sb("col", [EP, EC])
            later = sb("later", [EP, EP])
            row_i = sb("row_i", [EP, EC], I32)
            row = sb("row", [EP, EC])
            dst_up = sb("dst_up", [EP, EC])
            less = sb("less", [EP, PIECE, EC], F16)
            add = sb("add", [EP, EC])
            before = sb("before", [EP, EC])
            same = sb("same", [EP, EC])
            rank = sb("rank", [EP, EC])
            rank_u = sb("rank_u", [EP, EC], U32)
            idx = sb("idx", [EP, 1], U32)
            pay = sb("pay", [EP, 2], I32)

            s_given, s_next, s_copied, s_count, s_flag = (
                sem("s0_given"), sem("s0_next"), sem("s0_copied"), sem("s0_count"), sem("s0_flag"))
            s_v, s_aid, s_row, s_row_used, s_ranked, s_rank_st = (
                sem("s0_v"), sem("s0_aid"), sem("s0_row"), sem("s0_row_used"), sem("s0_ranked"), sem("s0_rank_st"))
            s_rv, s_tie, s_staged, s_pace, s_sc = (
                sem("s0_rv"), sem("s0_tie"), sem("s0_staged"), sem("s0_pace"), sem("s0_sc"))

            with nc.Block() as block:
                @block.sync
                def _(sp):
                    sp.dma_start(given[:, 1], dst.rearrange("(p c) -> p c", c=EC)).then_inc(s_given, 16)
                    sp.wait_ge(s_v, 1)
                    sp.dma_start(first_next[0:EP - 1, :], dst.rearrange("(p c) -> p c", c=EC)[1:EP, 0:1],
                                 allow_slow_non_contiguous=True).then_inc(s_next, 16)
                    sp.dma_start(src_sorted.rearrange("(p c) o -> p (c o)", c=EC),
                                 src.rearrange("(p c) -> p c", c=EC)).then_inc(s_copied, 16)
                    sp.dma_start(dst_sorted.rearrange("(p c) o -> p (c o)", c=EC),
                                 dst.rearrange("(p c) -> p c", c=EC)).then_inc(s_copied, 16)
                    sp.wait_ge(s_copied, 32)
                    sp.wait_ge(s_flag, 1)
                    with sp.If(sp.value_load(unsorted[:]) > 0):
                        sp.dma_start(given[:, 0], src.rearrange("(p c) -> p c", c=EC)).then_inc(s_given, 16)

                        def load_row(c):
                            sp.dma_start(row_i[:], dst.rearrange("(p c) -> p c", c=EC)[bass.ds(c, 1), :].broadcast_to(
                                [EP, EC])).then_inc(s_row, 16)

                        load_row(0)
                        with sp.Fori(1, EP) as c:
                            sp.wait_ge(s_row_used, c)
                            load_row(c)
                        sp.wait_ge(s_ranked, 1)
                        sp.dma_start(rank_d, rank_u[:]).then_inc(s_rank_st, 16)
                        sp.wait_ge(s_rank_st, 16)
                        sp.wait_ge(s_sc, 32 * EC)

                @block.gpsimd
                def _(pool):
                    pool.wait_ge(s_flag, 1)
                    with pool.If(pool.value_load(unsorted[:]) > 0):
                        max_edge = pool.to_reg(E - 1)
                        pool.iota(col[:], pattern=[[1, EC]], base=0, channel_multiplier=0,
                                  allow_small_or_imprecise_dtypes=True).then_inc(s_aid, 1)
                        pool.memset(later[:], 0.5).then_inc(s_aid, 1)
                        pool.wait_ge(s_aid, 2)
                        pool.affine_select(later[:], later[:], pattern=[[-1, EP]], compare_op=ALU.is_gt, fill=0.0,
                                           base=0, channel_multiplier=1).then_inc(s_aid, 1)
                        pool.wait_ge(s_given, 32)
                        pool.wait_ge(s_copied, 32)
                        pool.wait_ge(s_ranked, 1)
                        with pool.Fori(0, EC) as t:
                            pool.tensor_copy(idx[:], rank_u[:, bass.ds(t, 1)]).then_inc(s_staged, 1)
                            pool.tensor_copy(pay[:, 0:1], given[:, 0, bass.ds(t, 1)]).then_inc(s_staged, 1)
                            pool.tensor_copy(pay[:, 1:2], given[:, 1, bass.ds(t, 1)]).then_inc(s_staged, 1)
                            pool.wait_ge(s_staged, 3 * t + 3)
                            pool.sem_inc(s_pace, 1)
                            for a, to in enumerate((src_sorted, dst_sorted)):
                                pool.indirect_dma_start(
                                    to, bass.IndirectOffsetOnAxis(ap=idx[:], axis=0), pay[:, a:a + 1], None,
                                    bounds_check=max_edge, oob_is_err=False).then_inc(s_sc, 16)
                            pool.wait_ge(s_sc, 32 * t + 32)

                @block.tensor
                def _(pe):
                    pe.wait_ge(s_count, 1)
                    pe.matmul(bank0[0:1, 0:1], fall[:], one[:], start=True, stop=True).then_inc(s_count, 1)

                @block.vector
                def _(dve):
                    dve.memset(first_next[:], N).then_inc(s_v, 1)
                    dve.memset(one[:], 1.0)
                    dve.wait_ge(s_given, 16)
                    dve.tensor_copy(dst_e[:, 0:EC], given[:, 1])
                    dve.wait_ge(s_next, 16)
                    dve.tensor_copy(dst_e[:, EC:EC + 1], first_next[:]).then_inc(s_v, 1)
                    dve.wait_ge(s_v, 2)
                    dve.tensor_tensor(falls[:], dst_e[:, 1:EC + 1], dst_e[:, 0:EC], ALU.is_lt).then_inc(s_v, 1)
                    dve.wait_ge(s_v, 3)
                    dve.tensor_reduce(fall[:], falls[:], AX_X, ALU.add).then_inc(s_count, 1)
                    dve.wait_ge(s_count, 2)
                    dve.tensor_copy(unsorted[:], bank0[0:1, 0:1]).then_inc(s_flag, 1)
                    dve.wait_ge(s_flag, 1)
                    with dve.If(dve.value_load(unsorted[:]) > 0):
                        dve.wait_ge(s_aid, 3)
                        with dve.Fori(0, EC) as t:
                            dve.tensor_scalar(before[:], col[:], col[:, bass.ds(t, 1)], None,
                                              ALU.is_lt).then_inc(s_tie, 1)
                            dve.wait_ge(s_tie, 3 * t + 1)
                            dve.scalar_tensor_tensor(same[:], dst_e[:, 0:EC], dst_e[:, bass.ds(t, 1)], before[:],
                                                     ALU.is_equal, ALU.mult).then_inc(s_tie, 1)
                            dve.wait_ge(s_tie, 3 * t + 2)
                            dve.tensor_reduce(rank[:, bass.ds(t, 1)], same[:], AX_X, ALU.add).then_inc(s_tie, 1)
                            dve.wait_ge(s_tie, 3 * t + 3)
                        steps = 2 * (EC // PIECE) + 2
                        with dve.Fori(0, EP) as c:
                            dve.wait_ge(s_row, 16 * c + 16)
                            dve.tensor_copy(row[:], row_i[:]).then_inc(s_row_used, 1)
                            dve.wait_ge(s_row_used, c + 1)
                            dve.tensor_scalar(dst_up[:], dst_e[:, 0:EC], later[:, bass.ds(c, 1)], None,
                                              ALU.add).then_inc(s_rv, 1)
                            dve.wait_ge(s_rv, steps * c + 1)
                            for k in range(EC // PIECE):
                                cols = slice(k * PIECE, (k + 1) * PIECE)
                                dve.tensor_tensor(less[:], row[:].unsqueeze(1).broadcast_to([EP, PIECE, EC]),
                                                  dst_up[:, cols].unsqueeze(2).broadcast_to([EP, PIECE, EC]),
                                                  ALU.is_lt).then_inc(s_rv, 1)
                                dve.wait_ge(s_rv, steps * c + 2 + 2 * k)
                                dve.tensor_reduce(add[:, cols], less[:], AX_X, ALU.add).then_inc(s_rv, 1)
                                dve.wait_ge(s_rv, steps * c + 3 + 2 * k)
                            dve.tensor_tensor(rank[:], rank[:], add[:], ALU.add).then_inc(s_rv, 1)
                            dve.wait_ge(s_rv, steps * c + steps)
                        dve.tensor_copy(rank_u[:], rank[:]).then_inc(s_ranked, 1)

        nc.clear_and_free_semaphores(signals)
        nc.all_engine_barrier()


        signals = []
        with ExitStack() as ph:
            def sb(name, shape, dt=F32):
                return ph.enter_context(nc.sbuf_tensor(f"p1_{name}", shape, dt))

            def sem(name):
                signals.append(nc.alloc_semaphore(name))
                return signals[-1]

            s_padded, s_raw, s_rowf, s_rows, s_next = (
                sem("s_padded"), sem("s_raw"), sem("s_rowf"), sem("s_rows"), sem("s_next"))
            s_turned, s_slots, s_last, s_idx, s_chain, s_chain2 = (
                sem("s_turned"), sem("s_slots"), sem("s_last"), sem("s_idx"), sem("s_chain"), sem("s_chain2"))
            s_hot, s_hist, s_hist_end = sem("s_hot"), sem("s_hist"), sem("s_hist_end")
            s_neg, s_away, s_hot_lo = sem("s_neg"), sem("s_away"), sem("s_hot_lo")
            s_pp, s_pre, s_root, s_extra = sem("s_pp"), sem("s_pre"), sem("s_root"), sem("s_extra")
            s_staged = sem("s_staged")
            s_prev, s_carr, s_carz, s_carw, s_carc = (
                sem("s_prev"), sem("s_carr"), sem("s_carz"), sem("s_carw"), sem("s_carc"))
            s_rest_a, s_rest_v, s_rest_p = sem("s_rest_a"), sem("s_rest_v"), sem("s_rest_p")

            iota_hi = sb("iota_hi", [P, NC], F16)
            before = sb("before", [P, P])
            last_row = sb("last_row", [P, P])
            src_f = sb("src_f", [P, T])
            next_f = sb("next_f", [P, T])
            part_r = sb("part_r", [1, J * D])
            part_s = sb("part_s", [1, J * D])
            part_b = sb("part_b", [1, J * D], BF16)
            src_lo = sb("src_lo", [P, T])
            src_hi = sb("src_hi", [P, T])
            neg_lo = sb("neg_lo", [P, T])
            away = sb("away", [P, GROUP, P], F16)
            one_col = sb("one_col", [P, 1])
            dst_hi = sb("dst_hi", [P, T])
            dst_last = sb("dst_last", [P, T + 1])
            prev_col = sb("prev_col", [P, 2])
            carr = sb("carr", [P, 2, P])
            rest = sb("rest", [P, 4, D])
            rest_lhs = sb("rest_lhs", [D, P])
            raw = sb("raw", [P, 2, 2, P], I32)
            rowf = sb("rowf", [P, 2, 2, P])
            rown = sb("rown", [P, 2, P])
            bits = sb("bits", [P, 2, T], I32)
            bits_lo = sb("bits_lo", [P, 2, T], I32)
            bits_hi = sb("bits_hi", [P, 2, T], I32)
            bits_j = sb("bits_j", [P, 2, T], I32)
            hot_lo = sb("hot_lo", [P, GROUP, 2, P], F16)
            hot_hi = sb("hot_hi", [P, GROUP, 2, NC], F16)
            DEEP_X = 4
            idx = sb("idx", [P, DEEP_X, GROUP], U32)
            xg = sb("xg", [P, DEEP_X, GROUP, D])
            s_xg = [sem(f"s_xg{u}") for u in range(DEEP_X)]
            s_xs = [sem(f"s_xs{u}") for u in range(DEEP_X)]
            s_pace = sem("s_pace")
            in_cnt = sb("in_cnt", [P, NC])
            ends = sb("ends", [P, NC])
            nodes = sb("nodes", [P, NC])
            per_p = sb("per_p", [P, NBLK])
            base = sb("base", [P, NBLK])
            upto = sb("upto", [P, NBLK + 1])
            sq = sb("sq", [P, RING, 2, J * D])
            bank = [ph.enter_context(nc.psum_tensor(f"bank1_{k}", [P, 512], F32)) for k in range(8)]

            with nc.Block() as block:
                @block.sync
                def _(sp):
                    sp.sem_inc(s_hist, GROUP)
                    sp.wait_ge(s_padded, 1)
                    for a, v in enumerate((src_sorted[:, 0], dst_sorted[:, 0])):
                        sp.dma_start(raw[:, a, 0, :], v[0:P * P].rearrange("(t p) -> t p", p=P)).then_inc(s_raw, 16)
                        sp.dma_start(raw[0:TL - 1, a, 1, :],
                                     v[P * P:(T - 1) * P].rearrange("(t p) -> t p", p=P)).then_inc(s_raw, 16)
                        sp.dma_start(raw[TL - 1:TL, a, 1, 0:EL],
                                     v[(T - 1) * P:E].rearrange("(t p) -> t p", t=1)).then_inc(s_raw, 16)
                    sp.wait_ge(s_rowf, 1)
                    r = dst_rows[0]
                    sp.dma_start(r[0:P * P].rearrange("(t p) -> t p", p=P), rowf[:, 1, 0, :]).then_inc(s_rows, 16)
                    sp.dma_start(r[P * P:SLOTS + P].rearrange("(t p) -> t p", p=P),
                                 rowf[0:TL + 1, 1, 1, :]).then_inc(s_rows, 16)
                    sp.wait_ge(s_rows, 32)
                    sp.dma_start(rown[:, 0, :], r[1:P * P + 1].rearrange("(t p) -> t p", p=P)).then_inc(s_next, 16)
                    sp.dma_start(rown[0:TL, 1, :],
                                 r[P * P + 1:SLOTS + 1].rearrange("(t p) -> t p", p=P)).then_inc(s_next, 16)
                    sp.dma_start(prev_col[1:P, 0:1], r[0:P * P].rearrange("(t p) -> t p", p=P)[0:P - 1, P - 1:P],
                                 allow_slow_non_contiguous=True).then_inc(s_prev, 16)
                    sp.dma_start(prev_col[0:TL, 1:2],
                                 r[(P - 1) * P:(T - 1) * P].rearrange("(t p) -> t p", p=P)[:, P - 1:P],
                                 allow_slow_non_contiguous=True).then_inc(s_prev, 16)
                    sp.dma_start(carried.rearrange("g t c -> (g t) c").rearrange("(p a) c -> p a c", a=2),
                                 sq[0:T // 2, 0]).then_inc(s_carz, 16)
                    sp.wait_ge(s_const, 2)
                    loads = 0
                    for to, w in ((gW1_2[0:D, 0:D], gW1), (gW1_2[D:P, D:P], gW1), (gW2_2[0:D, 0:D], gW2),
                                  (gW2_2[D:P, D:P], gW2), (sW4_2[0:D, 0:D], sW4), (sW4_2[D:P, D:P], sW4),
                                  (gW1_a[0:D, 0:D], gW1), (sW3_a[0:D, 0:D], sW3), (gW2_s[:], gW2),
                                  (sW1_s[:], sW1), (sW2_s[:], sW2)):
                        sp.dma_start(to, w).then_inc(s_w, 16)
                        loads += 1
                    for row, b, n in ((b1_rows, gb1, J), (b2_rows, gb2, J), (sb1_row, sb1, 1), (sb2_rows, sb2, GROUP),
                                      (sb4_rows, sb4, GROUP)):
                        sp.dma_start(row[:].rearrange("o (n d) -> o n d", d=D),
                                     b.rearrange("(o n d) -> o n d", o=1,
                                                 n=1).broadcast_to([1, n, D])).then_inc(s_w, 16)
                        loads += 1
                    for full, b in ((b1_all, gb1), (b2_all, gb2), (sb3_all, sb3)):
                        sp.dma_start(full[:], b.rearrange("(o d) -> o d", o=1).broadcast_to([P, D])).then_inc(s_w, 16)
                        loads += 1
                    sp.dma_start(sb3_col[:], sb3.rearrange("(d o) -> d o", o=1),
                                 allow_slow_non_contiguous=True).then_inc(s_w, 16)
                    loads += 1

                    def store(g, u, turn):
                        sp.wait_ge(s_xg[u], 16 * GROUP * (turn + 1))
                        sp.dma_start(tiles(x_dst, g), xg[:, u]).then_inc(s_xs[u], 16)

                    each_group_staged(sp, NG, (0, store), ring=DEEP_X)

                    sp.wait_ge(s_carr, 1)
                    flat = carried_rows.rearrange("g t p -> (g t) p")
                    sp.dma_start(flat[0:P, :], carr[:, 0, :]).then_inc(s_carw, 16)
                    sp.dma_start(flat[P:T, :], carr[0:TL, 1, :]).then_inc(s_carw, 16)
                    sp.wait_ge(s_carw, 32)
                    sp.wait_ge(s_carz, 16)
                    for t in range(GROUP):
                        sp.dma_start(carried[:, t, t * P:(t + 1) * P], carried_rows[:, t, :]).then_inc(s_carc, 16)

                    sp.wait_ge(s_w, 16 * loads)
                    sp.wait_ge(s_carc, 16 * GROUP)
                    for u in range(DEEP_X):
                        sp.wait_ge(s_xs[u], 16 * len(range(u, NG, DEEP_X)))

                @block.gpsimd
                def _(pool):
                    pool.memset(ident[:], 0.0)
                    pool.memset(before[:], 0.0)
                    pool.memset(last_row[:], 0.0)
                    pool.memset(ones[:], 1.0)
                    pool.iota(iota_hi[:], pattern=[[1, NC]], base=0, channel_multiplier=0,
                              allow_small_or_imprecise_dtypes=True)
                    pool.iota(iota_lo[:], pattern=[[1, P]], base=0, channel_multiplier=0,
                              allow_small_or_imprecise_dtypes=True)
                    pool.iota(nodes[:].rearrange("p (b j) -> p b j", j=J), pattern=[[BLOCK, NBLK], [1, J]],
                              base=SLOTS, channel_multiplier=J,
                              allow_small_or_imprecise_dtypes=True).then_inc(s_chain, 1)
                    pool.wait_ge(s_chain, 1)
                    pool.affine_select(out=ident[:], in_=ident[:], compare_op=ALU.not_equal, fill=1.0, base=0,
                                       pattern=[[-1, P]], channel_multiplier=1)
                    pool.affine_select(out=before[:], in_=before[:], compare_op=ALU.is_ge, fill=1.0, base=0,
                                       pattern=[[-1, P]], channel_multiplier=1)
                    pool.affine_select(out=last_row[:], in_=last_row[:], compare_op=ALU.not_equal, fill=1.0,
                                       base=-(P - 1), pattern=[[0, P]], channel_multiplier=1).then_inc(s_const, 1)

                    max_node = pool.to_reg(N - 1)
                    pool.wait_ge(s_idx, 1)

                    def gather(g, u, turn):
                        if not early(g, DEEP_X):
                            pool.wait_ge(s_xs[u], 16 * turn)
                        pool.tensor_copy(idx[:, u, :], dst_u[:, bass.ds(g * GROUP, GROUP)]).then_inc(s_staged, 1)
                        pool.wait_ge(s_staged, g + 1)
                        pool.sem_inc(s_pace, 1)
                        for t in range(GROUP):
                            pool.indirect_dma_start(
                                xg[:, u, t, :], None, x, bass.IndirectOffsetOnAxis(ap=idx[:, u, t:t + 1], axis=0),
                                bounds_check=max_node, oob_is_err=False).then_inc(s_xg[u], 16)

                    each_group_staged(pool, NG, (0, gather), ring=DEEP_X)

                @block.tensor
                def _(pe):
                    pe.wait_ge(s_const, 2)
                    pe.wait_ge(s_rowf, 1)
                    for a in range(2):
                        pe.transpose(bank[4 + a][:, 0:P], rowf[:, a, 0, :], ident[:])
                        last = pe.transpose(bank[4 + a][:, P:T], rowf[0:TL, a, 1, :], ident[0:TL, 0:TL])
                    last.then_inc(s_turned, 1)
                    pe.wait_ge(s_next, 32)
                    pe.wait_ge(s_const, 2)
                    pe.transpose(bank[6][:, 0:P], rown[:, 0, :], ident[:])
                    pe.transpose(bank[6][:, P:T], rown[0:TL, 1, :], ident[0:TL, 0:TL]).then_inc(s_turned, 1)
                    pe.wait_ge(s_slots, 1)
                    pe.matmul(bank[7][:, 0:T], last_row[:], dst_f[:], start=True, stop=True).then_inc(s_last, 1)
                    for b in range(4):
                        pe.matmul(bank[b][:, 0:HC], zeros[:, 0:P], zeros[:], start=True, stop=False)
                    with pe.Fori(0, NG) as i:
                        for t in range(GROUP):
                            pe.wait_ge(s_hot, GROUP * i + t + 1)
                            pe.wait_ge(s_hot_lo, GROUP * i + t + 1)
                            for b in range(4):
                                last = pe.matmul(bank[b][:, 0:HC], hot_lo[:, t, b // 2, :],
                                                 hot_hi[:, t, b // 2, (b % 2) * HC:(b % 2 + 1) * HC],
                                                 start=False, stop=False)
                            last.then_inc(s_hist, 1)
                    for b in range(4):
                        last = pe.matmul(bank[b][:, 0:HC], zeros[:, 0:P], zeros[:], start=False, stop=True)
                    last.then_inc(s_hist_end, 1)
                    pe.wait_ge(s_pp, 1)
                    pe.matmul(bank[4][:, 0:NBLK], before[:], per_p[:], start=True, stop=True)
                    pe.matmul(bank[5][:, 0:NBLK], ones[:], per_p[:], start=True, stop=True).then_inc(s_pre, 1)
                    pe.wait_ge(s_rest_v, 1)
                    pe.matmul(bank[6][:, 0:D], rest_lhs[:], sW4_2[0:D, 0:D], start=True, stop=False)
                    pe.matmul(bank[6][:, 0:D], ones[0:1, :], sb4_rows[:, 0:D], start=False,
                              stop=True).then_inc(s_rest_p, 1)

                @block.scalar
                def _(act):
                    act.preload_act_table_set("natural_log_exp_and_others")
                    act.wait_ge(s_const, 2)
                    act.wait_ge(s_neg, 1)
                    with act.Fori(0, NG) as i:
                        for t in range(GROUP):
                            n = GROUP * i + t
                            act.wait_ge(s_hist, n + 1)
                            act.activation(away[:, t], iota_lo[:], ACT.Abs,
                                           bias=neg_lo[:, bass.ds(n, 1)]).then_inc(s_away, 1)
                            act.wait_ge(s_away, n + 1)
                            act.activation(hot_lo[:, t, 0], away[:, t], ACT.Relu, scale=-1.0,
                                           bias=one_col[:]).then_inc(s_hot_lo, 1)
                    act.wait_ge(s_hist_end, 1)
                    for b in range(2):
                        last = act.activation(ends[:, b * HC:(b + 1) * HC], bank[2 + b][:, 0:HC], ACT.Sqrt, bias=1.0)
                    last.then_inc(s_root, 1)
                    act.wait_ge(s_w, 16 * 20)
                    act.wait_ge(s_const, 2)

                    def half_softplus(y, r, n):
                        act.activation(r[0], y, ACT.Abs).then_inc(s_rest_a, 1)
                        act.wait_ge(s_rest_a, n + 1)
                        act.activation(r[1], r[0], ACT.Exp, scale=-1.0).then_inc(s_rest_a, 1)
                        act.wait_ge(s_rest_a, n + 2)
                        act.activation(r[0], r[1], ACT.Ln, bias=half_col[0:r[0].shape[0], :],
                                       scale=0.5).then_inc(s_rest_a, 1)

                    half_softplus(sb3_col[:], (rest[0:D, 0, 0:1], rest[0:D, 1, 0:1]), 0)
                    act.wait_ge(s_rest_p, 1)
                    half_softplus(bank[6][:, 0:D], (rest[:, 2, :], rest[:, 3, :]), 3)

                @block.vector
                def _(dve):
                    links = [0]

                    def link(ins):
                        links[0] += 1
                        ins.then_inc(s_chain2, 1)
                        dve.wait_ge(s_chain2, links[0])

                    dve.memset(raw[:], SKIP).then_inc(s_padded, 1)
                    for z in (gW1_2, gW2_2, sW4_2, gW1_a, sW3_a, center2):
                        dve.memset(z[:], 0.0)
                    dve.memset(sq[:], 0.0)
                    dve.memset(prev_col[:], -1.0)
                    dve.memset(half_col[:], 0.5)
                    dve.memset(one_col[:], 1.0)
                    dve.memset(upto[:, 0:1], 0.0)
                    dve.memset(eps_col[:], EPS)
                    dve.memset(ones_3[:], 1.0)
                    for parts in (b1_3, b2_3, sb1_3, sb2_3, sb4_3):
                        dve.memset(parts[:], 0.0)
                    link(dve.memset(zeros[:], 0.0))
                    dve.memset(gW1_a[D:D + 1, D:D + 1], 1.0)
                    dve.memset(sW3_a[D:D + 1, D:D + 1], 1.0)
                    dve.memset(center2[0:D, 0:D], -1.0 / D)
                    dve.memset(dst_last[:, 0:1], -1.0)
                    link(dve.memset(center2[D:P, D:P], -1.0 / D))
                    dve.wait_ge(s_const, 1)
                    dve.tensor_tensor(center2[:], center2[:], ident[:], ALU.add).then_inc(s_const, 1)
                    dve.wait_ge(s_raw, 96)
                    dve.tensor_copy(rowf[:], raw[:]).then_inc(s_rowf, 1)
                    dve.wait_ge(s_turned, 1)
                    dve.tensor_copy(src_f[:], bank[4][:, 0:T])
                    dve.tensor_copy(dst_f[:], bank[5][:, 0:T]).then_inc(s_slots, 1)
                    dve.wait_ge(s_slots, 1)
                    link(dve.tensor_copy(dst_u[:], dst_f[:]))
                    dve.tensor_copy(src_u[:], src_f[:]).then_inc(s_idx, 1)
                    link(dve.tensor_tensor(keep[:], src_f[:], dst_f[:], ALU.not_equal))
                    link(dve.scalar_tensor_tensor(dst_kept[:], dst_f[:], 1.0, keep[:], ALU.add, ALU.mult))
                    dve.tensor_scalar(dst_kept[:], dst_kept[:], -1.0, None, ALU.add)
                    dve.tensor_copy(bits[:, 0, :], src_f[:])
                    link(dve.tensor_copy(bits[:, 1, :], dst_f[:]))
                    dve.tensor_scalar(bits_lo[:], bits[:], 3, P - 1, ALU.logical_shift_right, ALU.bitwise_and)
                    dve.tensor_scalar(bits_hi[:], bits[:], 10, 3, ALU.logical_shift_right, ALU.logical_shift_left)
                    link(dve.tensor_scalar(bits_j[:], bits[:], J - 1, None, ALU.bitwise_and))
                    link(dve.tensor_tensor(bits_hi[:], bits_hi[:], bits_j[:], ALU.bitwise_or))
                    dve.tensor_copy(src_lo[:], bits_lo[:, 0, :])
                    dve.tensor_scalar(neg_lo[:], bits_lo[:, 1, :], -1.0, None, ALU.mult).then_inc(s_neg, 1)
                    dve.tensor_copy(src_hi[:], bits_hi[:, 0, :])
                    link(dve.tensor_copy(dst_hi[:], bits_hi[:, 1, :]))
                    with dve.Fori(0, NG) as i:
                        for t in range(GROUP):
                            n = GROUP * i + t
                            dve.wait_ge(s_hist, n + 1)
                            dve.tensor_scalar(hot_lo[:, t, 1, :], iota_lo[:], src_lo[:, bass.ds(n, 1)],
                                              keep[:, bass.ds(n, 1)], ALU.is_equal, ALU.mult)
                            dve.tensor_scalar(hot_hi[:, t, 0, :], iota_hi[:], dst_hi[:, bass.ds(n, 1)], None,
                                              ALU.is_equal)
                            dve.tensor_scalar(hot_hi[:, t, 1, :], iota_hi[:], src_hi[:, bass.ds(n, 1)], None,
                                              ALU.is_equal).then_inc(s_hot, 1)
                    dve.wait_ge(s_hist_end, 1)
                    for b in range(2):
                        half = slice(b * HC, (b + 1) * HC)
                        link(dve.tensor_copy(in_cnt[:, half], bank[b][:, 0:HC]))
                    dve.wait_ge(s_root, 1)
                    link(dve.reciprocal(out_scale[:], ends[:]))
                    dve.tensor_reduce(per_p[:], in_cnt[:].rearrange("p (b j) -> p b j", j=J), AX_X,
                                      ALU.add).then_inc(s_pp, 1)
                    dve.wait_ge(s_pre, 1)
                    link(dve.tensor_tensor_scan(upto[:, 1:NBLK + 1], ones[:, 0:NBLK], bank[5][:, 0:NBLK], 0.0,
                                                ALU.mult, ALU.add))
                    link(dve.tensor_tensor(base[:], bank[4][:, 0:NBLK], upto[:, 0:NBLK], ALU.add))
                    ends_v = ends[:].rearrange("p (b j) -> p b j", j=J)
                    cnt_v = in_cnt[:].rearrange("p (b j) -> p b j", j=J)
                    for j in range(J):
                        link(dve.tensor_tensor(ends_v[:, :, j], cnt_v[:, :, j],
                                               base[:] if j == 0 else ends_v[:, :, j - 1], ALU.add))
                    link(dve.scalar_tensor_tensor(ends[:], ends[:], -1.0, nodes[:], ALU.add, ALU.subtract))
                    link(dve.scalar_tensor_tensor(ends[:], in_cnt[:], 0.0, ends[:], ALU.is_gt, ALU.mult))
                    dve.tensor_tensor(code[:], ends[:], nodes[:], ALU.add).then_inc(s_extra, 1)
                    dve.wait_ge(s_extra, 1)
                    dve.wait_ge(s_last, 1)
                    link(dve.tensor_copy(dst_last[:, 1:T + 1], bank[7][:, 0:T]))
                    dve.tensor_tensor(goes_on[:], dst_last[:, 1:T + 1], dst_last[:, 0:T], ALU.is_equal)
                    dve.wait_ge(s_prev, 32)
                    dve.tensor_scalar(carr[:, 0, :], rowf[:, 1, 0, :], prev_col[:, 0:1], None, ALU.is_equal)
                    dve.tensor_scalar(carr[0:TL, 1, :], rowf[0:TL, 1, 1, :], prev_col[0:TL, 1:2], None,
                                      ALU.is_equal).then_inc(s_carr, 1)
                    dve.wait_ge(s_turned, 2)
                    link(dve.tensor_tensor(next_f[:], bank[6][:, 0:T], dst_f[:], ALU.is_equal))
                    link(dve.scalar_tensor_tensor(next_f[:], next_f[:], float(SKIP), dst_f[:], ALU.mult, ALU.add))
                    link(dve.tensor_copy(out_u[:], next_f[:]))
                    dve.wait_ge(s_w, 16 * 20)
                    for b, parts in ((b1_rows, b1_3), (b2_rows, b2_3), (sb1_row, sb1_3), (sb2_rows, sb2_3),
                                     (sb4_rows, sb4_3)):
                        n = b.shape[1]
                        link(dve.tensor_copy(parts[0:1, :], b[:]))
                        link(dve.tensor_tensor(part_r[:, 0:n], b[:], parts[0:1, :], ALU.subtract))
                        link(dve.tensor_copy(part_b[:, 0:n], part_r[:, 0:n]))
                        dve.tensor_copy(parts[32:33, :], part_r[:, 0:n])
                        link(dve.tensor_tensor(part_s[:, 0:n], part_r[:, 0:n], part_b[:, 0:n], ALU.subtract))
                        link(dve.tensor_copy(parts[64:65, :], part_s[:, 0:n]))
                    dve.wait_ge(s_rest_a, 3)
                    link(dve.scalar_tensor_tensor(rest[0:D, 1, 0:1], sb3_col[:], 0.0, rest[0:D, 0, 0:1], ALU.max,
                                                  ALU.add))
                    dve.tensor_scalar(rest_lhs[:], ones[0:D, :], rest[0:D, 1, 0:1], None,
                                      ALU.mult).then_inc(s_rest_v, 1)
                    dve.wait_ge(s_rest_a, 6)
                    dve.scalar_tensor_tensor(rest_row[:], bank[6][:, 0:D], 0.0, rest[:, 2, :], ALU.max, ALU.add)

        nc.clear_and_free_semaphores(signals)
        nc.all_engine_barrier()


        DEEP = 6
        signals = []
        with ExitStack() as ph:
            def sb(name, shape, dt=F32):
                return ph.enter_context(nc.sbuf_tensor(f"pn_{name}", shape, dt))

            def sem(name):
                signals.append(nc.alloc_semaphore(name))
                return signals[-1]

            xb, cb, tb, zbk = [[ph.enter_context(nc.psum_tensor(f"bankn_{n}{k}", [P, 512], F32)) for k in range(2)]
                               for n in ("x", "c", "t", "z")]
            xin = sb("xin", [P, DEEP, 2, J * D])
            arow = sb("arow", [P, DEEP, 2, J, AROW])
            h1 = sb("h1", [P, DEEP, 2, J * D])
            x1 = sb("x1", [P, DEEP, 2, J * D])
            res = sb("res", [P, DEEP, 2, J * D])
            xT = sb("xT", [P, 2, 4 * P])
            sq = sb("sq", [P, 2, J * D])
            var = sb("var", [P, 2 * J])
            sd = sb("sd", [P, 2 * J])
            rs = sb("rs", [P, 2 * J])
            rsio = sb("rsio", [P, 2 * J])
            hs = sb("hs", [P, RING, 2, J * D])
            hsT = sb("hsT", [P, 2, 4 * P])
            h1T = sb("h1T", [P, 2, 4 * P])
            h2 = sb("h2", [P, RING, 2, J * D])

            s_x = [sem(f"sn_in{u}") for u in range(DEEP)]
            s_sta = [sem(f"sn_sta{u}") for u in range(DEEP)]
            s_sth = [sem(f"sn_sth{u}") for u in range(DEEP)]
            s_stx = [sem(f"sn_stx{u}") for u in range(DEEP)]
            s_sto = [sem(f"sn_sto{u}") for u in range(DEEP)]
            s_paced, s_ones = sem("sn_paced"), sem("sn_ones")
            S = {n: sem("sn_" + n) for n in (
                "xt", "xtc", "cen", "sq", "var", "sd", "rs", "rsio", "hs", "codes", "arow",
                "t1", "t1c", "w1a", "w1", "y", "h1a", "h1", "t2a", "t2", "t2ca", "t2c",
                "w2a", "w2", "rela", "rel", "h2", "x1", "res")}

            def heads(buf, u, k):
                return buf[:, u, k].rearrange("p (j d) -> p j d", d=D)

            def lens(g):
                return (0, P), (1, PL if isinstance(g, int) and g == NG - 1 else P)

            with nc.Block() as block:
                @block.sync
                def _(sp):
                    for s in S.values():
                        sp.sem_inc(s, RING)

                    def fetch_x(g, u, turn):
                        if not early(g, DEEP):
                            sp.wait_ge(S["x1"], done(g - DEEP))
                        for k, n in lens(g):
                            sp.dma_start(xin[0:n, u, k], blocks(x, 2 * g + k, n)).then_inc(s_x[u], 16)

                    def store_a(g, u, turn):
                        sp.wait_ge(S["arow"], done(g))
                        sp.sem_inc(s_paced, 1)
                        for k, n in lens(g):
                            sp.dma_start(blocks(table_a, 2 * g + k, n),
                                         arow[0:n, u, k].rearrange("p j d -> p (j d)")).then_inc(s_sta[u], 16)

                    def store_h(g, u, turn):
                        sp.wait_ge(S["h1"], done(g))
                        sp.sem_inc(s_paced, 1)
                        sp.dma_start(both(local_h, g), h1[:, u]).then_inc(s_sth[u], 16)

                    def store_x(g, u, turn):
                        sp.wait_ge(S["res"], done(g))
                        sp.sem_inc(s_paced, 1)
                        sp.dma_start(both(local_x, g), x1[:, u]).then_inc(s_stx[u], 16)
                        if isinstance(g, int) and g == NG - 1:
                            sp.dma_start(blocks(out, 2 * g, P), res[:, u, 0]).then_inc(s_sto[u], 16)
                            sp.dma_start(blocks(out, 2 * g + 1, PL), res[0:PL, u, 1]).then_inc(s_sto[u], 16)
                        else:
                            sp.dma_start(both(out, g), res[:, u]).then_inc(s_sto[u], 16)

                    each_group_staged(sp, NG, (0, fetch_x), (6, store_h), (7, store_a), (7, store_x), ring=DEEP)
                    for u in range(DEEP):
                        n = len(range(u, NG, DEEP))
                        sp.wait_ge(s_sta[u], 32 * n)
                        sp.wait_ge(s_sth[u], 16 * n)
                        sp.wait_ge(s_stx[u], 16 * n)
                        sp.wait_ge(s_sto[u], 16 * n + (16 if (NG - 1) % DEEP == u else 0))

                @block.gpsimd
                def _(pool):
                    pool.memset(arow[:, :, :, :, D:D + 1], 1.0).then_inc(s_ones, 1)
                    pool.wait_ge(s_ones, 1)

                    def step_codes(g, u, turn):
                        if not early(g, DEEP):
                            pool.wait_ge(s_sta[u], 32 * turn)
                        pool.tensor_copy(arow[:, u, :, :, D + 1].rearrange("p k j -> p (k j)"),
                                         code[:, bass.ds(g * 2 * J, 2 * J)])
                        pool.tensor_copy(arow[:, u, :, :, D + 2].rearrange("p k j -> p (k j)"),
                                         out_scale[:, bass.ds(g * 2 * J, 2 * J)]).then_inc(S["codes"], 1)

                    def step_x1(g, u, turn):
                        pool.wait_ge(S["h2"], done(g))
                        pool.wait_ge(s_x[u], 32 * (turn + 1))
                        if not early(g, DEEP):
                            pool.wait_ge(s_stx[u], 16 * turn)
                        for k in range(2):
                            last = pool.tensor_tensor(x1[:, u, k], h2[:, u % RING, k], xin[:, u, k], ALU.add)
                        last.then_inc(S["x1"], 1)

                    def step_res(g, u, turn):
                        pool.wait_ge(S["x1"], done(g))
                        if not early(g, DEEP):
                            pool.wait_ge(s_sto[u], 16 * turn)
                        for k in range(2):
                            last = pool.tensor_tensor(heads(res, u, k), heads(x1, u, k),
                                                      rest_row[:].unsqueeze(1).broadcast_to([P, J, D]), ALU.add)
                        last.then_inc(S["res"], 1)

                    each_group_staged(pool, NG, (0, step_codes), (3, step_x1), (3, step_res), ring=DEEP)

                @block.tensor
                def _(pe):
                    def turned(bank, rows):
                        for k in range(2):
                            for q in range(4):
                                last = pe.transpose(bank[k][:, q * P:(q + 1) * P], rows[:, k, q * P:(q + 1) * P],
                                                    ident[:])
                        return last

                    def layer(cols, w, bias, half, g, first_cols, all_cols):
                        for k, there in ((0, first_cols), (1, all_cols)):
                            pe.wait_ge(S[there], done(g))
                            for q in range(4):
                                pe.matmul(zbk[k][:, q * P:(q + 1) * P], cols[:, k, q * P:(q + 1) * P], w[:],
                                          start=(q == 0), stop=False, skip_group_check=True)
                            last = pe.matmul(zbk[k][:], ones_3[:, 0:P], bias[:], start=False, stop=True,
                                             skip_group_check=True)
                            if k == 0:
                                last.then_inc(S[half], 1)
                        return last

                    def step_xt(g, u, turn):
                        pe.wait_ge(s_x[u], 32 * (turn + 1))
                        if not early(g, 3):
                            pe.wait_ge(S["t1c"], done(g - 3))
                        turned(xb, xin[:, u]).then_inc(S["xt"], 1)

                    def step_cen(g, u, turn):
                        pe.wait_ge(S["xtc"], done(g))
                        pe.wait_ge(S["hs"], done(g - 1))
                        for k in range(2):
                            for q in range(4):
                                last = pe.matmul(cb[k][:, q * P:(q + 1) * P], xT[:, k, q * P:(q + 1) * P], center2[:],
                                                 start=True, stop=True)
                        last.then_inc(S["cen"], 1)

                    def step_t1(g, u, turn):
                        pe.wait_ge(S["hs"], done(g))
                        last = min(g + 2, NG - 1) if isinstance(g, int) else g + 2
                        pe.wait_ge(S["xtc"], done(last))
                        turned(xb, hs[:, u % RING]).then_inc(S["t1"], 1)

                    def step_w1(g, u, turn):
                        pe.wait_ge(S["h2"], done(g - 1))
                        layer(hsT, gW1_2, b1_3, "w1a", g, "t1c", "t1c").then_inc(S["w1"], 1)

                    def step_t2(g, u, turn):
                        pe.wait_ge(S["t2c"], done(g - 1))
                        for k, half, turned_half in ((0, "h1a", "t2a"), (1, "h1", "t2")):
                            pe.wait_ge(S[half], done(g))
                            for q in range(4):
                                last = pe.transpose(tb[k][:, q * P:(q + 1) * P], h1[:, u, k, q * P:(q + 1) * P],
                                                    ident[:])
                            last.then_inc(S[turned_half], 1)

                    def step_w2(g, u, turn):
                        pe.wait_ge(S["arow"], done(g))
                        layer(h1T, gW2_2, b2_3, "w2a", g, "t2ca", "t2c").then_inc(S["w2"], 1)

                    each_group_staged(pe, NG, (0, step_xt), (3, step_t2), (2, step_t1), (3, step_w2), (0, step_cen),
                                      (2, step_w1), ring=DEEP)

                @block.scalar
                def _(act):
                    def copies(to, bank):
                        for k in range(2):
                            last = act.activation(to[:, k], bank[k][:], ACT.Copy)
                        return last

                    def step_xtc(g, u, turn):
                        act.wait_ge(S["xt"], done(g))
                        act.wait_ge(S["cen"], done(g - 1))
                        copies(xT, xb).then_inc(S["xtc"], 1)

                    def step_sq(g, u, turn):
                        act.wait_ge(S["cen"], done(g))
                        act.wait_ge(S["var"], done(g - 1))
                        for k in range(2):
                            last = act.activation(sq[:, k], cb[k][:], ACT.Square, scale=0.125)
                        last.then_inc(S["sq"], 1)

                    def step_sd(g, u, turn):
                        act.wait_ge(S["var"], done(g))
                        act.wait_ge(S["rs"], done(g - 1))
                        act.activation(sd[:], var[:], ACT.Sqrt, bias=eps_col[:]).then_inc(S["sd"], 1)

                    def step_arow(g, u, turn):
                        act.wait_ge(S["y"], done(g))
                        act.wait_ge(S["codes"], done(g))
                        for k in range(2):
                            last = act.activation(arow[:, u, k, :, 0:D], zbk[k][:].rearrange("p (j d) -> p j d", d=D),
                                                  ACT.Copy)
                        last.then_inc(S["arow"], 1)

                    def step_t1c(g, u, turn):
                        act.wait_ge(S["t1"], done(g))
                        act.wait_ge(S["w1"], done(g - 1))
                        copies(hsT, xb).then_inc(S["t1c"], 1)

                    def step_t2c(g, u, turn):
                        act.wait_ge(S["w2"], done(g - 1))
                        for k, half, copied in ((0, "t2a", "t2ca"), (1, "t2", "t2c")):
                            act.wait_ge(S[half], done(g))
                            act.activation(h1T[:, k], tb[k][:], ACT.Copy).then_inc(S[copied], 1)

                    def step_rel(g, u, turn):
                        act.wait_ge(S["x1"], freed(g))
                        for k, product, half in ((0, "w2a", "rela"), (1, "w2", "rel")):
                            act.wait_ge(S[product], done(g))
                            act.activation(h2[:, u % RING, k], zbk[k][:], ACT.Relu,
                                           scale=1.0 - SLOPE).then_inc(S[half], 1)

                    each_group_staged(act, NG, (0, step_xtc), (3, step_arow), (3, step_t2c), (1, step_sd), (2, step_t1c),
                                      (3, step_rel), (0, step_sq), ring=DEEP)

                @block.vector
                def _(dve):
                    def step_var(g, u, turn):
                        dve.wait_ge(S["sq"], done(g))
                        dve.wait_ge(S["sd"], done(g - 1))
                        dve.tensor_reduce(var[:], sq[:].rearrange("p k (j d) -> p (k j) d", d=D), AX_X,
                                          ALU.add).then_inc(S["var"], 1)

                    def step_rs(g, u, turn):
                        dve.wait_ge(S["sd"], done(g))
                        dve.wait_ge(S["rsio"], done(g - 1))
                        dve.reciprocal(rs[:], sd[:]).then_inc(S["rs"], 1)

                    def step_rsio(g, u, turn):
                        dve.wait_ge(S["rs"], done(g))
                        dve.wait_ge(S["hs"], done(g - 1))
                        dve.tensor_tensor(rsio[:], rs[:], out_scale[:, bass.ds(g * 2 * J, 2 * J)],
                                          ALU.mult).then_inc(S["rsio"], 1)

                    def step_hs(g, u, turn):
                        dve.wait_ge(S["rsio"], done(g))
                        dve.wait_ge(S["t1"], freed(g))
                        for k in range(2):
                            last = dve.scalar_tensor_tensor(
                                heads(hs, u % RING, k), cb[k][:].rearrange("p (j d) -> p j d", d=D), 0.0,
                                rsio[:, k * J:(k + 1) * J].unsqueeze(2).broadcast_to([P, J, D]), ALU.max, ALU.mult)
                        last.then_inc(S["hs"], 1)

                    def step_y(g, u, turn):
                        if not early(g, DEEP):
                            dve.wait_ge(s_sth[u], 16 * turn)
                            dve.wait_ge(S["t2"], done(g - DEEP))
                        for k, product in ((0, "w1a"), (1, "w1")):
                            dve.wait_ge(S[product], done(g))
                            last = dve.tensor_tensor(
                                heads(h1, u, k), zbk[k][:].rearrange("p (j d) -> p j d", d=D),
                                out_scale[:, bass.ds(g * 2 * J + k * J, J)].unsqueeze(2).broadcast_to([P, J, D]),
                                ALU.mult)
                        last.then_inc(S["y"], 1)

                    def step_h1(g, u, turn):
                        dve.wait_ge(S["y"], done(g))
                        for k, half in ((0, "h1a"), (1, "h1")):
                            dve.scalar_tensor_tensor(h1[:, u, k], h1[:, u, k], SLOPE, h1[:, u, k],
                                                     ALU.mult, ALU.max).then_inc(S[half], 1)

                    def step_h2(g, u, turn):
                        for k, half in ((0, "rela"), (1, "rel")):
                            dve.wait_ge(S[half], done(g))
                            last = dve.scalar_tensor_tensor(h2[:, u % RING, k], zbk[k][:], SLOPE, h2[:, u % RING, k],
                                                            ALU.mult, ALU.add)
                        last.then_inc(S["h2"], 1)

                    each_group_staged(dve, NG, (1, step_rs), (1, step_rsio), (1, step_hs), (3, step_h2), (2, step_y),
                                      (2, step_h1), (0, step_var), ring=DEEP)

        nc.clear_and_free_semaphores(signals)
        nc.all_engine_barrier()


        z_slot = ctx.enter_context(nc.sbuf_tensor("z_slot", [P, T, D + 1], F32))
        w_slot = ctx.enter_context(nc.sbuf_tensor("w_slot", [P, T, D], F32))
        signals = []
        with ExitStack() as ph:
            def sb(name, shape, dt=F32):
                return ph.enter_context(nc.sbuf_tensor(f"p2_{name}", shape, dt))

            def sem(name):
                signals.append(nc.alloc_semaphore(name))
                return signals[-1]

            agg, zb, etb, e1b, e2b = [ph.enter_context(nc.psum_tensor(f"bank2_{n}", [P, 512], F32))
                                      for n in ("agg", "z", "et", "e1", "e2")]

            idx = sb("idx", [P, RING, GROUP], U32)
            own_idx = sb("own_idx", [P, RING, GROUP], U32)
            msg = sb("msg", [P, RING, GROUP, AROW])
            own = sb("own", [P, RING, GROUP, AROW])
            rows = sb("rows", [P, RING, GC])
            car = sb("car", [GROUP, RING, GC])
            seg = sb("seg", [P, RING, GROUP, P])
            carry = sb("carry", [D + 1, RING, GROUP + 1])
            crow = sb("crow", [GROUP, RING, D + 1])
            aggs = sb("aggs", [D + 1, RING, GC])
            er = sb("er", [P, RING, GROUP, R])
            eh = sb("eh", [P, RING, GROUP, D])
            erT = sb("erT", [P, GC])
            pa = sb("pa", [D, 2, GC])
            w1 = sb("w1", [D, GC])
            pb_ = sb("pb_", [P, 2, GROUP * D])
            w2 = sb("w2", [P, GROUP * D])

            s_staged = sem("s2_staged")
            s_msg = [sem(f"s2_msg{u}") for u in range(RING)]
            s_er = [sem(f"s2_er{u}") for u in range(RING)]
            s_eh = [sem(f"s2_eh{u}") for u in range(RING)]
            s_own = [sem(f"s2_own{u}") for u in range(RING)]
            s_rows = [sem(f"s2_rows{u}") for u in range(RING)]
            s_in = [sem(f"s2_in{u}") for u in range(RING)]
            stages = {n: sem("s2_" + n) for n in (
                "seg", "agg", "scan", "crT", "crow", "carried", "aggs", "z", "zs", "codei",
                "et", "etc", "e1", "e1a", "e1e", "e1l", "w1", "e2", "e2a", "e2e", "e2l", "w2", "w")}
            S = stages
            s_link = sem("s2_link")

            s_pace = sem("s2_pace")
            with nc.Block() as block:
                @block.sync
                def _(sp):
                    for s in S.values():
                        sp.sem_inc(s, RING)

                    def fetch_rows(g, u, turn):
                        sp.wait_ge(S["seg"], freed(g))
                        sp.dma_start(rows[:, u],
                                     dst_rows[:, bass.ds(g * GC, GC)].broadcast_to([P, GC])).then_inc(s_rows[u], 16)

                    def fetch_car(g, u, turn):
                        sp.wait_ge(S["carried"], freed(g))
                        sp.dma_start(car[:, u],
                                     carried[bass.ds(g, 1)].rearrange("o t c -> (o t) c")).then_inc(s_in[u], 16)

                    def edges(to, v, s_to, g, u):
                        if isinstance(g, int) and g == NG - 1:
                            full, at = GROUP - 1, (T - 1) * P
                            sp.dma_start(to[:, u, 0:full],
                                         v[g * GC:at, :].rearrange("(t p) d -> p t d", p=P)).then_inc(s_to[u], 16)
                            sp.dma_start(to[0:EL, u, full], v[at:E, :]).then_inc(s_to[u], 16)
                        else:
                            sp.dma_start(to[:, u], tiles(v, g)).then_inc(s_to[u], 16)

                    def fetch_radial(g, u, turn):
                        sp.wait_ge(S["et"], freed(g))
                        edges(er, radial, s_er, g, u)

                    def fetch_edge_h(g, u, turn):
                        sp.wait_ge(S["w"], freed(g))
                        edges(eh, edge_h, s_eh, g, u)

                    each_group_staged(sp, NG, (0, fetch_rows), (0, fetch_radial), (2, fetch_edge_h), (0, fetch_car))

                @block.gpsimd
                def _(pool):
                    max_node = pool.to_reg(N - 1)

                    def gather(g, u, turn):
                        if not early(g):
                            pool.wait_ge(S["agg"], freed(g))
                            pool.wait_ge(S["codei"], freed(g))
                        pool.tensor_copy(idx[:, u, :], src_u[:, bass.ds(g * GROUP, GROUP)]).then_inc(s_staged, 1)
                        pool.wait_ge(s_staged, 2 * g + 1)
                        pool.sem_inc(s_pace, 1)
                        for t in range(GROUP):
                            pool.indirect_dma_start(
                                msg[:, u, t, :], None, table_a,
                                bass.IndirectOffsetOnAxis(ap=idx[:, u, t:t + 1], axis=0),
                                bounds_check=max_node, oob_is_err=False).then_inc(s_msg[u], 16)

                    def gather_own(g, u, turn):
                        if not early(g):
                            pool.wait_ge(S["zs"], freed(g))
                        pool.tensor_copy(own_idx[:, u, :], dst_u[:, bass.ds(g * GROUP, GROUP)]).then_inc(s_staged, 1)
                        pool.wait_ge(s_staged, 2 * g + 2)
                        pool.sem_inc(s_pace, 1)
                        for t in range(GROUP):
                            pool.indirect_dma_start(
                                own[:, u, t, :], None, table_a,
                                bass.IndirectOffsetOnAxis(ap=own_idx[:, u, t:t + 1], axis=0),
                                bounds_check=max_node, oob_is_err=False).then_inc(s_own[u], 16)

                    each_group_staged(pool, NG, (0, gather), (0, gather_own))

                @block.tensor
                def _(pe):
                    def step_agg(g, u, turn):
                        pe.wait_ge(s_msg[u], 16 * GROUP * (turn + 1))
                        pe.wait_ge(S["seg"], done(g))
                        pe.wait_ge(S["aggs"], done(g - 1))
                        for t in range(GROUP):
                            last = pe.matmul(agg[0:D + 1, t * P:(t + 1) * P], msg[:, u, t, 0:D + 1], seg[:, u, t, :],
                                             start=(t == 0), stop=False, skip_group_check=True)
                        last.then_inc(S["agg"], 1)

                    def step_crT(g, u, turn):
                        pe.wait_ge(S["scan"], done(g))
                        pe.wait_ge(S["zs"], done(g - 1))
                        pe.transpose(zb[0:GROUP, 0:D + 1], carry[:, u, 0:GROUP],
                                     ident[0:D + 1, 0:D + 1]).then_inc(S["crT"], 1)

                    def step_carried(g, u, turn):
                        pe.wait_ge(S["crow"], done(g))
                        pe.wait_ge(s_in[u], 16 * (turn + 1))
                        pe.matmul(agg[0:D + 1, :], crow[:, u, :], car[:, u, :], start=False, stop=True,
                                  skip_group_check=True).then_inc(S["carried"], 1)

                    def step_z(g, u, turn):
                        pe.wait_ge(S["aggs"], done(g))
                        for t in range(GROUP):
                            last = pe.transpose(zb[:, t * (D + 1):(t + 1) * (D + 1)], aggs[:, u, t * P:(t + 1) * P],
                                                ident[0:D + 1, 0:D + 1])
                        last.then_inc(S["z"], 1)

                    def step_et(g, u, turn):
                        pe.wait_ge(s_er[u], 16 * turn + (32 if isinstance(g, int) and g == NG - 1 else 16))
                        pe.wait_ge(S["etc"], done(g - 1))
                        for t in range(GROUP):
                            last = pe.transpose(etb[:, t * P:(t + 1) * P], er[:, u, t], ident[:])
                        last.then_inc(S["et"], 1)

                    def step_e1(g, u, turn):
                        pe.wait_ge(S["etc"], done(g))
                        pe.wait_ge(S["w1"], done(g - 1))
                        pe.matmul(e1b[0:D, :], sW1_s[:], erT[:], start=True, stop=False)
                        pe.matmul(e1b[0:D, :], sb1_3[:], ones_3[:], start=False, stop=True).then_inc(S["e1"], 1)

                    def step_e2(g, u, turn):
                        pe.wait_ge(S["w1"], done(g))
                        pe.wait_ge(S["w2"], done(g - 1))
                        for t in range(GROUP):
                            pe.matmul(e2b[:, t * D:(t + 1) * D], w1[:, t * P:(t + 1) * P], sW2_s[:], start=(t == 0),
                                      stop=False, skip_group_check=True)
                        pe.matmul(e2b[:, 0:GROUP * D], ones_3[:, 0:P], sb2_3[:], start=False, stop=True,
                                  skip_group_check=True).then_inc(S["e2"], 1)

                    each_group_staged(pe, NG, (0, step_et), (1, step_z), (0, step_agg), (0, step_crT), (0, step_e1),
                                      (0, step_carried), (1, step_e2))

                @block.scalar
                def _(act):
                    act.preload_act_table_set("natural_log_exp_and_others")

                    def step_aggs(g, u, turn):
                        act.wait_ge(S["carried"], done(g))
                        act.wait_ge(S["z"], freed(g))
                        act.activation(aggs[:, u], agg[0:D + 1, :], ACT.Copy).then_inc(S["aggs"], 1)

                    def step_etc(g, u, turn):
                        act.wait_ge(S["et"], done(g))
                        act.wait_ge(S["e1"], done(g - 1))
                        act.activation(erT[:], etb[:], ACT.Copy).then_inc(S["etc"], 1)

                    def step_e1a(g, u, turn):
                        act.wait_ge(S["e1"], done(g))
                        act.wait_ge(S["w1"], done(g - 1))
                        act.activation(pa[:, 0], e1b[0:D, :], ACT.Abs).then_inc(S["e1a"], 1)

                    def step_e1e(g, u, turn):
                        act.wait_ge(S["e1a"], done(g))
                        act.activation(pa[:, 1], pa[:, 0], ACT.Exp, scale=-1.0).then_inc(S["e1e"], 1)

                    def step_e1l(g, u, turn):
                        act.wait_ge(S["e1e"], done(g))
                        act.activation(pa[:, 0], pa[:, 1], ACT.Ln, bias=half_col[0:D, :],
                                       scale=0.5).then_inc(S["e1l"], 1)

                    def step_e2a(g, u, turn):
                        act.wait_ge(S["e2"], done(g))
                        act.wait_ge(S["w2"], done(g - 1))
                        act.activation(pb_[:, 0], e2b[:, 0:GROUP * D], ACT.Abs).then_inc(S["e2a"], 1)

                    def step_e2e(g, u, turn):
                        act.wait_ge(S["e2a"], done(g))
                        act.activation(pb_[:, 1], pb_[:, 0], ACT.Exp, scale=-1.0).then_inc(S["e2e"], 1)

                    def step_e2l(g, u, turn):
                        act.wait_ge(S["e2e"], done(g))
                        act.activation(pb_[:, 0], pb_[:, 1], ACT.Ln, bias=half_col[:], scale=0.5).then_inc(S["e2l"], 1)

                    each_group_staged(act, NG, (0, step_etc), (2, step_e2a), (2, step_e2e), (2, step_e2l),
                                      (0, step_e1a), (0, step_e1e), (0, step_e1l), (0, step_aggs))

                @block.vector
                def _(dve):
                    dve.memset(carry[:], 0.0).then_inc(s_link, 1)
                    dve.wait_ge(s_link, 1)

                    def step_seg(g, u, turn):
                        cols = bass.ds(g * GROUP, GROUP)
                        dve.wait_ge(s_rows[u], 16 * (turn + 1))
                        dve.wait_ge(S["agg"], freed(g))
                        dve.tensor_tensor(seg[:, u], rows[:, u].rearrange("p (t i) -> p t i", i=P),
                                          dst_kept[:, cols].unsqueeze(2).broadcast_to([P, GROUP, P]),
                                          ALU.is_equal).then_inc(S["seg"], 1)

                    def step_codei(g, u, turn):
                        cols = bass.ds(g * GROUP, GROUP)
                        dve.wait_ge(s_msg[u], 16 * GROUP * (turn + 1))
                        dve.tensor_copy(code_u[:, cols], msg[:, u, :, D + 1]).then_inc(S["codei"], 1)

                    def step_scan(g, u, turn):
                        cols = bass.ds(g * GROUP, GROUP)
                        dve.wait_ge(S["agg"], done(g))
                        dve.wait_ge(S["crT"], freed(g))
                        dve.wait_ge(S["scan"], done(g - 1))
                        dve.tensor_copy(carry[:, u, 0:1], carry[:, 1 - u, GROUP:GROUP + 1])
                        dve.tensor_tensor_scan(carry[:, u, 1:GROUP + 1], goes_on[0:D + 1, cols],
                                               agg[0:D + 1].rearrange("p (t i) -> p t i", i=P)[:, :, P - 1],
                                               carry[:, 1 - u, GROUP:GROUP + 1], ALU.mult,
                                               ALU.add).then_inc(S["scan"], 1)

                    def step_crow(g, u, turn):
                        dve.wait_ge(S["crT"], done(g))
                        dve.wait_ge(S["carried"], freed(g))
                        dve.tensor_copy(crow[:, u], zb[0:GROUP, 0:D + 1]).then_inc(S["crow"], 1)

                    def step_zs(g, u, turn):
                        cols = bass.ds(g * GROUP, GROUP)
                        dve.wait_ge(S["z"], done(g))
                        dve.wait_ge(s_own[u], 16 * GROUP * (turn + 1))
                        dve.tensor_copy(io_slot[:, cols], own[:, u, :, D + 2])
                        dve.tensor_tensor(z_slot[:, cols, :],
                                          zb[:, 0:GROUP * (D + 1)].rearrange("p (t d) -> p t d", d=D + 1),
                                          own[:, u, :, 0:D + 1], ALU.add).then_inc(S["zs"], 1)

                    def step_w1(g, u, turn):
                        dve.wait_ge(S["e1l"], done(g))
                        dve.wait_ge(S["e2"], done(g - 1))
                        dve.scalar_tensor_tensor(w1[:], e1b[0:D, :], 0.0, pa[:, 0], ALU.max,
                                                 ALU.add).then_inc(S["w1"], 1)

                    def step_w2(g, u, turn):
                        dve.wait_ge(S["e2l"], done(g))
                        dve.wait_ge(S["w"], done(g - 1))
                        dve.scalar_tensor_tensor(w2[:], e2b[:, 0:GROUP * D], 0.0, pb_[:, 0], ALU.max,
                                                 ALU.add).then_inc(S["w2"], 1)

                    def step_w(g, u, turn):
                        cols = bass.ds(g * GROUP, GROUP)
                        dve.wait_ge(S["w2"], done(g))
                        dve.wait_ge(s_eh[u], 16 * turn + (32 if isinstance(g, int) and g == NG - 1 else 16))
                        dve.tensor_tensor(w_slot[:, cols, :], w2[:].rearrange("p (t d) -> p t d", d=D), eh[:, u],
                                          ALU.mult).then_inc(S["w"], 1)

                    each_group_staged(dve, NG, (0, step_seg), (0, step_codei), (1, step_zs), (1, step_w1),
                                      (0, step_scan), (0, step_crow), (2, step_w2), (2, step_w))

        nc.clear_and_free_semaphores(signals)
        nc.all_engine_barrier()


        CH = T // 7
        assert T == 7 * CH
        signals = []
        with ExitStack() as ph:
            def sb(name, shape, dt=F32):
                return ph.enter_context(nc.sbuf_tensor(f"p3_{name}", shape, dt))

            def sem(name):
                signals.append(nc.alloc_semaphore(name))
                return signals[-1]

            root = sb("root", [P, 2, T])
            bias = sb("bias", [P, CH, D])
            h_slot = sb("h_slot", [P, T, D])
            s_root, s_inv, s_ii, s_b, s_leak, s_h, s_st3 = (
                sem("s3_root"), sem("s3_inv"), sem("s3_ii"), sem("s3_b"), sem("s3_leak"), sem("s3_h"), sem("s3_st"))

            with nc.Block() as block:
                def wide(col, c):
                    return col[:, bass.ds(c * CH, CH)].unsqueeze(2).broadcast_to([P, CH, D])

                @block.scalar
                def _(act):
                    act.activation(root[:, 0], z_slot[:, :, D], ACT.Sqrt).then_inc(s_root, 1)

                @block.gpsimd
                def _(pool):
                    with pool.Fori(0, 7) as c:
                        h = h_slot[:, bass.ds(c * CH, CH), :]
                        pool.wait_ge(s_leak, c + 1)
                        pool.tensor_tensor(h, h, wide(io_slot, c), ALU.mult).then_inc(s_h, 1)

                @block.vector
                def _(dve):
                    dve.wait_ge(s_root, 1)
                    dve.reciprocal(ii_slot[:], root[:, 0])
                    dve.tensor_scalar(root[:, 1], root[:, 0], -1.0, 1.0, ALU.mult, ALU.add).then_inc(s_inv, 1)
                    dve.wait_ge(s_inv, 1)
                    with dve.Fori(0, 7) as c:
                        h = h_slot[:, bass.ds(c * CH, CH), :]
                        dve.tensor_tensor(h, z_slot[:, bass.ds(c * CH, CH), 0:D], wide(ii_slot, c), ALU.mult)
                        dve.tensor_tensor(bias[:], b1_all[:].unsqueeze(1).broadcast_to([P, CH, D]),
                                          root[:, 1, bass.ds(c * CH, CH)].unsqueeze(2).broadcast_to([P, CH, D]),
                                          ALU.mult).then_inc(s_ii, 1)
                        dve.wait_ge(s_ii, c + 1)
                        dve.tensor_tensor(h, h, bias[:], ALU.add).then_inc(s_b, 1)
                        dve.wait_ge(s_b, c + 1)
                        dve.scalar_tensor_tensor(h, h, SLOPE, h, ALU.mult, ALU.max).then_inc(s_leak, 1)

                @block.sync
                def _(sp):
                    with sp.Fori(0, 7) as c:
                        sp.wait_ge(s_h, c + 1)
                        sp.dma_start(table_h[bass.ds(c * CH * P, CH * P), :].rearrange("(t p) d -> p t d", p=P),
                                     h_slot[:, bass.ds(c * CH, CH), :]).then_inc(s_st3, 16)
                    sp.wait_ge(s_st3, 16 * 7)

        nc.clear_and_free_semaphores(signals)
        nc.all_engine_barrier()


        signals = []
        with ExitStack() as ph:
            def sb(name, shape, dt=F32):
                return ph.enter_context(nc.sbuf_tensor(f"p4_{name}", shape, dt))

            def sem(name):
                signals.append(nc.alloc_semaphore(name))
                return signals[-1]

            agg0, agg1, z0, z1, hdb, crb = [ph.enter_context(nc.psum_tensor(f"bank4_{n}", [P, 512], F32))
                                            for n in ("agg0", "agg1", "z0", "z1", "hd", "cr")]
            aggb, zbb = (agg0, agg1), (z0, z1)
            idx = sb("idx", [P, RING, GROUP], U32)
            msg = sb("msg", [P, RING, GROUP, D])
            rows = sb("rows", [P, RING, GC])
            car = sb("car", [GROUP, RING, GC])
            seg = sb("seg", [P, RING, GROUP, P])
            carry = sb("carry", [D + 1, RING, GROUP + 1])
            crow = sb("crow", [GROUP, RING, D])
            aggs = sb("aggs", [D, RING, GC])
            hd = sb("hd", [P, RING, GROUP, D])
            hdT = sb("hdT", [P, RING, 2 * P])
            xd = sb("xd", [P, RING, GROUP, D])
            y = sb("y", [P, 3, GROUP * D])
            x1 = sb("x1", [P, RING, GROUP, D])

            s_staged = sem("s4_staged")
            s_msg = [sem(f"s4_msg{u}") for u in range(RING)]
            s_rows = [sem(f"s4_rows{u}") for u in range(RING)]
            s_in = [sem(f"s4_in{u}") for u in range(RING)]
            s_hd = [sem(f"s4_hd{u}") for u in range(RING)]
            s_sl = [sem(f"s4_sl{u}") for u in range(RING)]
            s_st = [sem(f"s4_st{u}") for u in range(RING)]
            s_link = sem("s4_link")
            S = {n: sem("s4_" + n) for n in (
                "seg", "agg", "scan", "crT", "crow", "carried", "aggs", "hd", "hdT", "z", "y0", "y1", "y2", "x1")}

            s_pace = sem("s4_pace")
            with nc.Block() as block:
                @block.sync
                def _(sp):
                    for s in S.values():
                        sp.sem_inc(s, RING)
                    for u in range(RING):
                        sp.sem_inc(s_st[u], 16)

                    def fetch_rows(g, u, turn):
                        sp.wait_ge(S["seg"], freed(g))
                        sp.dma_start(rows[:, u],
                                     dst_rows[:, bass.ds(g * GC, GC)].broadcast_to([P, GC])).then_inc(s_rows[u], 16)

                    def fetch_car(g, u, turn):
                        sp.wait_ge(S["carried"], freed(g))
                        sp.dma_start(car[:, u],
                                     carried[bass.ds(g, 1)].rearrange("o t c -> (o t) c")).then_inc(s_in[u], 16)

                    def fetch_slots(g, u, turn):
                        sp.wait_ge(S["hd"], freed(g))
                        sp.dma_start(hd[:, u], tiles(table_h, g)).then_inc(s_hd[u], 16)

                    def fetch_x(g, u, turn):
                        sp.wait_ge(S["x1"], freed(g))
                        sp.dma_start(xd[:, u], tiles(x_dst, g)).then_inc(s_sl[u], 16)

                    def store(g, u, turn):
                        sp.wait_ge(S["x1"], done(g))
                        sp.dma_start(tiles(table_x, g), x1[:, u]).then_inc(s_st[u], 16)

                    each_group_staged(sp, NG, (0, fetch_rows), (2, fetch_car), (2, fetch_slots), (3, fetch_x), (5, store))
                    sp.wait_ge(s_st[0], 16 * (PAIRS + 2))
                    sp.wait_ge(s_st[1], 16 * (PAIRS + 1))

                @block.gpsimd
                def _(pool):
                    max_row = pool.to_reg(SLOTS + N - 1)
                    def gather(g, u, turn):
                        pool.wait_ge(S["agg"], freed(g))
                        pool.tensor_copy(idx[:, u, :], code_u[:, bass.ds(g * GROUP, GROUP)]).then_inc(s_staged, 1)
                        pool.wait_ge(s_staged, g + 1)
                        pool.sem_inc(s_pace, 1)
                        for t in range(GROUP):
                            pool.indirect_dma_start(
                                msg[:, u, t, :], None, table_h,
                                bass.IndirectOffsetOnAxis(ap=idx[:, u, t:t + 1], axis=0),
                                bounds_check=max_row, oob_is_err=False).then_inc(s_msg[u], 16)

                    each_group_staged(pool, NG, (0, gather))

                @block.tensor
                def _(pe):
                    def step_hd(g, u, turn):
                        pe.wait_ge(s_hd[u], 16 * (turn + 1))
                        pe.wait_ge(S["hdT"], done(g - 1))
                        for q in range(2):
                            last = pe.transpose(hdb[:, q * P:(q + 1) * P],
                                                hd[:, u, 2 * q:2 * q + 2].rearrange("p t d -> p (t d)"), ident[:])
                        last.then_inc(S["hd"], 1)

                    def step_agg(g, u, turn):
                        pe.wait_ge(s_msg[u], 16 * GROUP * (turn + 1))
                        pe.wait_ge(S["seg"], done(g))
                        pe.wait_ge(S["aggs"], freed(g))
                        for t in range(GROUP):
                            last = pe.matmul(aggb[u][0:D, t * P:(t + 1) * P], msg[:, u, t, :], seg[:, u, t, :],
                                             start=(t == 0), stop=False, skip_group_check=True)
                        last.then_inc(S["agg"], 1)

                    def step_crT(g, u, turn):
                        pe.wait_ge(S["scan"], done(g))
                        pe.wait_ge(S["crow"], done(g - 1))
                        pe.transpose(crb[0:GROUP, 0:D + 1], carry[:, u, 0:GROUP],
                                     ident[0:D + 1, 0:D + 1]).then_inc(S["crT"], 1)

                    def step_carried(g, u, turn):
                        pe.wait_ge(S["crow"], done(g))
                        pe.wait_ge(s_in[u], 16 * (turn + 1))
                        pe.matmul(aggb[u][0:D, :], crow[:, u, :], car[:, u, :], start=False, stop=True,
                                  skip_group_check=True).then_inc(S["carried"], 1)

                    def step_z(g, u, turn):
                        pe.wait_ge(S["y0"], freed(g))
                        pe.wait_ge(S["hdT"], done(g))
                        pe.wait_ge(S["aggs"], done(g))
                        for q in range(2):
                            last = pe.matmul(zbb[u][:, q * P:(q + 1) * P], hdT[:, u, q * P:(q + 1) * P], gW2_2[:],
                                             start=(q == 0), stop=False, skip_group_check=True)
                            for t in (2 * q, 2 * q + 1):
                                last = pe.matmul(zbb[u][:, t * D:(t + 1) * D], aggs[:, u, t * P:(t + 1) * P], gW2_s[:],
                                                 start=False, stop=(t == GROUP - 1), skip_group_check=True)
                        last.then_inc(S["z"], 1)

                    each_group_staged(pe, NG, (1, step_agg), (2, step_carried), (2, step_hd), (3, step_z), (1, step_crT))

                @block.scalar
                def _(act):
                    def step_hdT(g, u, turn):
                        act.wait_ge(S["hd"], done(g))
                        act.wait_ge(S["z"], freed(g))
                        act.activation(hdT[:, u], hdb[:, 0:2 * P], ACT.Copy).then_inc(S["hdT"], 1)

                    def step_aggs(g, u, turn):
                        act.wait_ge(S["carried"], done(g))
                        act.wait_ge(S["z"], freed(g))
                        act.activation(aggs[:, u], aggb[u][0:D, :], ACT.Copy).then_inc(S["aggs"], 1)

                    each_group_staged(act, NG, (2, step_aggs), (2, step_hdT))

                @block.vector
                def _(dve):
                    y0, y1, y2 = [y[:, n].rearrange("p (t d) -> p t d", d=D) for n in range(3)]
                    dve.memset(carry[:], 0.0).then_inc(s_link, 1)
                    dve.wait_ge(s_link, 1)

                    def step_seg(g, u, turn):
                        cols = bass.ds(g * GROUP, GROUP)
                        dve.wait_ge(s_rows[u], 16 * (turn + 1))
                        dve.wait_ge(S["agg"], freed(g))
                        dve.tensor_tensor(seg[:, u], rows[:, u].rearrange("p (t i) -> p t i", i=P),
                                          dst_kept[:, cols].unsqueeze(2).broadcast_to([P, GROUP, P]),
                                          ALU.is_equal).then_inc(S["seg"], 1)

                    def step_scan(g, u, turn):
                        cols = bass.ds(g * GROUP, GROUP)
                        dve.wait_ge(S["agg"], done(g))
                        dve.wait_ge(S["crT"], freed(g))
                        dve.wait_ge(S["scan"], done(g - 1))
                        dve.tensor_copy(carry[:, u, 0:1], carry[:, 1 - u, GROUP:GROUP + 1])
                        dve.tensor_tensor_scan(carry[0:D, u, 1:GROUP + 1], goes_on[0:D, cols],
                                               aggb[u][0:D].rearrange("p (t i) -> p t i", i=P)[:, :, P - 1],
                                               carry[0:D, 1 - u, GROUP:GROUP + 1], ALU.mult,
                                               ALU.add).then_inc(S["scan"], 1)

                    def step_crow(g, u, turn):
                        dve.wait_ge(S["crT"], done(g))
                        dve.wait_ge(S["carried"], freed(g))
                        dve.tensor_copy(crow[:, u], crb[0:GROUP, 0:D]).then_inc(S["crow"], 1)

                    def step_y0(g, u, turn):
                        cols = bass.ds(g * GROUP, GROUP)
                        dve.wait_ge(S["z"], done(g))
                        dve.tensor_tensor(y0, zbb[u][:, 0:GROUP * D].rearrange("p (t d) -> p t d", d=D),
                                          ii_slot[:, cols].unsqueeze(2).broadcast_to([P, GROUP, D]),
                                          ALU.mult).then_inc(S["y0"], 1)

                    def step_y1(g, u, turn):
                        dve.wait_ge(S["y0"], done(g))
                        dve.tensor_tensor(y1, y0, b2_all[:].unsqueeze(1).broadcast_to([P, GROUP, D]),
                                          ALU.add).then_inc(S["y1"], 1)

                    def step_y2(g, u, turn):
                        dve.wait_ge(S["y1"], done(g))
                        dve.scalar_tensor_tensor(y2, y1, SLOPE, y1, ALU.mult, ALU.max).then_inc(S["y2"], 1)

                    def step_x1(g, u, turn):
                        dve.wait_ge(S["y2"], done(g))
                        dve.wait_ge(s_sl[u], 16 * (turn + 1))
                        dve.wait_ge(s_st[u], 16 * (turn + 1))
                        dve.tensor_tensor(x1[:, u], y2, xd[:, u], ALU.add).then_inc(S["x1"], 1)

                    each_group_staged(dve, NG, (1, step_scan), (0, step_seg), (3, step_y0), (3, step_y1),
                                      (1, step_crow), (3, step_y2), (3, step_x1))

        nc.clear_and_free_semaphores(signals)
        nc.all_engine_barrier()


        signals = []
        with ExitStack() as ph:
            def sb(name, shape, dt=F32):
                return ph.enter_context(nc.sbuf_tensor(f"pw_{name}", shape, dt))

            def sem(name):
                signals.append(nc.alloc_semaphore(name))
                return signals[-1]

            rank_u = sb("rank_u", [EP, EC], U32)
            idx = sb("idx", [EP, 1], U32)
            pay = sb("pay", [EP, D])
            s_st, s_ld, s_staged, s_pace, s_sc, s_back = (
                sem("sw_st"), sem("sw_ld"), sem("sw_staged"), sem("sw_pace"), sem("sw_sc"), sem("sw_back"))

            with nc.Block() as block:
                @block.sync
                def _(sp):
                    with sp.If(sp.value_load(unsorted[:]) > 0):
                        sp.dma_start(w_given.rearrange("(t p) d -> p t d", p=P), w_slot[:]).then_inc(s_st, 16)
                        sp.dma_start(rank_u[:], rank_d).then_inc(s_st, 16)
                        sp.wait_ge(s_sc, 16 * EC)
                        at = (T - 1) * P
                        sp.dma_start(w_slot[:, 0:T - 1, :],
                                     w_sorted[0:at, :].rearrange("(t p) d -> p t d", p=P)).then_inc(s_back, 16)
                        sp.dma_start(w_slot[0:EL, T - 1, :], w_sorted[at:E, :]).then_inc(s_back, 16)
                        sp.wait_ge(s_back, 32)

                @block.gpsimd
                def _(pool):
                    with pool.If(pool.value_load(unsorted[:]) > 0):
                        max_edge = pool.to_reg(E - 1)
                        pool.wait_ge(s_st, 32)
                        with pool.Fori(0, EC) as t:
                            pool.tensor_copy(idx[:], rank_u[:, bass.ds(t, 1)]).then_inc(s_staged, 1)
                            pool.dma_start(pay[:], w_given[0:E, :].rearrange("(p c) d -> p c d", c=EC)[:, bass.ds(t, 1), :]
                                           .rearrange("p c d -> p (c d)")).then_inc(s_ld, 16)
                            pool.wait_ge(s_staged, t + 1)
                            pool.wait_ge(s_ld, 16 * t + 16)
                            pool.sem_inc(s_pace, 1)
                            pool.indirect_dma_start(
                                w_sorted, bass.IndirectOffsetOnAxis(ap=idx[:], axis=0), pay[:], None,
                                bounds_check=max_edge, oob_is_err=False).then_inc(s_sc, 16)
                            pool.wait_ge(s_sc, 16 * t + 16)

        nc.clear_and_free_semaphores(signals)
        nc.all_engine_barrier()


        signals = []
        with ExitStack() as ph:
            def sb(name, shape, dt=F32):
                return ph.enter_context(nc.sbuf_tensor(f"p5_{name}", shape, dt))

            def sem(name):
                signals.append(nc.alloc_semaphore(name))
                return signals[-1]

            agg, zb, xb, sb_, qb = [
                ph.enter_context(nc.psum_tensor(f"bank5_{n}", [P, 512], F32))
                for n in ("agg", "z", "x", "s", "q")]
            idx = sb("idx", [P, RING, GROUP], U32)
            oidx = sb("oidx", [P, RING, GROUP], U32)
            xg = sb("xg", [P, RING, GROUP, D])
            rows = sb("rows", [P, RING, GC])
            car = sb("car", [GROUP, RING, GC])
            seg = sb("seg", [P, RING, GROUP, P])
            carry = sb("carry", [D + 1, RING, GROUP + 1])
            crow = sb("crow", [GROUP, RING, D + 1])
            aggs = sb("aggs", [D + 1, RING, GC])
            xT = sb("xT", [P, 2 * P])
            sq = sb("sq", [P, GROUP * D])
            var = sb("var", [P, GROUP])
            lnv = sb("lnv", [P, GROUP])
            rs = sb("rs", [P, 4, GROUP])
            xh = sb("xh", [P, GROUP, D])
            msg = sb("msg", [P, RING, GROUP, D + 1])
            cnt = sb("cnt", [P, 2, GROUP])
            y = sb("y", [P, 2, GROUP * D])
            pa = sb("pa", [P, 2, GROUP * D])
            s1 = sb("s1", [P, GROUP * D])
            s1T = sb("s1T", [P, 2 * P])
            pc = sb("pc", [P, 2, GROUP * D])
            f = sb("f", [P, GROUP * D])
            x1 = sb("x1", [P, RING, GROUP, D])
            res = sb("res", [P, RING, GROUP, D])

            s_staged, s_ostaged = sem("s5_staged"), sem("s5_ostaged")
            s_xg = [sem(f"s5_xg{u}") for u in range(RING)]
            s_rows = [sem(f"s5_rows{u}") for u in range(RING)]
            s_in = [sem(f"s5_in{u}") for u in range(RING)]
            s_sl = [sem(f"s5_sl{u}") for u in range(RING)]
            s_sc = [sem(f"s5_sc{u}") for u in range(RING)]
            s_link = sem("s5_link")
            S = {n: sem("s5_" + n) for n in (
                "xt", "xtc", "cen", "sq", "var", "lnv", "r0", "r1", "r2", "rs", "xh", "msg",
                "seg", "agg", "scan", "crT", "crow", "carried", "aggs", "z", "cnt", "rc", "y0", "y1",
                "ya", "ye", "yl", "s1", "st", "stc", "q", "qa", "qe", "ql", "f", "res")}

            s_pace = sem("s5_pace")
            with nc.Block() as block:
                @block.sync
                def _(sp):
                    for s in S.values():
                        sp.sem_inc(s, RING)

                    def fetch_rows(g, u, turn):
                        sp.wait_ge(S["seg"], freed(g))
                        sp.dma_start(rows[:, u],
                                     dst_rows[:, bass.ds(g * GC, GC)].broadcast_to([P, GC])).then_inc(s_rows[u], 16)

                    def fetch_car(g, u, turn):
                        sp.wait_ge(S["carried"], freed(g))
                        sp.dma_start(car[:, u],
                                     carried[bass.ds(g, 1)].rearrange("o t c -> (o t) c")).then_inc(s_in[u], 16)

                    def fetch_x1(g, u, turn):
                        sp.wait_ge(S["res"], freed(g))
                        sp.dma_start(x1[:, u], tiles(table_x, g)).then_inc(s_sl[u], 16)

                    each_group_staged(sp, NG, (0, fetch_rows), (1, fetch_car), (2, fetch_x1))
                    sp.wait_ge(s_sc[0], 16 * GROUP * (PAIRS + 1))
                    sp.wait_ge(s_sc[1], 16 * GROUP * PAIRS)

                @block.gpsimd
                def _(pool):
                    max_node = pool.to_reg(N - 1)
                    max_row = pool.to_reg(SLOTS + N - 1)
                    def gather(g, u, turn):
                        if not early(g):
                            pool.wait_ge(S["xt"], freed(g))
                        pool.tensor_copy(idx[:, u, :], code_u[:, bass.ds(g * GROUP, GROUP)]).then_inc(s_staged, 1)
                        pool.wait_ge(s_staged, g + 1)
                        pool.sem_inc(s_pace, 1)
                        for t in range(GROUP):
                            pool.indirect_dma_start(
                                xg[:, u, t, :], None, table_x,
                                bass.IndirectOffsetOnAxis(ap=idx[:, u, t:t + 1], axis=0),
                                bounds_check=max_row, oob_is_err=False).then_inc(s_xg[u], 16)

                    def scatter(g, u, turn):
                        if not early(g):
                            pool.wait_ge(s_sc[u], 16 * GROUP * turn)
                        pool.tensor_copy(oidx[:, u, :], out_u[:, bass.ds(g * GROUP, GROUP)]).then_inc(s_ostaged, 1)
                        pool.wait_ge(s_ostaged, g + 1)
                        pool.wait_ge(S["res"], done(g))
                        pool.sem_inc(s_pace, 1)
                        for t in range(GROUP):
                            pool.indirect_dma_start(
                                out, bass.IndirectOffsetOnAxis(ap=oidx[:, u, t:t + 1], axis=0),
                                res[:, u, t, :], None,
                                bounds_check=max_node, oob_is_err=False).then_inc(s_sc[u], 16)

                    each_group_staged(pool, NG, (0, gather), (4, scatter))

                @block.tensor
                def _(pe):
                    def step_xt(g, u, turn):
                        pe.wait_ge(s_xg[u], 16 * GROUP * (turn + 1))
                        pe.wait_ge(S["xh"], done(g - 1))
                        for q in range(2):
                            last = pe.transpose(xb[:, q * P:(q + 1) * P],
                                                xg[:, u, 2 * q:2 * q + 2, :].rearrange("p t d -> p (t d)"), ident[:])
                        last.then_inc(S["xt"], 1)

                    def step_cen(g, u, turn):
                        pe.wait_ge(S["xtc"], done(g))
                        for q in range(2):
                            last = pe.matmul(xb[:, (2 + q) * P:(3 + q) * P], xT[:, q * P:(q + 1) * P], center2[:],
                                             start=True, stop=True)
                        last.then_inc(S["cen"], 1)

                    def step_agg(g, u, turn):
                        pe.wait_ge(S["msg"], done(g))
                        pe.wait_ge(S["seg"], done(g))
                        pe.wait_ge(S["aggs"], done(g - 1))
                        for t in range(GROUP):
                            last = pe.matmul(agg[0:D + 1, t * P:(t + 1) * P], msg[:, u, t, :], seg[:, u, t, :],
                                             start=(t == 0), stop=False, skip_group_check=True)
                        last.then_inc(S["agg"], 1)

                    def step_crT(g, u, turn):
                        pe.wait_ge(S["scan"], done(g))
                        pe.wait_ge(S["y0"], done(g - 1))
                        pe.wait_ge(S["cnt"], done(g - 1))
                        pe.transpose(zb[0:GROUP, 320:320 + D + 1], carry[:, u, 0:GROUP],
                                     ident[0:D + 1, 0:D + 1]).then_inc(S["crT"], 1)

                    def step_carried(g, u, turn):
                        pe.wait_ge(S["crow"], done(g))
                        pe.wait_ge(s_in[u], 16 * (turn + 1))
                        pe.matmul(agg[0:D + 1, :], crow[:, u, :], car[:, u, :], start=False, stop=True,
                                  skip_group_check=True).then_inc(S["carried"], 1)

                    def step_z(g, u, turn):
                        pe.wait_ge(S["aggs"], done(g))
                        for t in range(GROUP):
                            last = pe.matmul(zb[:, t * (D + 1):(t + 1) * (D + 1)], aggs[:, u, t * P:(t + 1) * P],
                                             sW3_a[:], start=True, stop=True)
                        last.then_inc(S["z"], 1)

                    def step_st(g, u, turn):
                        pe.wait_ge(S["s1"], done(g))
                        pe.wait_ge(S["stc"], done(g - 1))
                        for q in range(2):
                            last = pe.transpose(sb_[:, q * P:(q + 1) * P], s1[:, q * P:(q + 1) * P], ident[:])
                        last.then_inc(S["st"], 1)

                    def step_q(g, u, turn):
                        pe.wait_ge(S["stc"], done(g))
                        pe.wait_ge(S["f"], done(g - 1))
                        for q in range(2):
                            pe.matmul(qb[:, q * P:(q + 1) * P], s1T[:, q * P:(q + 1) * P], sW4_2[:], start=(q == 0),
                                      stop=False, skip_group_check=True)
                        pe.matmul(qb[:, 0:2 * P], ones_3[:, 0:P], sb4_3[:], start=False, stop=True,
                                  skip_group_check=True).then_inc(S["q"], 1)

                    each_group_staged(pe, NG, (0, step_xt), (1, step_agg), (0, step_cen), (1, step_crT),
                                      (1, step_carried), (2, step_st), (1, step_z), (2, step_q))

                @block.scalar
                def _(act):
                    act.preload_act_table_set("natural_log_exp_and_others")

                    def step_xtc(g, u, turn):
                        act.wait_ge(S["xt"], done(g))
                        act.wait_ge(S["cen"], done(g - 1))
                        act.activation(xT[:], xb[:, 0:2 * P], ACT.Copy).then_inc(S["xtc"], 1)

                    def step_sq(g, u, turn):
                        act.wait_ge(S["cen"], done(g))
                        act.wait_ge(S["var"], done(g - 1))
                        act.activation(sq[:], xb[:, 2 * P:4 * P], ACT.Square, scale=0.125).then_inc(S["sq"], 1)

                    def step_lnv(g, u, turn):
                        act.wait_ge(S["var"], done(g))
                        act.activation(lnv[:], var[:], ACT.Ln, bias=eps_col[:]).then_inc(S["lnv"], 1)

                    def step_r0(g, u, turn):
                        act.wait_ge(S["lnv"], done(g))
                        act.wait_ge(S["rs"], done(g - 1))
                        act.activation(rs[:, 0], lnv[:], ACT.Exp, scale=-0.5).then_inc(S["r0"], 1)

                    def step_aggs(g, u, turn):
                        act.wait_ge(S["carried"], done(g))
                        act.wait_ge(S["z"], freed(g))
                        act.activation(aggs[:, u], agg[0:D + 1, :], ACT.Copy).then_inc(S["aggs"], 1)

                    def step_ya(g, u, turn):
                        act.wait_ge(S["y1"], done(g))
                        act.wait_ge(S["s1"], done(g - 1))
                        act.activation(pa[:, 0], y[:, 1], ACT.Abs).then_inc(S["ya"], 1)

                    def step_ye(g, u, turn):
                        act.wait_ge(S["ya"], done(g))
                        act.activation(pa[:, 1], pa[:, 0], ACT.Exp, scale=-1.0).then_inc(S["ye"], 1)

                    def step_yl(g, u, turn):
                        act.wait_ge(S["ye"], done(g))
                        act.activation(pa[:, 0], pa[:, 1], ACT.Ln, bias=half_col[:], scale=0.5).then_inc(S["yl"], 1)

                    def step_stc(g, u, turn):
                        act.wait_ge(S["st"], done(g))
                        act.wait_ge(S["q"], done(g - 1))
                        act.activation(s1T[:], sb_[:, 0:2 * P], ACT.Copy).then_inc(S["stc"], 1)

                    def step_qa(g, u, turn):
                        act.wait_ge(S["q"], done(g))
                        act.wait_ge(S["f"], done(g - 1))
                        act.activation(pc[:, 0], qb[:, 0:2 * P], ACT.Abs).then_inc(S["qa"], 1)

                    def step_qe(g, u, turn):
                        act.wait_ge(S["qa"], done(g))
                        act.activation(pc[:, 1], pc[:, 0], ACT.Exp, scale=-1.0).then_inc(S["qe"], 1)

                    def step_ql(g, u, turn):
                        act.wait_ge(S["qe"], done(g))
                        act.activation(pc[:, 0], pc[:, 1], ACT.Ln, bias=half_col[:], scale=0.5).then_inc(S["ql"], 1)

                    each_group_staged(act, NG, (2, step_ya), (0, step_xtc), (2, step_ye), (0, step_sq),
                                      (2, step_yl), (1, step_aggs), (0, step_lnv), (2, step_stc), (0, step_r0),
                                      (2, step_qa), (2, step_qe), (2, step_ql))

                @block.vector
                def _(dve):
                    zv = zb[:, 0:GROUP * (D + 1)].rearrange("p (t d) -> p t d", d=D + 1)
                    y0, y1 = [y[:, n].rearrange("p (t d) -> p t d", d=D) for n in range(2)]
                    dve.memset(msg[:], 1.0)
                    dve.memset(carry[:], 0.0).then_inc(s_link, 1)
                    dve.wait_ge(s_link, 1)

                    def step_seg(g, u, turn):
                        cols = bass.ds(g * GROUP, GROUP)
                        dve.wait_ge(s_rows[u], 16 * (turn + 1))
                        dve.wait_ge(S["agg"], freed(g))
                        dve.tensor_tensor(seg[:, u], rows[:, u].rearrange("p (t i) -> p t i", i=P),
                                          dst_f[:, cols].unsqueeze(2).broadcast_to([P, GROUP, P]),
                                          ALU.is_equal).then_inc(S["seg"], 1)

                    def step_var(g, u, turn):
                        dve.wait_ge(S["sq"], done(g))
                        dve.wait_ge(S["rs"], done(g - 1))
                        dve.tensor_reduce(var[:], sq[:].rearrange("p (t d) -> p t d", d=D), AX_X,
                                          ALU.add).then_inc(S["var"], 1)

                    def step_r1(g, u, turn):
                        dve.wait_ge(S["r0"], done(g))
                        dve.scalar_tensor_tensor(rs[:, 1], var[:], EPS, rs[:, 0], ALU.add,
                                                 ALU.mult).then_inc(S["r1"], 1)

                    def step_r2(g, u, turn):
                        dve.wait_ge(S["r1"], done(g))
                        dve.scalar_tensor_tensor(rs[:, 2], rs[:, 1], -0.5, rs[:, 0], ALU.mult,
                                                 ALU.mult).then_inc(S["r2"], 1)

                    def step_rs(g, u, turn):
                        dve.wait_ge(S["r2"], done(g))
                        dve.wait_ge(S["xh"], done(g - 1))
                        dve.scalar_tensor_tensor(rs[:, 3], rs[:, 2], 1.5, rs[:, 0], ALU.add,
                                                 ALU.mult).then_inc(S["rs"], 1)

                    def step_xh(g, u, turn):
                        dve.wait_ge(S["rs"], done(g))
                        dve.wait_ge(S["msg"], done(g - 1))
                        dve.scalar_tensor_tensor(xh[:], xb[:, 2 * P:4 * P].rearrange("p (t d) -> p t d", d=D), 0.0,
                                                 rs[:, 3].unsqueeze(2).broadcast_to([P, GROUP, D]), ALU.max,
                                                 ALU.mult).then_inc(S["xh"], 1)

                    def step_msg(g, u, turn):
                        cols = bass.ds(g * GROUP, GROUP)
                        dve.wait_ge(S["xh"], done(g))
                        dve.tensor_tensor(msg[:, u, :, 0:D], xh[:], w_slot[:, cols, :], ALU.mult).then_inc(S["msg"], 1)

                    def step_scan(g, u, turn):
                        cols = bass.ds(g * GROUP, GROUP)
                        dve.wait_ge(S["agg"], done(g))
                        dve.wait_ge(S["crT"], freed(g))
                        dve.wait_ge(S["scan"], done(g - 1))
                        dve.tensor_copy(carry[:, u, 0:1], carry[:, 1 - u, GROUP:GROUP + 1])
                        dve.tensor_tensor_scan(carry[:, u, 1:GROUP + 1], goes_on[0:D + 1, cols],
                                               agg[0:D + 1].rearrange("p (t i) -> p t i", i=P)[:, :, P - 1],
                                               carry[:, 1 - u, GROUP:GROUP + 1], ALU.mult,
                                               ALU.add).then_inc(S["scan"], 1)

                    def step_crow(g, u, turn):
                        dve.wait_ge(S["crT"], done(g))
                        dve.wait_ge(S["carried"], freed(g))
                        dve.tensor_copy(crow[:, u], zb[0:GROUP, 320:320 + D + 1]).then_inc(S["crow"], 1)

                    def step_cnt(g, u, turn):
                        dve.wait_ge(S["z"], done(g))
                        dve.tensor_scalar(cnt[:, 0], zv[:, :, D], 1.0, None, ALU.max).then_inc(S["cnt"], 1)

                    def step_rc(g, u, turn):
                        dve.wait_ge(S["cnt"], done(g))
                        dve.reciprocal(cnt[:, 1], cnt[:, 0]).then_inc(S["rc"], 1)

                    def step_y0(g, u, turn):
                        dve.wait_ge(S["rc"], done(g))
                        dve.tensor_tensor(y0, zv[:, :, 0:D], cnt[:, 1].unsqueeze(2).broadcast_to([P, GROUP, D]),
                                          ALU.mult).then_inc(S["y0"], 1)

                    def step_y1(g, u, turn):
                        dve.wait_ge(S["y0"], done(g))
                        dve.tensor_tensor(y1, y0, sb3_all[:].unsqueeze(1).broadcast_to([P, GROUP, D]),
                                          ALU.add).then_inc(S["y1"], 1)

                    def step_s1(g, u, turn):
                        dve.wait_ge(S["yl"], done(g))
                        dve.wait_ge(S["st"], done(g - 1))
                        dve.scalar_tensor_tensor(s1[:], y[:, 1], 0.0, pa[:, 0], ALU.max, ALU.add).then_inc(S["s1"], 1)

                    def step_f(g, u, turn):
                        dve.wait_ge(S["ql"], done(g))
                        dve.scalar_tensor_tensor(f[:], qb[:, 0:2 * P], 0.0, pc[:, 0], ALU.max,
                                                 ALU.add).then_inc(S["f"], 1)

                    def step_res(g, u, turn):
                        dve.wait_ge(S["f"], done(g))
                        dve.wait_ge(s_sl[u], 16 * (turn + 1))
                        if not early(g):
                            dve.wait_ge(s_sc[u], 16 * GROUP * turn)
                        dve.tensor_tensor(res[:, u], f[:].rearrange("p (t d) -> p t d", d=D), x1[:, u],
                                          ALU.add).then_inc(S["res"], 1)

                    each_group_staged(dve, NG, (0, step_seg), (1, step_scan), (1, step_crow), (0, step_var),
                                      (2, step_s1), (0, step_r1), (1, step_cnt), (0, step_r2), (1, step_rc),
                                      (0, step_rs), (1, step_y0), (0, step_xh), (1, step_y1), (0, step_msg),
                                      (2, step_f), (2, step_res))


_INS = ['x', 'src', 'dst', 'edge_attr_128', 'edge_attr_64', 'L0_gnn_W1', 'L0_gnn_b1', 'L0_gnn_W2', 'L0_gnn_b2',
        'L1_gnn_W1', 'L1_gnn_b1', 'L1_gnn_W2', 'L1_gnn_b2', 'L1_gnn_W3', 'L1_gnn_b3', 'L1_gnn_W4', 'L1_gnn_b4']
_OUTS = [((100000, 64), 'float32')]


def kernel(**inputs):
    import numpy as _np
    import concourse.bacc as _bacc
    from concourse import mybir as _mybir
    from concourse.bass_utils import run_bass_kernel_spmd as _run

    nc = _bacc.Bacc("TRN2", target_bir_lowering=False, num_devices=1)
    arrays, args = {}, []
    for name in _INS:
        a = _np.ascontiguousarray(inputs[name])
        arrays[f"in_{name}_dram"] = a
        args.append(nc.dram_tensor(f"in_{name}_dram", a.shape, _mybir.dt.from_np(a.dtype), kind="ExternalInput").ap())
    for i, (shape, dtype) in enumerate(_OUTS):
        dt = _mybir.dt.from_np(_np.dtype(dtype))
        args.append(nc.dram_tensor(f"out_{i}_dram", shape, dt, kind="ExternalOutput").ap())
    gnn_kernel(nc, *args)
    r = _run(nc, [arrays], core_ids=[0])
    got = tuple(r.results[0][f"out_{i}_dram"] for i in range(len(_OUTS)))
    return got[0]
```
